# Optimizing a Trainium2 kernel written in Bass

```python
import numpy as np
import jax
import jax.numpy as jnp

def _softmax(x, axis=-1):
    return jax.nn.softmax(x, axis=axis)

def _gelu(x):
    return jax.nn.gelu(x, approximate=True)

def _silu(x):
    return jax.nn.silu(x)

def _sigmoid(x):
    return jax.nn.sigmoid(x)

def _layernorm(x, axis=-1, eps=1e-05):
    m = jnp.mean(x, axis=axis, keepdims=True)
    v = jnp.var(x, axis=axis, keepdims=True)
    return (x - m) / jnp.sqrt(v + eps)

def _scatter_add(tgt, idx, src, axis=0):
    return tgt.at[idx].add(src)

def _segment_sum(src, seg, n):
    return jax.ops.segment_sum(src, seg, n)
kernel_name = 'mk_decoder_preln_d2_seqx_r4_218c71'

def setup_inputs(seed: int=0):
    np.random.seed(seed)
    _w = jnp.asarray

    def _rec_inputs():
        import jax
        import jax.numpy as jnp
        _rk = jax.random.key(seed)
        x = -0.0002928 + 1 * jax.random.normal(jax.random.fold_in(_rk, 1), (16, 256, 256), jnp.float32)
        _lenS = 256 - jax.random.randint(jax.random.fold_in(_rk, 7), (16,), 0, max(1, 256 // 4) + 1, jnp.int32)
        _lenS2 = 256 - jax.random.randint(jax.random.fold_in(_rk, 8), (16,), 0, max(1, 256 // 4) + 1, jnp.int32)
        _ctx_1024P = jax.random.normal(jax.random.fold_in(_rk, 11), (16, 16, 256), jnp.float32)
        _ctx_1024c = jax.random.dirichlet(jax.random.fold_in(_rk, 511), 0.3 * jnp.ones((16,), jnp.float32), (16, 256))
        _ctx_1024t = jnp.einsum('bsk,bkd->bsd', _ctx_1024c, _ctx_1024P)
        _ctx_1024t = _ctx_1024t * jax.lax.rsqrt(jnp.mean(jnp.square(_ctx_1024t)) + 1e-12) * 0.953939
        ctx_1024 = -1.39393e-06 + 0.999914 * (_ctx_1024t + 0.3 * jax.random.normal(jax.random.fold_in(_rk, 611), (16, 256, 256), jnp.float32))
        fside_Bx1xSxS2_0 = -4.48278e-06 + 1.00019 * jax.random.normal(jax.random.fold_in(_rk, 12), (16, 1, 256, 256), jnp.float32)
        return (x, ctx_1024, fside_Bx1xSxS2_0)
    x, ctx_1024, fside_Bx1xSxS2_0 = _rec_inputs()

    def _L0_attn_setup():
        import jax, jax.numpy as jnp
        import numpy as np
        B, S, D, H, A = (2, 512, 256, 16, 64)
        INIT_STD = 0.02
        key = jax.random.key(seed)
        ks = jax.random.split(key, 5)
        return {'residual': jax.random.normal(ks[0], (B, S, D), dtype=jnp.float32), 'Wq': jax.random.normal(ks[1], (H, D, A), dtype=jnp.float32) * INIT_STD, 'Wk': jax.random.normal(ks[2], (H, D, A), dtype=jnp.float32) * INIT_STD, 'Wv': jax.random.normal(ks[3], (H, D, A), dtype=jnp.float32) * INIT_STD, 'Wo': jax.random.normal(ks[4], (H, A, D), dtype=jnp.float32) * INIT_STD, 'bq': jnp.zeros((H, A), dtype=jnp.float32), 'bk': jnp.zeros((H, A), dtype=jnp.float32), 'bv': jnp.zeros((H, A), dtype=jnp.float32), 'bo': jnp.zeros((D,), dtype=jnp.float32)}
    _L0_attn_all = _L0_attn_setup()
    _L0_attn_in = {k: v for k, v in _L0_attn_all.items() if k in ('Wq', 'Wk', 'Wv', 'Wo', 'bq', 'bk', 'bv', 'bo')}
    del _L0_attn_all

    def _L0_xattn_setup():
        import jax, jax.numpy as jnp
        import numpy as np
        B, S, D_FF = (2, 512, 256)
        NUM_HEADS, D_KV = (16, 64)
        INNER = NUM_HEADS * D_KV
        key = jax.random.key(seed)
        ks = jax.random.split(key, 8)
        scale = 1.0 / np.sqrt(D_FF)
        return {'q': jax.random.normal(ks[0], (B, S, D_FF), jnp.float32), 'k': jax.random.normal(ks[1], (B, S, D_FF), jnp.float32), 'v': jax.random.normal(ks[2], (B, S, D_FF), jnp.float32), 'attn_mask': jax.random.normal(ks[3], (B, 1, S, S), jnp.float32), 'Wq': jax.random.normal(ks[4], (INNER, D_FF), jnp.float32) * scale, 'Wk': jax.random.normal(ks[5], (INNER, D_FF), jnp.float32) * scale, 'Wv': jax.random.normal(ks[6], (INNER, D_FF), jnp.float32) * scale, 'Wo': jax.random.normal(ks[7], (D_FF, INNER), jnp.float32) * scale, 'num_heads': NUM_HEADS}
    _L0_xattn_all = _L0_xattn_setup()
    _L0_xattn_in = {k: v for k, v in _L0_xattn_all.items() if k in ('Wq', 'Wk', 'Wv', 'Wo')}
    del _L0_xattn_all

    def _L0_ffn_setup():
        import jax, jax.numpy as jnp
        import numpy as np
        D_MODEL, HIDDEN, N_EXPERTS, TOP_K = (256, 512, 8, 2)
        RMS_EPS = 1e-06
        key = jax.random.key(seed)
        ks = jax.random.split(key, 6)
        B, S = (4, 512)
        return {'x': jax.random.normal(ks[0], (B, S, D_MODEL), jnp.float32), 'norm_weight': jnp.ones((D_MODEL,), jnp.float32), 'gate_w': jax.random.normal(ks[1], (N_EXPERTS, D_MODEL), jnp.float32) * 0.02, 'w1': jax.random.normal(ks[2], (N_EXPERTS, HIDDEN, D_MODEL), jnp.float32) * 0.02, 'b1': jnp.zeros((N_EXPERTS, HIDDEN), jnp.float32), 'w2': jax.random.normal(ks[3], (N_EXPERTS, D_MODEL, HIDDEN), jnp.float32) * 0.02, 'b2': jnp.zeros((N_EXPERTS, D_MODEL), jnp.float32)}
    _L0_ffn_all = _L0_ffn_setup()
    _L0_ffn_in = {k: v for k, v in _L0_ffn_all.items() if k in ('norm_weight', 'gate_w', 'w1', 'b1', 'w2', 'b2')}
    del _L0_ffn_all

    def _L1_attn_setup():
        import jax, jax.numpy as jnp
        import numpy as np
        D_MODEL = 256
        N_HEADS = 16
        D_HEAD = D_MODEL // N_HEADS
        EPS = 1e-06

        def _phi(x):
            return jax.nn.elu(x) + 1.0
        key = jax.random.key(seed)
        k1, k2, k3 = jax.random.split(key, 3)
        x = jax.random.normal(k1, (4, 1024, D_MODEL), dtype=jnp.float32)
        s = 1.0 / np.sqrt(D_MODEL)
        w_qkv = jax.random.uniform(k2, (3 * D_MODEL, D_MODEL), minval=-s, maxval=s, dtype=jnp.float32)
        w_out = jax.random.uniform(k3, (D_MODEL, D_MODEL), minval=-s, maxval=s, dtype=jnp.float32)
        return {'x': x, 'w_qkv': w_qkv, 'w_out': w_out}
    _L1_attn_all = _L1_attn_setup()
    _L1_attn_in = {k: v for k, v in _L1_attn_all.items() if k in ('w_qkv', 'w_out')}
    del _L1_attn_all

    def _L1_xattn_setup():
        import jax, jax.numpy as jnp
        import numpy as np
        EMBD = 256
        NUM_HEAD = 16
        HEAD = EMBD // NUM_HEAD
        key = jax.random.key(seed)
        ks = jax.random.split(key, 9)
        B, S, D = (2, 512, EMBD)
        s = 1.0 / np.sqrt(D)
        return {'q': jax.random.normal(ks[0], (B, S, D), jnp.float32), 'k': jax.random.normal(ks[1], (B, S, D), jnp.float32), 'v': jax.random.normal(ks[2], (B, S, D), jnp.float32), 'Wq': jax.random.uniform(ks[3], (D, D), jnp.float32, -s, s), 'bq': jax.random.uniform(ks[4], (D,), jnp.float32, -s, s), 'Wk': jax.random.uniform(ks[5], (D, D), jnp.float32, -s, s), 'bk': jax.random.uniform(ks[6], (D,), jnp.float32, -s, s), 'Wv': jax.random.uniform(ks[7], (D, D), jnp.float32, -s, s), 'bv': jax.random.uniform(ks[8], (D,), jnp.float32, -s, s)}
    _L1_xattn_all = _L1_xattn_setup()
    _L1_xattn_in = {k: v for k, v in _L1_xattn_all.items() if k in ('Wq', 'bq', 'Wk', 'bk', 'Wv', 'bv')}
    del _L1_xattn_all

    def _L1_ffn_setup():
        import jax, jax.numpy as jnp
        import numpy as np
        B, N, DIM = (2, 512, 256)
        HEADS, DIM_HEAD, EXPERTS = (8, 64, 8)
        SCALE = DIM_HEAD ** (-0.5)
        key = jax.random.key(seed)
        ks = jax.random.split(key, 6)
        dim_inner = HEADS * DIM_HEAD
        return {'x': jax.random.normal(ks[0], (B, N, DIM), jnp.float32), 'w_q': jax.random.normal(ks[1], (DIM, dim_inner), jnp.float32) * 0.02, 'w_k': jax.random.normal(ks[2], (DIM, dim_inner), jnp.float32) * 0.02, 'w_gate': jax.random.normal(ks[3], (DIM, HEADS * EXPERTS), jnp.float32) * 0.02, 'value_experts': jax.random.normal(ks[4], (EXPERTS, HEADS, DIM, DIM_HEAD), jnp.float32) * 0.02, 'output_experts': jax.random.normal(ks[5], (EXPERTS, HEADS, DIM_HEAD, DIM), jnp.float32) * 0.02}
    _L1_ffn_all = _L1_ffn_setup()
    _L1_ffn_in = {k: v for k, v in _L1_ffn_all.items() if k in ('w_q', 'w_k', 'w_gate', 'value_experts', 'output_experts')}
    del _L1_ffn_all
    return {'x': x, 'ctx_1024': ctx_1024, 'fside_Bx1xSxS2_0': fside_Bx1xSxS2_0, 'L0_attn_Wq': _L0_attn_in['Wq'], 'L0_attn_Wk': _L0_attn_in['Wk'], 'L0_attn_Wv': _L0_attn_in['Wv'], 'L0_attn_Wo': _L0_attn_in['Wo'], 'L0_attn_bq': _L0_attn_in['bq'], 'L0_attn_bk': _L0_attn_in['bk'], 'L0_attn_bv': _L0_attn_in['bv'], 'L0_attn_bo': _L0_attn_in['bo'], 'L0_xattn_Wq': _L0_xattn_in['Wq'], 'L0_xattn_Wk': _L0_xattn_in['Wk'], 'L0_xattn_Wv': _L0_xattn_in['Wv'], 'L0_xattn_Wo': _L0_xattn_in['Wo'], 'L0_ffn_norm_weight': _L0_ffn_in['norm_weight'], 'L0_ffn_gate_w': _L0_ffn_in['gate_w'], 'L0_ffn_w1': _L0_ffn_in['w1'], 'L0_ffn_b1': _L0_ffn_in['b1'], 'L0_ffn_w2': _L0_ffn_in['w2'], 'L0_ffn_b2': _L0_ffn_in['b2'], 'L1_attn_w_qkv': _L1_attn_in['w_qkv'], 'L1_attn_w_out': _L1_attn_in['w_out'], 'L1_xattn_Wq': _L1_xattn_in['Wq'], 'L1_xattn_bq': _L1_xattn_in['bq'], 'L1_xattn_Wk': _L1_xattn_in['Wk'], 'L1_xattn_bk': _L1_xattn_in['bk'], 'L1_xattn_Wv': _L1_xattn_in['Wv'], 'L1_xattn_bv': _L1_xattn_in['bv'], 'L1_ffn_w_q': _L1_ffn_in['w_q'], 'L1_ffn_w_k': _L1_ffn_in['w_k'], 'L1_ffn_w_gate': _L1_ffn_in['w_gate'], 'L1_ffn_value_experts': _L1_ffn_in['value_experts'], 'L1_ffn_output_experts': _L1_ffn_in['output_experts']}

def reference(x, ctx_1024, fside_Bx1xSxS2_0, L0_attn_Wq, L0_attn_Wk, L0_attn_Wv, L0_attn_Wo, L0_attn_bq, L0_attn_bk, L0_attn_bv, L0_attn_bo, L0_xattn_Wq, L0_xattn_Wk, L0_xattn_Wv, L0_xattn_Wo, L0_ffn_norm_weight, L0_ffn_gate_w, L0_ffn_w1, L0_ffn_b1, L0_ffn_w2, L0_ffn_b2, L1_attn_w_qkv, L1_attn_w_out, L1_xattn_Wq, L1_xattn_bq, L1_xattn_Wk, L1_xattn_bk, L1_xattn_Wv, L1_xattn_bv, L1_ffn_w_q, L1_ffn_w_k, L1_ffn_w_gate, L1_ffn_value_experts, L1_ffn_output_experts):
    import jax
    import jax.numpy as jnp

    def _L0_attn_ref(residual, Wq, Wk, Wv, Wo, bq, bk, bv, bo):
        import jax, jax.numpy as jnp
        import numpy as np
        B, S, D, H, A = (2, 512, 256, 16, 64)
        INIT_STD = 0.02
        q = jnp.einsum('bsd,hda->bhsa', residual, Wq) + bq[None, :, None, :]
        k = jnp.einsum('bsd,hda->bhsa', residual, Wk) + bk[None, :, None, :]
        v = jnp.einsum('bsd,hda->bhsa', residual, Wv) + bv[None, :, None, :]
        scale = 1.0 / jnp.sqrt(jnp.float32(q.shape[-1]))
        scores = jnp.einsum('bhsa,bhta->bhst', q, k) * scale
        s = scores.shape[-1]
        causal = jnp.tril(jnp.ones((s, s), dtype=bool))
        masked = jnp.where(causal, scores, jnp.float32(-100000.0))
        pattern = jax.nn.softmax(masked, axis=-1)
        z = jnp.einsum('bhst,bhta->bshа'.replace('а', 'a'), pattern, v)
        out = jnp.einsum('bsha,had->bsd', z, Wo) + bo
        return out

    def _L0_xattn_ref(q, k, v, attn_mask, Wq, Wk, Wv, Wo, num_heads):
        import jax, jax.numpy as jnp
        import numpy as np
        B, S, D_FF = (2, 512, 256)
        NUM_HEADS, D_KV = (16, 64)
        INNER = NUM_HEADS * D_KV
        b, s, _ = q.shape

        def proj_heads(x, W):
            y = jnp.einsum('bsd,ed->bse', x, W)
            return y.reshape(b, s, num_heads, -1).transpose(0, 2, 1, 3)
        qh = proj_heads(q, Wq)
        kh = proj_heads(k, Wk)
        vh = proj_heads(v, Wv)
        scores = jnp.einsum('bhqd,bhkd->bhqk', qh, kh) + attn_mask
        probs = jax.nn.softmax(scores, axis=-1)
        ctx = jnp.einsum('bhqk,bhkd->bhqd', probs, vh)
        ctx = ctx.transpose(0, 2, 1, 3).reshape(b, s, -1)
        return jnp.einsum('bse,de->bsd', ctx, Wo)

    def _L0_ffn_ref(x, norm_weight, gate_w, w1, b1, w2, b2):
        import jax, jax.numpy as jnp
        import numpy as np
        D_MODEL, HIDDEN, N_EXPERTS, TOP_K = (256, 512, 8, 2)
        RMS_EPS = 1e-06
        B, S, D = x.shape
        E = gate_w.shape[0]
        t = x * jax.lax.rsqrt(jnp.mean(x * x, axis=-1, keepdims=True) + RMS_EPS) * norm_weight
        tokens = t.reshape(-1, D)
        T = tokens.shape[0]
        gate_logits = tokens @ gate_w.T
        gate_scores, expert_idx = jax.lax.top_k(gate_logits, TOP_K)
        routing_weights = jax.nn.softmax(gate_scores, axis=-1)
        combine = jnp.zeros((T, E), tokens.dtype).at[jnp.arange(T)[:, None], expert_idx].add(routing_weights)

        def body(acc, params):
            W1, B1, W2, B2, c = params
            h = jax.nn.gelu(tokens @ W1.T + B1, approximate=False)
            o = h @ W2.T + B2
            return (acc + c[:, None] * o, None)
        out, _ = jax.lax.scan(body, jnp.zeros_like(tokens), (w1, b1, w2, b2, combine.T))
        return x + out.reshape(B, S, D)

    def _L1_attn_ref(x, w_qkv, w_out):
        import jax, jax.numpy as jnp
        import numpy as np
        D_MODEL = 256
        N_HEADS = 16
        D_HEAD = D_MODEL // N_HEADS
        EPS = 1e-06

        def _phi(x):
            return jax.nn.elu(x) + 1.0
        B, L, D = x.shape
        H, dh = (N_HEADS, D_HEAD)
        qkv = jnp.einsum('bld,ed->ble', x, w_qkv)
        qkv = qkv.reshape(B, L, 3, H, dh).transpose(2, 0, 3, 1, 4)
        q, k, v = (_phi(qkv[0]), _phi(qkv[1]), qkv[2])
        qT = q.transpose(2, 0, 1, 3)
        kT = k.transpose(2, 0, 1, 3)
        vT = v.transpose(2, 0, 1, 3)
        S0 = jnp.zeros((B, H, dh, dh), dtype=x.dtype)
        z0 = jnp.zeros((B, H, dh), dtype=x.dtype)

        def step(carry, inp):
            S, z = carry
            q_t, k_t, v_t = inp
            S = S + k_t[..., :, None] * v_t[..., None, :]
            z = z + k_t
            num = jnp.einsum('bhde,bhd->bhe', S, q_t)
            den = jnp.maximum(jnp.sum(z * q_t, axis=-1, keepdims=True), EPS)
            return ((S, z), num / den)
        _, out = jax.lax.scan(step, (S0, z0), (qT, kT, vT))
        out = out.transpose(1, 0, 2, 3).reshape(B, L, D)
        return jnp.einsum('bld,ed->ble', out, w_out)

    def _L1_xattn_ref(q, k, v, Wq, bq, Wk, bk, Wv, bv):
        import jax, jax.numpy as jnp
        import numpy as np
        EMBD = 256
        NUM_HEAD = 16
        HEAD = EMBD // NUM_HEAD
        B, S, D = q.shape
        H, Hd = (NUM_HEAD, HEAD)
        qp = jnp.einsum('bsd,ed->bse', q, Wq) + bq
        kp = jnp.einsum('bsd,ed->bse', k, Wk) + bk
        vp = jnp.einsum('bsd,ed->bse', v, Wv) + bv
        qp = qp.reshape(B, S, H, Hd).transpose(0, 2, 1, 3)
        kp = kp.reshape(B, S, H, Hd).transpose(0, 2, 1, 3)
        vp = vp.reshape(B, S, H, Hd).transpose(0, 2, 1, 3)
        score = jnp.einsum('bhqd,bhkd->bhqk', qp, kp) / jnp.sqrt(jnp.float32(Hd))
        attn = jax.nn.softmax(score, axis=-1)
        out = jnp.einsum('bhqk,bhkd->bhqd', attn, vp)
        return out.transpose(0, 2, 1, 3).reshape(B, S, H * Hd)

    def _L1_ffn_ref(x, w_q, w_k, w_gate, value_experts, output_experts):
        import jax, jax.numpy as jnp
        import numpy as np
        B, N, DIM = (2, 512, 256)
        HEADS, DIM_HEAD, EXPERTS = (8, 64, 8)
        SCALE = DIM_HEAD ** (-0.5)
        b, n, _ = x.shape
        q = (x @ w_q).reshape(b, n, HEADS, DIM_HEAD).transpose(0, 2, 1, 3)
        k = (x @ w_k).reshape(b, n, HEADS, DIM_HEAD).transpose(0, 2, 1, 3)
        gates = jax.nn.sigmoid((x @ w_gate).reshape(b, n, HEADS, EXPERTS).transpose(0, 2, 1, 3))
        sel = jnp.argmax(gates, axis=-1)
        gm = jax.nn.one_hot(sel, EXPERTS, dtype=x.dtype) * gates
        values = jnp.einsum('bhne,ehdk,bnd->bhnk', gm, value_experts, x)
        sim = jnp.einsum('bhid,bhjd->bhij', q * SCALE, k)
        causal_mask = jnp.triu(jnp.ones((n, n), dtype=bool), 1)
        sim = jnp.where(causal_mask, jnp.finfo(sim.dtype).min, sim)
        attn = jax.nn.softmax(sim, axis=-1)
        out = jnp.einsum('bhij,bhjk->bhik', attn, values)
        out = jnp.einsum('bhne,ehkd,bhnk->bhnd', gm, output_experts, out)
        return out.sum(axis=1)
    x = x + _L0_attn_ref(_layernorm(x, axis=-1), L0_attn_Wq, L0_attn_Wk, L0_attn_Wv, L0_attn_Wo, L0_attn_bq, L0_attn_bk, L0_attn_bv, L0_attn_bo)
    x = x + _L0_xattn_ref(_layernorm(x, axis=-1), ctx_1024, ctx_1024, fside_Bx1xSxS2_0, L0_xattn_Wq, L0_xattn_Wk, L0_xattn_Wv, L0_xattn_Wo, 16)
    x = x + _L0_ffn_ref(_layernorm(x, axis=-1), L0_ffn_norm_weight, L0_ffn_gate_w, L0_ffn_w1, L0_ffn_b1, L0_ffn_w2, L0_ffn_b2)
    x = x + _L1_attn_ref(_layernorm(x, axis=-1), L1_attn_w_qkv, L1_attn_w_out)
    x = x + _L1_xattn_ref(_layernorm(x, axis=-1), ctx_1024, ctx_1024, L1_xattn_Wq, L1_xattn_bq, L1_xattn_Wk, L1_xattn_bk, L1_xattn_Wv, L1_xattn_bv)
    x = x + _L1_ffn_ref(_layernorm(x, axis=-1), L1_ffn_w_q, L1_ffn_w_k, L1_ffn_w_gate, L1_ffn_value_experts, L1_ffn_output_experts)
    return x

_drawn_inputs = setup_inputs


def setup_inputs(seed=0):
    import zlib

    import numpy as np

    out = dict(_drawn_inputs(seed))
    spreads = {'L0_attn_bq': (0.0, 0.8),
     'L0_attn_bk': (0.0, 0.8),
     'L0_attn_bv': (0.0, 0.1),
     'L0_attn_bo': (0.0, 0.1),
     'L0_ffn_norm_weight': (1.0, 0.6),
     'L0_ffn_b1': (0.0, 0.8),
     'L0_ffn_b2': (0.0, 0.383)}
    factors = {'L0_attn_Wq': 8.0,
     'L0_attn_Wk': 8.0,
     'L0_ffn_w1': 3.36,
     'L0_ffn_w2': 3.138,
     'L1_xattn_Wq': 5.34,
     'L1_xattn_bq': 8.0,
     'L1_xattn_Wk': 5.341,
     'L1_xattn_bk': 8.0,
     'L1_xattn_bv': 5.509,
     'L1_ffn_w_q': 8.0,
     'L1_ffn_w_k': 8.0,
     'L1_ffn_w_gate': 8.0,
     'L1_ffn_value_experts': 8.0,
     'L1_ffn_output_experts': 8.0}
    for name, (base, spread) in spreads.items():
        noise = np.random.default_rng([zlib.crc32(name.encode()), seed]).standard_normal(out[name].shape)
        drawn = base * np.exp(spread * noise) if base else spread * noise
        out[name] = jnp.asarray(drawn.astype(out[name].dtype))
    for name, factor in factors.items():
        out[name] = (out[name] * factor).astype(out[name].dtype)
    return out
```

```python
from contextlib import ExitStack

import concourse.bass as bass
from concourse import mybir

ALU = mybir.AluOpType
ACT = mybir.ActivationFunctionType
F32 = mybir.dt.float32
X = mybir.AxisListType.X

P = 128
D = 256
DC = D // P
S = 256
ST = S // P
B = 16
TILES = B * ST
LN_EPS = 1e-5
NEG_L0 = -100000.0
NEG_MIN = -1.0e30


def late(g, n):
    return not isinstance(g, int) or g >= n


class Core:
    pass


def run_steps(eng, steps, stages, last_lag):
    def batch(b):
        for s in range(steps):
            stages(b, s)
    lead = -(-last_lag // steps)
    for b in range(lead):
        batch(b)
    with eng.Fori(lead, B - 1) as b:
        batch(b)
    batch(B - 1)
    for s in range(last_lag):
        stages(B, s)


def lagged(b, s, d, steps):
    back = s - d
    at = back % steps
    over = (at - back) // steps
    if isinstance(b, int):
        n = b * steps + back
        if n < 0 or n >= B * steps:
            return None
        return n, at, b - over
    return b * steps + back, at, (b - over if over else b)


def constants(nc, c):
    with nc.semaphore("s_zero") as filled, nc.semaphore("s_const") as const_ready, \
            nc.semaphore("s_stats") as stats, nc.Block() as block:
        c.spent += [filled, const_ready, stats]

        @block.gpsimd
        def _(pool):
            nc.gpsimd.memset(c.ident[:], 0.0).then_inc(filled, 1)
            nc.gpsimd.memset(c.causal[:], 0.0).then_inc(filled, 1)
            nc.gpsimd.memset(c.causal_min[:], 0.0).then_inc(filled, 1)
            nc.gpsimd.memset(c.keep[:], 1.0).then_inc(filled, 1)
            nc.gpsimd.memset(c.half[:], 64 ** -0.5).then_inc(filled, 1)
            nc.gpsimd.memset(c.half1[:], 1.0).then_inc(filled, 1)
            nc.gpsimd.memset(c.head16[:], 0.25).then_inc(filled, 1)
            nc.gpsimd.memset(c.head16k[:], 1.0).then_inc(filled, 1)
            pool.wait_ge(filled, 8)
            nc.gpsimd.affine_select(out=c.ident[:], in_=c.ident[:], compare_op=ALU.not_equal, fill=1.0,
                                    base=0, pattern=[[-1, P]], channel_multiplier=1).then_inc(const_ready, 1)
            for mask, fill in ((c.causal, NEG_L0), (c.causal_min, NEG_MIN)):
                nc.gpsimd.affine_select(out=mask[:, P:], in_=mask[:, P:], compare_op=ALU.is_ge, fill=fill,
                                        base=0, pattern=[[-1, P]], channel_multiplier=1).then_inc(const_ready, 1)
            for blk in (0, 2):
                nc.gpsimd.affine_select(out=c.keep[:, blk * P:(blk + 1) * P], in_=c.keep[:, blk * P:(blk + 1) * P],
                                        compare_op=ALU.is_ge, fill=0.0, base=0, pattern=[[1, P]],
                                        channel_multiplier=-1).then_inc(const_ready, 1)
            ready = 5
            for mask, width in ((c.half, 64), (c.half1, 64), (c.head16, 16), (c.head16k, 16)):
                n = P // width
                nc.gpsimd.affine_select(out=mask[:], in_=mask[:], compare_op=ALU.is_ge, fill=0.0, base=0,
                                        pattern=[[-width, n]], channel_multiplier=1).then_inc(const_ready, 1)
                ready += 1
                pool.wait_ge(const_ready, ready)
                nc.gpsimd.affine_select(out=mask[:], in_=mask[:], compare_op=ALU.is_ge, fill=0.0, base=width - 1,
                                        pattern=[[width, n]], channel_multiplier=-1).then_inc(const_ready, 1)
                ready += 1

        @block.sync
        def _(sp):
            for q in range(4):
                t = TILES // 4
                sp.dma_start(c.x[:, q * t:(q + 1) * t, :], c.dram["x"][:, q * t:(q + 1) * t, :]).then_inc(c.x_in[q], 16)

        @block.vector
        def _(dve):
            nc.vector.memset(c.eps[:], LN_EPS).then_inc(c.begun, 1)
            for b in range(B):
                if b % (B // 4) == 0:
                    dve.wait_ge(c.x_in[b // (B // 4)], 16)
                batch_stats(nc, dve, c, stats, b)


def batch_stats(nc, dve, c, stats, b):
    if late(b, 1):
        dve.wait_ge(stats, 3 * b)
    dve.sem_inc(c.waited, 1)
    for i in range(ST):
        last = nc.vector.bn_stats(c.bn[:, i, :], c.x[:, bass.ds(b * ST + i, 1), :].rearrange("p a d -> p (a d)"))
    last.then_inc(stats, 1)
    dve.wait_ge(stats, 3 * b + 1)
    dve.sem_inc(c.waited, 1)
    for i in range(ST):
        last = nc.vector.bn_aggr(c.mv2[:, i, :], c.bn[:, i, :])
    last.then_inc(stats, 1)
    dve.wait_ge(stats, 3 * b + 2)
    nc.vector.tensor_scalar(c.mv[:, bass.ds(b * ST, ST), :].rearrange("p a d -> p (a d)"),
                            c.mv2[:].rearrange("p a d -> p (a d)"), 1.0, None, ALU.mult).then_inc(stats, 1)


def attention(nc, c, tag, w_pairs, wo, load_next, cross=False, causal=False, bias=None, bo=None):
    PAIRS = 8
    LAST = 4
    with ExitStack() as ctx:
        sb = lambda name, shape: ctx.enter_context(nc.sbuf_tensor(f"{tag}_{name}", shape, F32))
        ps = lambda name: ctx.enter_context(nc.psum_tensor(f"{tag}_{name}", [P, 512], F32))

        def sem(name):
            c.spent.append(ctx.enter_context(nc.semaphore(f"{tag}_{name}")))
            return c.spent[-1]


        rstd = sb("rstd", [P, TILES])
        xn = sb("xn", [P, ST, D])
        xnT = sb("xnT", [P, DC, S])
        if cross:
            ctx_stage = sb("ctx_stage", [P, DC, S])
            ctxT = sb("ctxT", [P, DC, S])
            mask_stage = sb("mask_stage", [P, ST, S])
            mask = sb("mask", [P, ST, S])
        qT = sb("qT", [P, 2, 2, S])
        kT = sb("kT", [P, 2, S])
        v = sb("v", [P, 4, ST, P])
        sm = sb("sm", [P, 2, ST, S])
        pr = sb("pr", [P, 4, ST, S])
        prT = sb("prT", [P, 4, ST, S])
        zT = sb("zT", [P, 2, S])
        mx = sb("mx", [P, 2, ST])
        nmx = sb("nmx", [P, 2, ST])
        sums = sb("sums", [P, 4, ST])
        inv = sb("inv", [P, 4, ST])

        ps_q, ps_kv, ps_z, ps_out = ps("ps_q"), ps("ps_kv"), ps("ps_z"), ps("ps_out")
        ps_s = [ps("ps_s0"), ps("ps_s1")]
        ps_t = [ps("ps_t0"), ps("ps_t1")]

        rstd_s = sem("rstd")
        xn_ready = sem("xn_ready")
        xnT_ps = sem("xnT_ps")
        xnT_ready = sem("xnT_ready")
        ctx_in = sem("ctx_in")
        ctx_ready = sem("ctx_ready")
        mask_in = sem("mask_in")
        mask_ready = sem("mask_ready")
        proj = sem("proj")
        q_ready = sem("q_ready")
        k_ready = sem("k_ready")
        v_ready = sem("v_ready")
        scored = sem("scored")
        maxed = sem("maxed")
        negated = sem("negated")
        exped = sem("exped")
        inverted = sem("inverted")
        normed = sem("normed")
        turned = sem("turned")
        prT_ready = sem("prT_ready")
        z_done = sem("z_done")
        zT_ready = sem("zT_ready")
        projected = sem("projected")
        out_read = sem("out_read")
        biased = sem("biased")
        stats = sem("stats")

        block = ctx.enter_context(nc.Block())

        def steps(eng, slot):
            run_steps(eng, PAIRS, slot, LAST)

        @block.sync
        def _(sp):
            if not cross:
                load_next(sp)
            else:
                def batch(b):
                    if late(b, 1):
                        sp.wait_ge(ctx_ready, b)
                        sp.wait_ge(mask_ready, b)
                    sp.dma_start(ctx_stage[:], c.dram["ctxT"][:, bass.ds(b, 1), :, :].rearrange("p a c s -> p (a c) s")).then_inc(ctx_in, 16)
                    sp.dma_start(mask_stage[:], c.dram["mask"][:, bass.ds(b, 1), :, :].rearrange("p a c s -> p (a c) s")).then_inc(mask_in, 16)
                batch(0)
                load_next(sp)
                with sp.Fori(1, B) as b:
                    batch(b)

        if cross:
            @block.gpsimd
            def _(pool):
                def batch(b):
                    pool.wait_ge(ctx_in, 16 * b + 16)
                    if late(b, 1):
                        pool.wait_ge(proj, 2 * PAIRS * b)
                    pool.sem_inc(c.pool_waited, 1)
                    nc.gpsimd.tensor_copy(ctxT[:], ctx_stage[:]).then_inc(ctx_ready, 1)
                batch(0)
                with pool.Fori(1, B) as b:
                    batch(b)

        @block.tensor
        def _(pe):
            c.wait_weights(pe, tag)

            def turn_x(b):
                pe.wait_ge(xn_ready, b + 1)
                if late(b, 1):
                    pe.wait_ge(q_ready, PAIRS * b)
                for dc in range(DC):
                    for i in range(ST):
                        last = nc.tensor.transpose(ps_q[:, dc * S + i * P:dc * S + (i + 1) * P],
                                                   xn[:, i, dc * P:(dc + 1) * P], c.ident[:])
                last.then_inc(xnT_ps, 1)

            def project(g, s, b):
                if s == 0:
                    pe.wait_ge(xnT_ready, b + 1)
                if late(g, 1):
                    pe.wait_ge(q_ready, g)
                for dc in range(DC):
                    last = nc.tensor.matmul(ps_q[:, 0:S], w_pairs[:, s, 0, dc, :], xnT[:, dc, :],
                                            start=(dc == 0), stop=(dc == DC - 1))
                last.then_inc(proj, 1)
                if s == 0 and cross:
                    pe.wait_ge(ctx_ready, b + 1)
                src = ctxT if cross else xnT
                if late(g, 1):
                    pe.wait_ge(v_ready, g)
                for dc in range(DC):
                    last = nc.tensor.matmul(ps_kv[:, 0:S], w_pairs[:, s, 1, dc, :], src[:, dc, :],
                                            start=(dc == 0), stop=(dc == DC - 1))
                for i in range(ST):
                    for dc in range(DC):
                        last = nc.tensor.matmul(ps_kv[:, S + i * P:S + (i + 1) * P], src[:, dc, i * P:(i + 1) * P],
                                                w_pairs[:, s, 2, dc, :], start=(dc == 0), stop=(dc == DC - 1))
                last.then_inc(proj, 1)

            def scores(g, s):
                pe.wait_ge(q_ready, g + 1)
                pe.wait_ge(k_ready, g + 1)
                for j in range(2):
                    if late(g, 1):
                        pe.wait_ge(maxed, 2 * g + j - 1)
                    for i in range(ST):
                        n = (i + 1) * P if causal else S
                        last = nc.tensor.matmul(ps_s[j][:, i * S:i * S + n], qT[:, s % 2, j, i * P:(i + 1) * P],
                                                kT[:, s % 2, 0:n], start=True, stop=True)
                    last.then_inc(scored, 1)

            def turn(g, s):
                for j in range(2):
                    pe.wait_ge(normed, 2 * g + j + 1)
                    if late(g, 1):
                        pe.wait_ge(prT_ready, 2 * g + j - 1)
                    for i in range(ST):
                        for t in range(i + 1 if causal else ST):
                            last = nc.tensor.transpose(ps_t[j][:, t * S + i * P:t * S + (i + 1) * P],
                                                       pr[:, 2 * (s % 2) + j, i, t * P:(t + 1) * P], c.ident[:])
                    last.then_inc(turned, 1)

            def values(g, s):
                pe.wait_ge(v_ready, g + 1)
                pe.wait_ge(prT_ready, 2 * g + 2)
                if late(g, 1):
                    pe.wait_ge(zT_ready, g)
                z0 = (s % 2) * S
                for t in range(ST):
                    q0 = t * P if causal else 0
                    for j in range(2):
                        last = nc.tensor.matmul(ps_z[64 * j:64 * j + 64, z0 + q0:z0 + S],
                                                v[:, s % 4, t, 64 * j:64 * j + 64],
                                                prT[:, 2 * (s % 2) + j, t, q0:S], start=(t == 0), stop=(t == ST - 1))
                last.then_inc(z_done, 1)

            def output(g, s, b):
                pe.wait_ge(zT_ready, g + 1)
                if s == 0 and late(g, PAIRS):
                    pe.wait_ge(out_read, b)
                for i in range(ST):
                    last = nc.tensor.matmul(ps_out[:, i * D:(i + 1) * D], zT[:, s % 2, i * P:(i + 1) * P],
                                            wo[:, s, :], start=(s == 0 and i == 0), stop=(s == PAIRS - 1),
                                            skip_group_check=True)
                last.then_inc(projected, 1)

            def slot(b, s):
                if at := lagged(b, s, 0, PAIRS):
                    project(*at)
                if at := lagged(b, s, 1, PAIRS):
                    scores(at[0], at[1])
                if s == PAIRS - 1:
                    if not isinstance(b, int) or b + 1 < B:
                        turn_x(b + 1)
                if at := lagged(b, s, 2, PAIRS):
                    turn(at[0], at[1])
                if at := lagged(b, s, 3, PAIRS):
                    values(at[0], at[1])
                if at := lagged(b, s, 4, PAIRS):
                    output(*at)

            turn_x(0)
            steps(pe, slot)

        @block.vector
        def _(dve):
            dve.wait_ge(rstd_s, 1)
            nc.vector.reciprocal(rstd[:], rstd[:]).then_inc(rstd_s, 1)
            dve.wait_ge(rstd_s, 2)

            def normalise(b):
                if late(b, 1):
                    dve.wait_ge(xnT_ps, b)
                for i in range(ST):
                    n = b * ST + i
                    last = nc.vector.tensor_scalar(xn[:, i, :], c.x[:, bass.ds(n, 1), :].rearrange("p a d -> p (a d)"),
                                                   c.mv[:, bass.ds(n, 1), 0:1].rearrange("p a d -> p (a d)"),
                                                   rstd[:, bass.ds(n, 1)], ALU.subtract, ALU.mult)
                last.then_inc(xn_ready, 1)

            def take_mask(b):
                dve.wait_ge(mask_in, 16 * b + 16)
                nc.vector.tensor_copy(mask[:], mask_stage[:]).then_inc(mask_ready, 1)
                dve.wait_ge(mask_ready, b + 1)

            def take_q(g, s):
                dve.wait_ge(proj, 2 * g + 1)
                if late(g, 2):
                    dve.wait_ge(scored, 2 * g - 2)
                for j in range(2):
                    if bias is not None:
                        last = nc.vector.tensor_scalar(qT[:, s % 2, j, :], ps_q[:, 0:S], bias["q"][:, s:s + 1],
                                                       c.half[:, j:j + 1], ALU.add, ALU.mult)
                    else:
                        last = nc.vector.tensor_scalar(qT[:, s % 2, j, :], ps_q[:, 0:S], c.half1[:, j:j + 1],
                                                       None, ALU.mult)
                last.then_inc(q_ready, 1)

            def row_max(g, s, j):
                dve.wait_ge(scored, 2 * g + j + 1)
                if late(g, 1):
                    dve.wait_ge(exped, 2 * g + j - 1)
                dve.sem_inc(c.waited, 1)
                for i in range(ST):
                    n = (i + 1) * P if causal else S
                    add = c.causal[:, (ST - 1 - i) * P:(ST - 1 - i) * P + n] if causal else mask[:, i, :]
                    last = nc.vector.tensor_tensor_reduce(sm[:, j, i, 0:n], ps_s[j][:, i * S:i * S + n], add, 1.0,
                                                          -3.0e38, ALU.add, ALU.max, mx[:, j, i:i + 1])
                last.then_inc(maxed, 1)
                dve.wait_ge(maxed, 2 * g + j + 1)
                nc.vector.tensor_scalar(nmx[:, j, :], mx[:, j, :], -1.0, None, ALU.mult).then_inc(negated, 1)

            def norm(g, s, j):
                r = 2 * (s % 2) + j
                dve.wait_ge(exped, 2 * g + j + 1)
                nc.vector.reciprocal(inv[:, r, :], sums[:, r, :]).then_inc(inverted, 1)
                dve.wait_ge(inverted, 2 * g + j + 1)
                for i in range(ST):
                    n = (i + 1) * P if causal else S
                    last = nc.vector.tensor_scalar(pr[:, r, i, 0:n], pr[:, r, i, 0:n], inv[:, r, i:i + 1], None, ALU.mult)
                last.then_inc(normed, 1)

            def take_z(g, s):
                dve.wait_ge(z_done, g + 1)
                if late(g, 2):
                    dve.wait_ge(projected, g - 1)
                z = ps_z[:, (s % 2) * S:(s % 2 + 1) * S]
                if bias is not None:
                    nc.vector.tensor_scalar(zT[:, s % 2, :], z, bias["v"][:, s:s + 1], None, ALU.add).then_inc(zT_ready, 1)
                else:
                    nc.vector.tensor_copy(zT[:, s % 2, :], z).then_inc(zT_ready, 1)

            def add_to_x(b):
                dve.wait_ge(projected, PAIRS * b + PAIRS)
                xb = c.x[:, bass.ds(b * ST, ST), :].rearrange("p a d -> p (a d)")
                nc.vector.tensor_tensor(xb, xb, ps_out[:], ALU.add).then_inc(out_read, 1)
                dve.wait_ge(out_read, b + 1)
                if bo is not None:
                    for i in range(ST):
                        xt = c.x[:, bass.ds(b * ST + i, 1), :].rearrange("p a d -> p (a d)")
                        last = nc.vector.tensor_tensor(xt, xt, bo[:], ALU.add)
                    last.then_inc(biased, 1)
                    dve.wait_ge(biased, b + 1)
                batch_stats(nc, dve, c, stats, b)

            def slot(b, s):
                if at := lagged(b, s, 2, PAIRS):
                    norm(at[0], at[1], 1)
                if at := lagged(b, s, 0, PAIRS):
                    take_q(at[0], at[1])
                if at := lagged(b, s, 1, PAIRS):
                    if at[1] == 0 and cross:
                        take_mask(at[2])
                    row_max(at[0], at[1], 0)
                if at := lagged(b, s, 1, PAIRS):
                    row_max(at[0], at[1], 1)
                    norm(at[0], at[1], 0)
                if at := lagged(b, s, 3, PAIRS):
                    take_z(at[0], at[1])
                if s == 2 and (not isinstance(b, int) or b + 1 < B):
                    normalise(b + 1)
                if (at := lagged(b, s, 4, PAIRS)) and at[1] == PAIRS - 1:
                    add_to_x(at[2])

            normalise(0)
            steps(dve, slot)

        @block.scalar
        def _(act):
            nc.scalar.activation(rstd[:], c.mv[:, :, 1:2].rearrange("p a d -> p (a d)"), ACT.Sqrt,
                                 bias=c.eps[:]).then_inc(rstd_s, 1)
            c.wait_small(act, tag)

            def take_xT(b):
                act.wait_ge(xnT_ps, b + 1)
                nc.scalar.copy(xnT[:].rearrange("p c s -> p (c s)"), ps_q[:]).then_inc(xnT_ready, 1)

            def take_kv(g, s):
                act.wait_ge(proj, 2 * g + 2)
                if late(g, 2):
                    act.wait_ge(scored, 2 * g - 2)
                if bias is not None:
                    nc.scalar.activation(kT[:, s % 2, :], ps_kv[:, 0:S], ACT.Identity,
                                         bias=bias["k"][:, s:s + 1]).then_inc(k_ready, 1)
                else:
                    nc.scalar.copy(kT[:, s % 2, :], ps_kv[:, 0:S]).then_inc(k_ready, 1)
                if late(g, 4):
                    act.wait_ge(z_done, g - 3)
                nc.scalar.copy(v[:, s % 4, :, :].rearrange("p i m -> p (i m)"), ps_kv[:, S:2 * S]).then_inc(v_ready, 1)

            def exponentials(g, s, j):
                r = 2 * (s % 2) + j
                act.wait_ge(negated, 2 * g + j + 1)
                if late(g, 2):
                    act.wait_ge(turned, 2 * g + j - 3)
                for i in range(ST):
                    n = (i + 1) * P if causal else S
                    last = nc.scalar.activation(pr[:, r, i, 0:n], sm[:, j, i, 0:n], ACT.Exp, bias=nmx[:, j, i:i + 1],
                                                accum_out=sums[:, r, i:i + 1])
                last.then_inc(exped, 1)

            def take_prT(g, s, j):
                r = 2 * (s % 2) + j
                act.wait_ge(turned, 2 * g + j + 1)
                if late(g, 2):
                    act.wait_ge(z_done, g - 1)
                if causal:
                    nc.scalar.copy(prT[:, r, 0, :], ps_t[j][:, 0:S])
                    nc.scalar.copy(prT[:, r, 1, P:S], ps_t[j][:, S + P:2 * S]).then_inc(prT_ready, 1)
                else:
                    nc.scalar.copy(prT[:, r, :, :].rearrange("p t s -> p (t s)"), ps_t[j][:]).then_inc(prT_ready, 1)

            def slot(b, s):
                if at := lagged(b, s, 0, PAIRS):
                    take_kv(at[0], at[1])
                if at := lagged(b, s, 1, PAIRS):
                    exponentials(at[0], at[1], 0)
                if at := lagged(b, s, 2, PAIRS):
                    take_prT(at[0], at[1], 0)
                if at := lagged(b, s, 1, PAIRS):
                    exponentials(at[0], at[1], 1)
                if s == PAIRS - 1 and (not isinstance(b, int) or b + 1 < B):
                    take_xT(b + 1)
                if at := lagged(b, s, 2, PAIRS):
                    take_prT(at[0], at[1], 1)

            take_xT(0)
            steps(act, slot)


def experts(nc, c, tag, w1, w2, gate_w, b1, b2, norm_w, load_next):
    E, FC, LAST = 8, 4, 1
    with ExitStack() as ctx:
        sb = lambda name, shape: ctx.enter_context(nc.sbuf_tensor(f"{tag}_{name}", shape, F32))
        ps = lambda name: ctx.enter_context(nc.psum_tensor(f"{tag}_{name}", [P, 512], F32))
        sem = lambda name: ctx.enter_context(nc.semaphore(f"{tag}_{name}"))
        rstd = sb("rstd", [P, TILES])
        ms = sb("ms", [P, TILES])
        rms_eps = sb("rms_eps", [P, 1])
        t = sb("t", [P, ST, D])
        tT = sb("tT", [P, DC, S])
        y = sb("y", [P, ST, D])
        hT = sb("hT", [P, 2, FC, S])
        rev = sb("rev", [P, ST, E])
        logits = sb("logits", [P, ST, E])
        eq = sb("eq", [P, ST, E])
        one = sb("one", [P, 2, ST, E])
        top = sb("top", [P, 2, ST])
        pick = sb("pick", [P, ST])
        diff = sb("diff", [P, ST])
        ex = sb("ex", [P, ST])
        wt = sb("wt", [P, 2, ST])
        part = sb("part", [P, 2, ST, E])
        mix = sb("mix", [P, ST, P])
        mixT = sb("mixT", [P, ST, P])
        ps_h = [ps(f"ps_h{n}") for n in range(FC)]
        ps_o = [ps("ps_o0"), ps("ps_o1")]
        ps_m, ps_c = ps("ps_m"), ps("ps_c")

        root = sem("root")
        t_ready = sem("t_ready")
        tT_ps = sem("tT_ps")
        tT_ready = sem("tT_ready")
        gated = sem("gated")
        pick_s = sem("pick_s")
        ex_ready = sem("ex_ready")
        mixT_ps = sem("mixT_ps")
        mixT_ready = sem("mixT_ready")
        b2_ps = sem("b2_ps")
        h_ps = sem("h_ps")
        h_ready = sem("h_ready")
        o_ps = sem("o_ps")
        y_s = sem("y_s")
        summed = sem("summed")
        stats = sem("stats")
        weighed = sem("weighed")
        SUMS = 2 + 2 * E
        PICKS = 14

        def late_batch(b):
            return not isinstance(b, int) or b < B

        def place(e):
            return 2 + 2 * e + (1 if e >= 2 else 0)

        block = ctx.enter_context(nc.Block())

        @block.sync
        def _(sp):
            load_next(sp)

        @block.gpsimd
        def _(pool):
            for spent in c.spent:
                pool.sem_clear(spent)
            nc.gpsimd.iota(rev[:], pattern=[[0, ST], [-1, E]], base=E, channel_multiplier=0,
                           allow_small_or_imprecise_dtypes=True).then_inc(root, 1)
            nc.gpsimd.memset(mix[:], 0.0).then_inc(root, 1)
            nc.gpsimd.memset(rms_eps[:], 1e-6).then_inc(root, 1)

        @block.tensor
        def _(pe):
            c.wait_weights(pe, tag)

            def turn_t(b):
                pe.wait_ge(t_ready, b + 1)
                if late(b, 1):
                    pe.wait_ge(summed, SUMS * (b - 1) + 6)
                for dc in range(DC):
                    for i in range(ST):
                        last = nc.tensor.transpose(ps_m[:, dc * S + i * P:dc * S + (i + 1) * P],
                                                   t[:, i, dc * P:(dc + 1) * P], c.ident[:])
                last.then_inc(tT_ps, 1)

            def gates(b):
                pe.wait_ge(tT_ready, b + 1)
                for i in range(ST):
                    for dc in range(DC):
                        last = nc.tensor.matmul(ps_m[:, i * E:(i + 1) * E], tT[:, dc, i * P:(i + 1) * P],
                                                gate_w[:, dc, :], start=(dc == 0), stop=(dc == DC - 1))
                last.then_inc(gated, 1)

            def weighted_b2(b):
                pe.wait_ge(pick_s, PICKS * b + PICKS)
                if late(b, 1):
                    pe.wait_ge(mixT_ready, b)
                for i in range(ST):
                    last = nc.tensor.transpose(ps_c[:, i * P:(i + 1) * P], mix[:, i, :], c.ident[:])
                last.then_inc(mixT_ps, 1)
                pe.wait_ge(mixT_ready, b + 1)
                for i in range(ST):
                    last = nc.tensor.matmul(ps_m[:, i * D:(i + 1) * D], mixT[:, i, :], b2[:], start=True, stop=True)
                last.then_inc(b2_ps, 1)

            def first(g, s, b):
                if s == 0:
                    pe.wait_ge(tT_ready, b + 1)
                for f in range(FC):
                    if late(g, 1):
                        pe.wait_ge(h_ready, FC * g + f - FC + 1)
                    for dc in range(DC):
                        last = nc.tensor.matmul(ps_h[f][:, 0:S], w1[:, s, f, dc, :], tT[:, dc, :],
                                                start=(dc == 0), stop=(dc == DC - 1))
                    last.then_inc(h_ps, 1)

            def second(g, s, b):
                pe.wait_ge(h_ready, FC * g + FC)
                for i in range(ST):
                    if late(g, 1):
                        pe.wait_ge(summed, SUMS * b + place(s - 1) + i if s else SUMS * (b - 1) + place(E - 1) + i)
                    for f in range(FC):
                        last = nc.tensor.matmul(ps_o[i][:, 0:D], hT[:, s % 2, f, i * P:(i + 1) * P], w2[:, s, f, :],
                                                start=(f == 0), stop=(f == FC - 1))
                    last.then_inc(o_ps, 1)

            def slot(b, s):
                if s == 0 and late_batch(b):
                    gates(b)
                if at := lagged(b, s, 0, E):
                    first(*at)
                if s == E - 1 and (not isinstance(b, int) or b + 1 < B):
                    turn_t(b + 1)
                if at := lagged(b, s, 1, E):
                    second(*at)
                if s == 2:
                    weighted_b2(b)

            turn_t(0)
            run_steps(pe, E, slot, LAST)

        @block.vector
        def _(dve):
            dve.wait_ge(root, 4)
            nc.vector.reciprocal(rstd[:], rstd[:]).then_inc(root, 1)
            dve.wait_ge(root, 5)
            nc.vector.tensor_tensor(ms[:], rstd[:], rstd[:], ALU.mult).then_inc(root, 1)
            dve.wait_ge(root, 6)
            nc.vector.tensor_tensor(ms[:], ms[:], c.mv[:, :, 1:2].rearrange("p a d -> p (a d)"), ALU.mult).then_inc(root, 1)
            dve.wait_ge(root, 8)
            nc.vector.reciprocal(ms[:], ms[:]).then_inc(root, 1)
            dve.wait_ge(root, 9)
            nc.vector.tensor_tensor(ms[:], ms[:], rstd[:], ALU.mult).then_inc(root, 1)
            dve.wait_ge(root, 10)

            def normalise(b):
                if late(b, 1):
                    dve.wait_ge(tT_ps, b)
                for i in range(ST):
                    n = b * ST + i
                    last = nc.vector.tensor_scalar(t[:, i, :], c.x[:, bass.ds(n, 1), :].rearrange("p a d -> p (a d)"),
                                                   c.mv[:, bass.ds(n, 1), 0:1].rearrange("p a d -> p (a d)"),
                                                   ms[:, bass.ds(n, 1)], ALU.subtract, ALU.mult)
                last.then_inc(t_ready, 1)

            def add_y(b):
                if late(b, 1):
                    dve.wait_ge(summed, SUMS * b)
                for i in range(ST):
                    n = b * ST + i
                    last = nc.vector.tensor_scalar(y[:, i, :], c.x[:, bass.ds(n, 1), :].rearrange("p a d -> p (a d)"),
                                                   c.mv[:, bass.ds(n, 1), 0:1].rearrange("p a d -> p (a d)"),
                                                   rstd[:, bass.ds(n, 1)], ALU.subtract, ALU.mult)
                last.then_inc(y_s, 1)
                dve.wait_ge(y_s, b + 1)
                xb = c.x[:, bass.ds(b * ST, ST), :].rearrange("p a d -> p (a d)")
                nc.vector.tensor_tensor(xb, xb, y[:].rearrange("p a d -> p (a d)"), ALU.add).then_inc(summed, 1)

            def choose(b):
                k = 0

                def done(ins):
                    nonlocal k
                    k += 1
                    ins.then_inc(pick_s, 1)
                    dve.wait_ge(pick_s, PICKS * b + k)

                dve.wait_ge(gated, b + 1)
                if late(b, 1):
                    dve.wait_ge(mixT_ps, b)
                done(nc.vector.tensor_copy(logits[:].rearrange("p i e -> p (i e)"), ps_m[:, 0:ST * E]))
                for r in range(2):
                    done(nc.vector.tensor_reduce(top[:, r, :], logits[:], X, ALU.max))
                    done(nc.vector.tensor_tensor(eq[:], logits[:], top[:, r, :].unsqueeze(2).broadcast_to([P, ST, E]), ALU.is_equal))
                    done(nc.vector.tensor_tensor(eq[:], eq[:], rev[:], ALU.mult))
                    done(nc.vector.tensor_reduce(pick[:], eq[:], X, ALU.max))
                    done(nc.vector.tensor_tensor(one[:, r], eq[:], pick[:].unsqueeze(2).broadcast_to([P, ST, E]), ALU.is_equal))
                    if r == 0:
                        done(nc.vector.scalar_tensor_tensor(logits[:], one[:, 0], NEG_MIN, logits[:], ALU.mult, ALU.add))
                done(nc.vector.tensor_tensor(diff[:], top[:, 1, :], top[:, 0, :], ALU.subtract))
                dve.wait_ge(ex_ready, b + 1)
                nc.vector.tensor_scalar(wt[:, 0, :], ex[:], 1.0, None, ALU.add).then_inc(weighed, 1)
                dve.wait_ge(weighed, 5 * b + 1)
                nc.vector.reciprocal(wt[:, 0, :], wt[:, 0, :]).then_inc(weighed, 1)
                dve.wait_ge(weighed, 5 * b + 2)
                nc.vector.tensor_tensor(wt[:, 1, :], wt[:, 0, :], ex[:], ALU.mult).then_inc(weighed, 1)
                dve.wait_ge(weighed, 5 * b + 3)
                for r in range(2):
                    last = nc.vector.tensor_tensor(part[:, r], one[:, r], wt[:, r, :].unsqueeze(2).broadcast_to([P, ST, E]), ALU.mult)
                    last.then_inc(weighed, 1)
                dve.wait_ge(weighed, 5 * b + 5)
                done(nc.vector.tensor_tensor(mix[:, :, 0:E], part[:, 0], part[:, 1], ALU.add))
                assert k == PICKS

            def take_mixT(b):
                dve.wait_ge(mixT_ps, b + 1)
                if late(b, 1):
                    dve.wait_ge(b2_ps, b)
                nc.vector.tensor_copy(mixT[:].rearrange("p i e -> p (i e)"), ps_c[:, 0:ST * P]).then_inc(mixT_ready, 1)
                dve.wait_ge(b2_ps, b + 1)
                dve.wait_ge(summed, SUMS * b + 5)
                xb = c.x[:, bass.ds(b * ST, ST), :].rearrange("p a d -> p (a d)")
                nc.vector.tensor_tensor(xb, xb, ps_m[:], ALU.add).then_inc(summed, 1)

            def add_expert(g, s, b):
                for i in range(ST):
                    dve.wait_ge(o_ps, 2 * g + i + 1)
                    dve.wait_ge(summed, SUMS * b + (1, 2 + i, 6)[s] if s < 3 else SUMS * b + place(s - 1) + i)
                    xt = c.x[:, bass.ds(b * ST + i, 1), :].rearrange("p a d -> p (a d)")
                    nc.vector.scalar_tensor_tensor(xt, ps_o[i][:, 0:D], mix[:, i, s:s + 1], xt, ALU.mult, ALU.add).then_inc(summed, 1)

            def slot(b, s):
                if at := lagged(b, s, 1, E):
                    if at[1] == 0:
                        add_y(at[2])
                    add_expert(*at)
                    if at[1] == E - 1:
                        dve.wait_ge(summed, SUMS * at[2] + SUMS)
                        batch_stats(nc, dve, c, stats, at[2])
                if s == 0 and late_batch(b):
                    choose(b)
                if s == 2:
                    take_mixT(b)
                if s == 4 and (not isinstance(b, int) or b + 1 < B):
                    normalise(b + 1)

            normalise(0)
            run_steps(dve, E, slot, LAST)

        @block.scalar
        def _(act):
            act.wait_ge(root, 3)
            nc.scalar.activation(rstd[:], c.mv[:, :, 1:2].rearrange("p a d -> p (a d)"), ACT.Sqrt, bias=c.eps[:]).then_inc(root, 1)
            act.wait_ge(root, 7)
            nc.scalar.activation(ms[:], ms[:], ACT.Sqrt, bias=rms_eps[:]).then_inc(root, 1)
            c.wait_weights(act, tag)

            def take_tT(b):
                act.wait_ge(tT_ps, b + 1)
                for dc in range(DC):
                    last = nc.scalar.mul(tT[:, dc, :], ps_m[:, dc * S:(dc + 1) * S], norm_w[:, dc:dc + 1])
                last.then_inc(tT_ready, 1)

            def gelu(g, s):
                for f in range(FC):
                    act.wait_ge(h_ps, FC * g + f + 1)
                    if late(g, 2) and f == 0:
                        act.wait_ge(o_ps, 2 * g - 2)
                    nc.scalar.activation(hT[:, s % 2, f, :], ps_h[f][:, 0:S], ACT.Gelu,
                                         bias=b1[:, FC * s + f:FC * s + f + 1]).then_inc(h_ready, 1)

            def slot(b, s):
                if at := lagged(b, s, 0, E):
                    gelu(at[0], at[1])
                if s == 0 and late_batch(b):
                    act.wait_ge(pick_s, PICKS * b + PICKS - 1)
                    if late(b, 1):
                        act.wait_ge(weighed, 5 * b)
                    nc.scalar.activation(ex[:], diff[:], ACT.Exp).then_inc(ex_ready, 1)
                if s == E - 1 and (not isinstance(b, int) or b + 1 < B):
                    take_tT(b + 1)

            take_tT(0)
            run_steps(act, E, slot, LAST)


def small_heads(nc, c, tag, w_qk, w_v, load_next, softmax, bq=None, bk=None, bv=None, w_out=None):
    STEPS, J, HD, W = 4, 4, 16, 32
    V_LAG = 3 if softmax else 2
    B_LAG = V_LAG + 1
    LAST = B_LAG if softmax else B_LAG + 2
    SW = ST * S if softmax else 3 * P
    with ExitStack() as ctx:
        sb = lambda name, shape: ctx.enter_context(nc.sbuf_tensor(f"{tag}_{name}", shape, F32))
        ps = lambda name: ctx.enter_context(nc.psum_tensor(f"{tag}_{name}", [P, 512], F32))
        sem = lambda name: ctx.enter_context(nc.semaphore(f"{tag}_{name}"))
        rstd = sb("rstd", [P, TILES])
        xn = sb("xn", [P, ST, D])
        xnT = sb("xnT", [P, DC, S])
        v_all = sb("v_all", [P, ST, D])
        qk = sb("qk", [P, 2, 2, S])
        split = sb("split", [P, 2, J, S])
        vp = sb("vp", [P, STEPS, ST, J, W])
        wT = sb("wT", [P, 2, J, SW])
        zT = sb("zT", [P, 2, S])
        den = sb("den", [P, ST, J])
        inv = sb("inv", [P, ST, J])
        if softmax:
            ctx_stage = sb("ctx_stage", [P, DC, S])
            ctxT = sb("ctxT", [P, DC, S])
            nmx = sb("nmx", [P, J, ST])
            pr = sb("pr", [P, J, ST, S])
            o = sb("o", [P, ST, J, HD])
        else:
            low = sb("low", [P, 2 * S])
            o_all = sb("o_all", [P, ST, D])
            oT = sb("oT", [P, DC, S])
        ps_p = ps("ps_p")
        ps_s = [ps(f"ps_s{j}") for j in range(J)]
        ps_z = ps("ps_z")
        ps_t = [ps("ps_t0"), ps("ps_t1")]

        root = sem("root")
        xn_ready = sem("xn_ready")
        xnT_ps = sem("xnT_ps")
        xnT_ready = sem("xnT_ready")
        ctx_in = sem("ctx_in")
        ctx_ready = sem("ctx_ready")
        proj = sem("proj")
        v_ps = sem("v_ps")
        v_taken = sem("v_taken")
        qk_ready = sem("qk_ready")
        phi_s = sem("phi_s")
        filled = sem("filled")
        v_ready = sem("v_ready")
        split_ready = sem("split_ready")
        scored = sem("scored")
        maxed = sem("maxed")
        exped = sem("exped")
        turned = sem("turned")
        w_even = sem("w_even")
        w_odd = sem("w_odd")
        z_done = sem("z_done")
        zT_ready = sem("zT_ready")
        backed = sem("backed")
        den_s = sem("den_s")
        o_ready = sem("o_ready")
        oT_ps = sem("oT_ps")
        oT_ready = sem("oT_ready")
        out_ps = sem("out_ps")
        added = sem("added")
        stats = sem("stats")

        block = ctx.enter_context(nc.Block())

        @block.sync
        def _(sp):
            if not softmax:
                load_next(sp)
            else:
                def batch(b):
                    if late(b, 1):
                        sp.wait_ge(ctx_ready, b)
                    sp.dma_start(ctx_stage[:], c.dram["ctxT"][:, bass.ds(b, 1), :, :].rearrange("p a c s -> p (a c) s")).then_inc(ctx_in, 16)
                batch(0)
                load_next(sp)
                with sp.Fori(1, B) as b:
                    batch(b)

        if softmax:
            @block.gpsimd
            def _(pool):
                def batch(b):
                    pool.wait_ge(ctx_in, 16 * b + 16)
                    if late(b, 1):
                        pool.wait_ge(proj, 2 * b)
                    pool.sem_inc(c.pool_waited, 1)
                    nc.gpsimd.tensor_copy(ctxT[:], ctx_stage[:]).then_inc(ctx_ready, 1)
                batch(0)
                with pool.Fori(1, B) as b:
                    batch(b)

        @block.tensor
        def _(pe):
            c.wait_weights(pe, tag)
            src = ctxT if softmax else xnT

            def turn_x(b):
                pe.wait_ge(xn_ready, b + 1)
                if late(b, 1):
                    pe.wait_ge(qk_ready, 2 * b)
                for dc in range(DC):
                    for i in range(ST):
                        last = nc.tensor.transpose(ps_p[:, dc * S + i * P:dc * S + (i + 1) * P],
                                                   xn[:, i, dc * P:(dc + 1) * P], c.ident[:])
                last.then_inc(xnT_ps, 1)

            def project(g, s, b):
                if s == 0:
                    pe.wait_ge(xnT_ready, b + 1)
                    if softmax:
                        pe.wait_ge(ctx_ready, b + 1)
                if s == 1:
                    pe.wait_ge(qk_ready, 2 * b + 1)
                    for i in range(ST):
                        for dc in range(DC):
                            last = nc.tensor.matmul(ps_p[:, i * D:(i + 1) * D], src[:, dc, i * P:(i + 1) * P],
                                                    w_v[:, dc, :], start=(dc == 0), stop=(dc == DC - 1))
                    last.then_inc(v_ps, 1)
                if s == 2:
                    pe.wait_ge(v_taken, b + 1)
                if s % 2 == 0:
                    for w in range(2):
                        for dc in range(DC):
                            last = nc.tensor.matmul(ps_p[:, w * S:(w + 1) * S], w_qk[:, s // 2, w, dc, :],
                                                    (xnT if w == 0 else src)[:, dc, :], start=(dc == 0), stop=(dc == DC - 1))
                    last.then_inc(proj, 1)

            def scores(g, s, j):
                if j == 0:
                    pe.wait_ge(split_ready, g + 1)
                if late(g, 1):
                    if softmax:
                        pe.wait_ge(exped, J * g + j - J + 1)
                    else:
                        pe.wait_ge((w_even, w_odd)[j % 2], 2 * g - 1 + j // 2)
                for i in range(ST):
                    if softmax:
                        last = nc.tensor.matmul(ps_s[j][:, i * S:(i + 1) * S], split[:, s % 2, j, i * P:(i + 1) * P],
                                                qk[:, s // 2, 1, :], start=True, stop=True)
                    else:
                        last = nc.tensor.matmul(ps_s[j][:, i * S:(i + 1) * S - i * P], split[:, s % 2, j, i * P:(i + 1) * P],
                                                qk[:, s // 2, 0, i * P:S], start=True, stop=True)
                last.then_inc(scored, 1)

            def turn(g, s, j):
                pe.wait_ge(exped, J * g + j + 1)
                if late(g, 1) or j >= 2:
                    pe.wait_ge((w_even, w_odd)[j % 2], 2 * g + j // 2)
                for i in range(ST):
                    for t in range(ST):
                        last = nc.tensor.transpose(ps_t[j % 2][:, t * S + i * P:t * S + (i + 1) * P],
                                                   pr[:, j, i, t * P:(t + 1) * P], c.ident[:])
                last.then_inc(turned, 1)

            def values(g, s):
                pe.wait_ge(v_ready, g + 1)
                pe.wait_ge(w_even, 2 * g + 2)
                pe.wait_ge(w_odd, 2 * g + 2)
                if late(g, 1):
                    pe.wait_ge(zT_ready, g)
                    pe.wait_ge(o_ready, g)
                for t in range(ST):
                    q0 = 0 if softmax else t * P
                    for j in range(J):
                        last = nc.tensor.matmul(ps_z[W * j:W * (j + 1), q0:S], vp[:, s, t, j, :],
                                                wT[:, s % 2, j, t * S:t * S + S - q0], start=(t == 0), stop=(t == ST - 1),
                                                tile_position=(0, W * j))
                last.then_inc(z_done, 1)

            def back(g, s):
                pe.wait_ge(zT_ready, g + 1)
                for i in range(ST):
                    last = nc.tensor.transpose(ps_z[:, S + i * P:S + (i + 1) * P], zT[:, s % 2, i * P:(i + 1) * P], c.ident[:])
                last.then_inc(backed, 1)

            def turn_o(b):
                pe.wait_ge(o_ready, STEPS * b + STEPS)
                if late(b, 1):
                    pe.wait_ge(added, b)
                for dc in range(DC):
                    for i in range(ST):
                        last = nc.tensor.transpose(ps_t[0][:, dc * S + i * P:dc * S + (i + 1) * P],
                                                   o_all[:, i, dc * P:(dc + 1) * P], c.ident[:])
                last.then_inc(oT_ps, 1)

            def output(b):
                pe.wait_ge(oT_ready, b + 1)
                for i in range(ST):
                    for dc in range(DC):
                        last = nc.tensor.matmul(ps_t[0][:, i * D:(i + 1) * D], oT[:, dc, i * P:(i + 1) * P],
                                                w_out[:, dc, :], start=(dc == 0), stop=(dc == DC - 1))
                last.then_inc(out_ps, 1)

            def slot(b, s):
                if at := lagged(b, s, 0, STEPS):
                    project(*at)
                if at := lagged(b, s, B_LAG, STEPS):
                    back(at[0], at[1])
                if w_out is not None and (at := lagged(b, s, B_LAG + 1, STEPS)) and at[1] == STEPS - 1:
                    turn_o(at[2])
                for j in range(J):
                    if at := lagged(b, s, 1, STEPS):
                        scores(at[0], at[1], j)
                    if softmax and (at := lagged(b, s, 2, STEPS)):
                        turn(at[0], at[1], j)
                if s == STEPS - 1 and (not isinstance(b, int) or b + 1 < B):
                    turn_x(b + 1)
                if at := lagged(b, s, V_LAG, STEPS):
                    values(at[0], at[1])
                if w_out is not None:
                    if (at := lagged(b, s, B_LAG + 2, STEPS)) and at[1] == STEPS - 1:
                        output(at[2])

            turn_x(0)
            run_steps(pe, STEPS, slot, LAST)

        @block.vector
        def _(dve):
            nc.vector.memset(vp[:], 0.0).then_inc(filled, 1)
            dve.wait_ge(filled, 1)
            nc.vector.memset(vp[:, :, :, :, HD:HD + 1], 1.0).then_inc(filled, 1)
            dve.wait_ge(root, 1)
            nc.vector.reciprocal(rstd[:], rstd[:]).then_inc(root, 1)
            dve.wait_ge(root, 2)
            dve.wait_ge(filled, 2)
            c.wait_weights(dve, tag)

            def normalise(b):
                if late(b, 1):
                    dve.wait_ge(xnT_ps, b)
                for i in range(ST):
                    n = b * ST + i
                    last = nc.vector.tensor_scalar(xn[:, i, :], c.x[:, bass.ds(n, 1), :].rearrange("p a d -> p (a d)"),
                                                   c.mv[:, bass.ds(n, 1), 0:1].rearrange("p a d -> p (a d)"),
                                                   rstd[:, bass.ds(n, 1)], ALU.subtract, ALU.mult)
                last.then_inc(xn_ready, 1)

            def features(g, s, b):
                n = 2 * b + s // 2
                dve.wait_ge(proj, n + 1)
                if late(g, 1):
                    dve.wait_ge(qk_ready, n)
                nc.vector.tensor_scalar(low[:], ps_p[:], 0.0, None, ALU.min).then_inc(phi_s, 1)
                dve.wait_ge(phi_s, 2 * n + 2)
                if late(g, STEPS):
                    dve.wait_ge(scored, J * g - 2 * J)
                nc.vector.scalar_tensor_tensor(qk[:, s // 2].rearrange("p w s -> p (w s)"), ps_p[:], 0.0, low[:],
                                               ALU.max, ALU.add).then_inc(qk_ready, 1)

            def fill_v(g, s, b):
                dve.wait_ge(v_taken, b + 1)
                if late(g, STEPS):
                    dve.wait_ge(z_done, g - STEPS + 1)
                for i in range(ST):
                    got = v_all[:, i, s * J * HD:(s + 1) * J * HD].rearrange("p (j e) -> p j e", j=J)
                    if bv is not None:
                        last = nc.vector.tensor_tensor(vp[:, s, i, :, 0:HD], got,
                                                       bv[:, s * J * HD:(s + 1) * J * HD].rearrange("p (j e) -> p j e", j=J), ALU.add)
                    else:
                        last = nc.vector.tensor_copy(vp[:, s, i, :, 0:HD], got)
                last.then_inc(v_ready, 1)

            def apart(g, s, b):
                dve.wait_ge(qk_ready, 2 * b + s // 2 + 1)
                if late(g, 2):
                    dve.wait_ge(scored, J * g - J)
                which, mask = (0, c.head16) if softmax else (1, c.head16k)
                for j in range(J):
                    m = J * (s % 2) + j
                    last = nc.vector.tensor_scalar(split[:, s % 2, j, :], qk[:, s // 2, which, :], mask[:, m:m + 1], None, ALU.mult)
                last.then_inc(split_ready, 1)

            def row_max(g, s, j):
                dve.wait_ge(scored, J * g + j + 1)
                if late(g, 1):
                    dve.wait_ge(exped, J * g + j - J + 1)
                nc.vector.tensor_reduce(nmx[:, j, :], ps_s[j][:].rearrange("p (i s) -> p i s", i=ST), X, ALU.max,
                                        negate=True).then_inc(maxed, 1)

            def take_odd(g, s, j):
                dve.wait_ge(turned, J * g + j + 1)
                if late(g, 2):
                    dve.wait_ge(z_done, g - 1)
                nc.vector.tensor_copy(wT[:, s % 2, j, :], ps_t[1][:]).then_inc(w_odd, 1)

            def keep_past(g, s, j):
                dve.wait_ge(scored, J * g + j + 1)
                if late(g, 2):
                    dve.wait_ge(z_done, g - 1)
                nc.vector.tensor_tensor(wT[:, s % 2, j, :], ps_s[j][:, 0:SW], c.keep[:], ALU.mult).then_inc((w_even, w_odd)[j % 2], 1)

            def finish(g, s, b):
                z = ps_z[:, S:2 * S].rearrange("p (i j w) -> p i j w", i=ST, j=J)
                dve.wait_ge(backed, g + 1)
                nc.vector.tensor_scalar(den[:], z[:, :, :, HD:HD + 1].rearrange("p i j w -> p i (j w)"), 1e-6, None,
                                        ALU.max).then_inc(den_s, 1)
                dve.wait_ge(den_s, 2 * g + 1)
                nc.vector.reciprocal(inv[:], den[:]).then_inc(den_s, 1)
                dve.wait_ge(den_s, 2 * g + 2)
                if softmax:
                    if late(g, 1):
                        dve.wait_ge(added, g)
                    dst = o[:]
                else:
                    if s == 0 and late(g, STEPS):
                        dve.wait_ge(oT_ps, b)
                    dst = o_all[:, :, s * J * HD:(s + 1) * J * HD].rearrange("p i (j e) -> p i j e", j=J)
                for i in range(ST):
                    last = nc.vector.tensor_tensor(dst[:, i], z[:, i, :, 0:HD],
                                                   inv[:, i, :].unsqueeze(2).broadcast_to([P, J, HD]), ALU.mult)
                last.then_inc(o_ready, 1)
                if softmax:
                    dve.wait_ge(o_ready, g + 1)
                    xs = c.x[:, bass.ds(b * ST, ST), s * J * HD:(s + 1) * J * HD]
                    nc.vector.tensor_tensor(xs, xs, o[:].rearrange("p i j e -> p i (j e)"), ALU.add).then_inc(added, 1)
                    if s == STEPS - 1:
                        dve.wait_ge(added, g + 1)
                        batch_stats(nc, dve, c, stats, b)

            def add_output(b):
                dve.wait_ge(out_ps, b + 1)
                xb = c.x[:, bass.ds(b * ST, ST), :].rearrange("p a d -> p (a d)")
                nc.vector.tensor_tensor(xb, xb, ps_t[0][:], ALU.add).then_inc(added, 1)
                dve.wait_ge(added, b + 1)
                batch_stats(nc, dve, c, stats, b)

            def slot(b, s):
                if at := lagged(b, s, 0, STEPS):
                    if not softmax and s % 2 == 0:
                        features(*at)
                    apart(*at)
                if at := lagged(b, s, B_LAG, STEPS):
                    finish(*at)
                if at := lagged(b, s, 1, STEPS):
                    fill_v(*at)
                for j in range(J):
                    if at := lagged(b, s, 1, STEPS):
                        if softmax:
                            row_max(at[0], at[1], j)
                        else:
                            keep_past(at[0], at[1], j)
                    if softmax and j % 2 and (at := lagged(b, s, 2, STEPS)):
                        take_odd(at[0], at[1], j)
                if w_out is not None and (at := lagged(b, s, B_LAG + 2, STEPS)) and at[1] == STEPS - 1:
                    add_output(at[2])
                if s == 1 and (not isinstance(b, int) or b + 1 < B):
                    normalise(b + 1)

            normalise(0)
            run_steps(dve, STEPS, slot, LAST)

        @block.scalar
        def _(act):
            nc.scalar.activation(rstd[:], c.mv[:, :, 1:2].rearrange("p a d -> p (a d)"), ACT.Sqrt,
                                 bias=c.eps[:]).then_inc(root, 1)
            c.wait_weights(act, tag)

            def take_xT(b):
                act.wait_ge(xnT_ps, b + 1)
                nc.scalar.copy(xnT[:].rearrange("p c s -> p (c s)"), ps_p[:]).then_inc(xnT_ready, 1)

            def take_qk(g, s, b):
                if s % 2:
                    return
                n = 2 * b + s // 2
                if softmax:
                    act.wait_ge(proj, n + 1)
                    if late(g, STEPS):
                        act.wait_ge(scored, J * g - 2 * J)
                    for w, bias in enumerate((bq, bk)):
                        last = nc.scalar.activation(qk[:, s // 2, w, :], ps_p[:, w * S:(w + 1) * S], ACT.Identity,
                                                    bias=bias[:, s // 2:s // 2 + 1])
                    last.then_inc(qk_ready, 1)
                else:
                    act.wait_ge(phi_s, 2 * n + 1)
                    nc.scalar.activation(low[:], low[:], ACT.Exp).then_inc(phi_s, 1)

            def take_v(b):
                act.wait_ge(v_ps, b + 1)
                if late(b, 1):
                    act.wait_ge(v_ready, STEPS * b)
                nc.scalar.copy(v_all[:].rearrange("p i d -> p (i d)"), ps_p[:]).then_inc(v_taken, 1)

            def exponentials(g, s, j):
                act.wait_ge(maxed, J * g + j + 1)
                if late(g, 1):
                    act.wait_ge(turned, J * g + j - J + 1)
                for i in range(ST):
                    last = nc.scalar.activation(pr[:, j, i, :], ps_s[j][:, i * S:(i + 1) * S], ACT.Exp, bias=nmx[:, j, i:i + 1])
                last.then_inc(exped, 1)

            def take_even(g, s, j):
                act.wait_ge(turned, J * g + j + 1)
                if late(g, 2):
                    act.wait_ge(z_done, g - 1)
                nc.scalar.copy(wT[:, s % 2, j, :], ps_t[0][:]).then_inc(w_even, 1)

            def take_z(g, s):
                act.wait_ge(z_done, g + 1)
                if late(g, 2):
                    act.wait_ge(backed, g - 1)
                nc.scalar.copy(zT[:, s % 2, :], ps_z[:, 0:S]).then_inc(zT_ready, 1)

            def slot(b, s):
                if at := lagged(b, s, 0, STEPS):
                    take_qk(*at)
                    if s == 1:
                        take_v(b)
                if softmax:
                    for j in range(J):
                        if at := lagged(b, s, 1, STEPS):
                            exponentials(at[0], at[1], j)
                        if j % 2 == 0 and (at := lagged(b, s, 2, STEPS)):
                            take_even(at[0], at[1], j)
                if s == STEPS - 1 and (not isinstance(b, int) or b + 1 < B):
                    take_xT(b + 1)
                if at := lagged(b, s, V_LAG, STEPS):
                    take_z(at[0], at[1])
                if w_out is not None and (at := lagged(b, s, B_LAG + 1, STEPS)) and at[1] == STEPS - 1:
                    act.wait_ge(oT_ps, at[2] + 1)
                    if late(at[2], 1):
                        act.wait_ge(out_ps, at[2])
                    nc.scalar.copy(oT[:].rearrange("p c s -> p (c s)"), ps_t[0][:]).then_inc(oT_ready, 1)

            take_xT(0)
            run_steps(act, STEPS, slot, LAST)


def gated_heads(nc, c, tag, w_qk, w_gate, w_val, w_out, load_next):
    STEPS, E, HEADS, LAST = 4, 8, 8, 5
    K = 4
    with ExitStack() as ctx:
        sb = lambda name, shape: ctx.enter_context(nc.sbuf_tensor(f"{tag}_{name}", shape, F32))
        ps = lambda name: ctx.enter_context(nc.psum_tensor(f"{tag}_{name}", [P, 512], F32))
        sem = lambda name: ctx.enter_context(nc.semaphore(f"{tag}_{name}"))
        rstd = sb("rstd", [P, TILES])
        xn = sb("xn", [P, ST, D])
        xnT = sb("xnT", [P, DC, S])
        rev = sb("rev", [P, ST * HEADS, E])
        gate = sb("gate", [P, ST * HEADS, E])
        eq = sb("eq", [P, ST * HEADS, E])
        best = sb("best", [P, ST * HEADS])
        gm = sb("gm", [P, ST * HEADS, E])
        gm_step = sb("gm_step", [P, STEPS, ST, 2, E])
        gm_late = sb("gm_late", [P, STEPS, ST, 2, E])
        qT = sb("qT", [P, 2, 2, S])
        kT = sb("kT", [P, 2, S])
        gv = sb("gv", [P, 2, E, 64])
        v = sb("v", [P, STEPS, ST, P])
        sm = sb("sm", [P, 2, ST, S])
        mx = sb("mx", [P, 2, ST])
        nmx = sb("nmx", [P, 2, ST])
        pr = sb("pr", [P, 4, ST, S])
        sums = sb("sums", [P, 4, ST])
        inv = sb("inv", [P, 4, ST])
        prT = sb("prT", [P, 4, ST, S])
        zT = sb("zT", [P, 2, S])
        z = sb("z", [P, ST, P])
        zg = sb("zg", [P, 2, E, 64])
        zgT = sb("zgT", [P, 2, 4, P])
        ps_qk, ps_s, ps_t, ps_g, ps_z, ps_out = (ps(n) for n in ("ps_qk", "ps_s", "ps_t", "ps_g", "ps_z", "ps_out"))
        ps_v = [ps("ps_v0"), ps("ps_v1")]

        root = sem("root")
        xn_ready = sem("xn_ready")
        xnT_ps = sem("xnT_ps")
        xnT_ready = sem("xnT_ready")
        gate_ps = sem("gate_ps")
        gate_exp = sem("gate_exp")
        pick_s = sem("pick_s")
        piece = sem("piece")
        kept = sem("kept")
        proj = sem("proj")
        q_ready = sem("q_ready")
        v_ps = sem("v_ps")
        v_gated = sem("v_gated")
        v_ready = sem("v_ready")
        scored = sem("scored")
        maxed = sem("maxed")
        negated = sem("negated")
        exped = sem("exped")
        inverted = sem("inverted")
        normed = sem("normed")
        turned = sem("turned")
        prT_ready = sem("prT_ready")
        z_done = sem("z_done")
        zT_ready = sem("zT_ready")
        backed = sem("backed")
        z_ready = sem("z_ready")
        zg_ready = sem("zg_ready")
        zg_ps = sem("zg_ps")
        zgT_ready = sem("zgT_ready")
        out_ps = sem("out_ps")
        added = sem("added")
        stored = sem("stored")
        PICKS = 8

        block = ctx.enter_context(nc.Block())

        @block.sync
        def _(sp):
            load_next(sp)

            def batch(b):
                sp.wait_ge(added, b + 1)
                sp.dma_start(c.out[:, bass.ds(b * ST, ST), :], c.x[:, bass.ds(b * ST, ST), :]).then_inc(stored, 16)
            batch(0)
            with sp.Fori(1, B) as b:
                batch(b)
            sp.wait_ge(stored, 16 * B)

        @block.gpsimd
        def _(pool):
            nc.gpsimd.iota(rev[:], pattern=[[0, ST * HEADS], [-1, E]], base=E, channel_multiplier=0,
                           allow_small_or_imprecise_dtypes=True).then_inc(root, 1)

        @block.tensor
        def _(pe):
            c.wait_weights(pe, tag)

            def turn_x(b):
                pe.wait_ge(xn_ready, b + 1)
                if late(b, 1):
                    pe.wait_ge(q_ready, STEPS * b)
                for dc in range(DC):
                    for i in range(ST):
                        last = nc.tensor.transpose(ps_qk[:, dc * S + i * P:dc * S + (i + 1) * P],
                                                   xn[:, i, dc * P:(dc + 1) * P], c.ident[:])
                last.then_inc(xnT_ps, 1)

            def gates(b):
                pe.wait_ge(xnT_ready, b + 1)
                if late(b, 2):
                    pe.wait_ge(zgT_ready, K * (STEPS * b - LAST))
                for i in range(ST):
                    for dc in range(DC):
                        last = nc.tensor.matmul(ps_g[:, i * E * HEADS:(i + 1) * E * HEADS], xnT[:, dc, i * P:(i + 1) * P],
                                                w_gate[:, dc, :], start=(dc == 0), stop=(dc == DC - 1))
                last.then_inc(gate_ps, 1)

            def project(g, s):
                if late(g, 1):
                    pe.wait_ge(q_ready, g)
                for w in range(2):
                    for dc in range(DC):
                        last = nc.tensor.matmul(ps_qk[:, w * S:(w + 1) * S], w_qk[:, s, w, dc, :], xnT[:, dc, :],
                                                start=(dc == 0), stop=(dc == DC - 1))
                last.then_inc(proj, 1)

            def project_v(g, s, k):
                j, i = k // 2, k % 2
                if late(g, 1) or k >= 2:
                    pe.wait_ge(v_gated, K * g + k - 1)
                for dc in range(DC):
                    last = nc.tensor.matmul(ps_v[i][:], xnT[:, dc, i * P:(i + 1) * P], w_val[:, 2 * s + j, dc, :],
                                            start=(dc == 0), stop=(dc == DC - 1))
                last.then_inc(v_ps, 1)

            def scores(g, s, j):
                pe.wait_ge(q_ready, g + 1)
                if late(g, 1) or j:
                    pe.wait_ge(maxed, 2 * g + j)
                for i in range(ST):
                    last = nc.tensor.matmul(ps_s[:, i * S:i * S + (i + 1) * P], qT[:, s % 2, j, i * P:(i + 1) * P],
                                            kT[:, s % 2, 0:(i + 1) * P], start=True, stop=True)
                last.then_inc(scored, 1)

            def turn(g, s, j):
                pe.wait_ge(normed, 2 * g + j + 1)
                if late(g, 1) or j:
                    pe.wait_ge(prT_ready, 2 * g + j)
                for i in range(ST):
                    for t in range(i + 1):
                        last = nc.tensor.transpose(ps_t[:, t * S + i * P:t * S + (i + 1) * P],
                                                   pr[:, 2 * (s % 2) + j, i, t * P:(t + 1) * P], c.ident[:])
                last.then_inc(turned, 1)

            def values(g, s):
                pe.wait_ge(v_ready, K * g + K)
                pe.wait_ge(prT_ready, 2 * g + 2)
                if late(g, 1):
                    pe.wait_ge(zT_ready, g)
                    pe.wait_ge(z_ready, g)
                for t in range(ST):
                    for j in range(2):
                        last = nc.tensor.matmul(ps_z[64 * j:64 * j + 64, t * P:S], v[:, s, t, 64 * j:64 * j + 64],
                                                prT[:, 2 * (s % 2) + j, t, t * P:S], start=(t == 0), stop=(t == ST - 1))
                last.then_inc(z_done, 1)

            def back(g, s):
                pe.wait_ge(zT_ready, g + 1)
                for i in range(ST):
                    last = nc.tensor.transpose(ps_z[:, S + i * P:S + (i + 1) * P], zT[:, s % 2, i * P:(i + 1) * P], c.ident[:])
                last.then_inc(backed, 1)

            def turn_zg(g, s, k, b):
                pe.wait_ge(zg_ready, K * g + k + 1)
                if late(g, 1) or k:
                    pe.wait_ge(zgT_ready, K * g + k)
                if s == STEPS - LAST % STEPS and k == 0:
                    pe.wait_ge(gate_exp, b)
                for p in range(E // 2):
                    last = nc.tensor.transpose(ps_g[:, p * P:(p + 1) * P],
                                               zg[:, k % 2, 2 * p:2 * p + 2, :].rearrange("p e k -> p (e k)"), c.ident[:])
                last.then_inc(zg_ps, 1)

            def output(g, s, k, b):
                j, i = k // 2, k % 2
                pe.wait_ge(zgT_ready, K * g + k + 1)
                if s == 0 and k == 0 and late(g, STEPS):
                    pe.wait_ge(added, b)
                for p in range(E // 2):
                    last = nc.tensor.matmul(ps_out[:, i * D:(i + 1) * D], zgT[:, k % 2, p, :], w_out[:, 2 * s + j, p, :],
                                            start=(s == 0 and k == 0 and p == 0), stop=(s == STEPS - 1 and j == 1 and p == E // 2 - 1),
                                            skip_group_check=True)
                last.then_inc(out_ps, 1)

            def slot(b, s):
                now, one, two = (lagged(b, s, d, STEPS) for d in range(3))
                five = lagged(b, s, 5, STEPS)
                if now:
                    if s == 0:
                        gates(b)
                    project(now[0], s)
                if at := lagged(b, s, 4, STEPS):
                    back(at[0], at[1])
                for k in range(K):
                    if now:
                        project_v(now[0], s, k)
                    if k % 2 == 0 and one:
                        scores(one[0], one[1], k // 2)
                    if k % 2 and two:
                        turn(two[0], two[1], k // 2)
                    if five:
                        turn_zg(five[0], five[1], k, b if now else B)
                        if k:
                            output(five[0], five[1], k - 1, five[2])
                if s == STEPS - 1 and (not isinstance(b, int) or b + 1 < B):
                    turn_x(b + 1)
                if at := lagged(b, s, 3, STEPS):
                    values(at[0], at[1])
                if five:
                    output(five[0], five[1], K - 1, five[2])

            turn_x(0)
            run_steps(pe, STEPS, slot, LAST)

        @block.vector
        def _(dve):
            dve.wait_ge(root, 2)
            nc.vector.reciprocal(rstd[:], rstd[:]).then_inc(root, 1)
            dve.wait_ge(root, 3)

            def normalise(b):
                if late(b, 1):
                    dve.wait_ge(xnT_ps, b)
                for i in range(ST):
                    n = b * ST + i
                    last = nc.vector.tensor_scalar(xn[:, i, :], c.x[:, bass.ds(n, 1), :].rearrange("p a d -> p (a d)"),
                                                   c.mv[:, bass.ds(n, 1), 0:1].rearrange("p a d -> p (a d)"),
                                                   rstd[:, bass.ds(n, 1)], ALU.subtract, ALU.mult)
                last.then_inc(xn_ready, 1)

            def choose(b):
                k = 0

                def done(ins):
                    nonlocal k
                    k += 1
                    ins.then_inc(pick_s, 1)
                    dve.wait_ge(pick_s, PICKS * b + k)

                wide = lambda a: a[:].unsqueeze(2).broadcast_to([P, ST * HEADS, E])
                dve.wait_ge(gate_exp, b + 1)
                done(nc.vector.tensor_scalar(gate[:], gate[:], 1.0, None, ALU.add))
                done(nc.vector.reciprocal(gate[:], gate[:]))
                done(nc.vector.tensor_reduce(best[:], gate[:], X, ALU.max))
                done(nc.vector.tensor_tensor(eq[:], gate[:], wide(best), ALU.is_equal))
                done(nc.vector.tensor_tensor(eq[:], eq[:], rev[:], ALU.mult))
                done(nc.vector.tensor_reduce(best[:], eq[:], X, ALU.max))
                done(nc.vector.tensor_tensor(eq[:], eq[:], wide(best), ALU.is_equal))
                if late(b, 1):
                    dve.wait_ge(piece, STEPS * b)
                done(nc.vector.tensor_tensor(gm[:], eq[:], gate[:], ALU.mult))

            def cut_piece(g, s):
                if late(g, STEPS):
                    dve.wait_ge(kept, g - STEPS + 1)
                nc.vector.tensor_scalar(gm_step[:, s], gm[:].rearrange("p (i h) e -> p i h e", i=ST)[:, :, 2 * s:2 * s + 2, :],
                                        1.0, None, ALU.mult).then_inc(piece, 1)
                dve.wait_ge(piece, g + 1)

            def keep_piece(g, s):
                if late(g, STEPS):
                    dve.wait_ge(zg_ready, K * (g - STEPS + 1))
                nc.vector.tensor_copy(gm_late[:, s], gm_step[:, s]).then_inc(kept, 1)

            def gate_v(g, s, k):
                j, i = k // 2, k % 2
                dve.wait_ge(v_ps, K * g + k + 1)
                if late(g, 1) or k >= 2:
                    dve.wait_ge(v_ready, K * g + k - 1)
                nc.vector.tensor_tensor(gv[:, k % 2], ps_v[i][:].rearrange("p (e k) -> p e k", e=E),
                                        gm_step[:, s, i, j, :].unsqueeze(2).broadcast_to([P, E, 64]), ALU.mult).then_inc(v_gated, 1)

            def sum_v(g, s, k):
                j, i = k // 2, k % 2
                dve.wait_ge(v_gated, K * g + k + 1)
                if late(g, STEPS):
                    dve.wait_ge(z_done, g - STEPS + 1)
                nc.vector.tensor_reduce(v[:, s, i, 64 * j:64 * j + 64], gv[:, k % 2].rearrange("p e k -> p k e"), X,
                                        ALU.add).then_inc(v_ready, 1)

            def row_max(g, s, j):
                dve.wait_ge(scored, 2 * g + j + 1)
                if late(g, 1):
                    dve.wait_ge(exped, 2 * g + j - 1)
                dve.sem_inc(c.waited, 1)
                for i in range(ST):
                    n = (i + 1) * P
                    add = c.causal_min[:, (ST - 1 - i) * P:(ST - 1 - i) * P + n]
                    last = nc.vector.tensor_tensor_reduce(sm[:, j, i, 0:n], ps_s[:, i * S:i * S + n], add, 1.0,
                                                          -3.0e38, ALU.add, ALU.max, mx[:, j, i:i + 1])
                last.then_inc(maxed, 1)
                dve.wait_ge(maxed, 2 * g + j + 1)
                nc.vector.tensor_scalar(nmx[:, j, :], mx[:, j, :], -1.0, None, ALU.mult).then_inc(negated, 1)

            def norm(g, s, j):
                r = 2 * (s % 2) + j
                dve.wait_ge(exped, 2 * g + j + 1)
                nc.vector.reciprocal(inv[:, r, :], sums[:, r, :]).then_inc(inverted, 1)
                dve.wait_ge(inverted, 2 * g + j + 1)
                for i in range(ST):
                    n = (i + 1) * P
                    last = nc.vector.tensor_scalar(pr[:, r, i, 0:n], pr[:, r, i, 0:n], inv[:, r, i:i + 1], None, ALU.mult)
                last.then_inc(normed, 1)

            def take_z(g):
                dve.wait_ge(backed, g + 1)
                if late(g, 1):
                    dve.wait_ge(zg_ready, K * g)
                nc.vector.tensor_copy(z[:].rearrange("p i m -> p (i m)"), ps_z[:, S:2 * S]).then_inc(z_ready, 1)

            def gate_z(g, s, k):
                j, i = k // 2, k % 2
                dve.wait_ge(z_ready, g + 1)
                dve.wait_ge(kept, g + 1)
                if late(g, 1) or k >= 2:
                    dve.wait_ge(zg_ps, K * g + k - 1)
                nc.vector.tensor_tensor(zg[:, k % 2], z[:, i, 64 * j:64 * j + 64].unsqueeze(1).broadcast_to([P, E, 64]),
                                        gm_late[:, s, i, j, :].unsqueeze(2).broadcast_to([P, E, 64]), ALU.mult).then_inc(zg_ready, 1)

            def add_to_x(b):
                dve.wait_ge(out_ps, K * STEPS * (b + 1))
                xb = c.x[:, bass.ds(b * ST, ST), :].rearrange("p a d -> p (a d)")
                nc.vector.tensor_tensor(xb, xb, ps_out[:], ALU.add).then_inc(added, 1)

            def slot(b, s):
                now, one, five = (lagged(b, s, d, STEPS) for d in (0, 1, 5))
                if now and s == 0:
                    choose(b)
                for k in range(K):
                    if five:
                        gate_z(five[0], five[1], k)
                    if now:
                        if k == 0:
                            cut_piece(now[0], s)
                        gate_v(now[0], s, k)
                    if one and k % 2 == 0:
                        row_max(one[0], one[1], k // 2)
                    if now:
                        sum_v(now[0], s, k)
                    if one and k % 2:
                        norm(one[0], one[1], k // 2)
                if at := lagged(b, s, 3, STEPS):
                    keep_piece(at[0], at[1])
                if at := lagged(b, s, 4, STEPS):
                    take_z(at[0])
                if five and five[1] == STEPS - 1:
                    add_to_x(five[2])
                if s == 1 and (not isinstance(b, int) or b + 1 < B):
                    normalise(b + 1)

            normalise(0)
            run_steps(dve, STEPS, slot, LAST)

        @block.scalar
        def _(act):
            act.wait_ge(root, 1)
            nc.scalar.activation(rstd[:], c.mv[:, :, 1:2].rearrange("p a d -> p (a d)"), ACT.Sqrt,
                                 bias=c.eps[:]).then_inc(root, 1)

            def take_xT(b):
                act.wait_ge(xnT_ps, b + 1)
                nc.scalar.copy(xnT[:].rearrange("p c s -> p (c s)"), ps_qk[:]).then_inc(xnT_ready, 1)

            def take_gates(b):
                act.wait_ge(gate_ps, b + 1)
                if late(b, 1):
                    act.wait_ge(pick_s, PICKS * b)
                nc.scalar.activation(gate[:].rearrange("p h e -> p (h e)"), ps_g[:, 0:ST * HEADS * E], ACT.Exp,
                                     scale=-1.0).then_inc(gate_exp, 1)

            def take_qk(g, s):
                act.wait_ge(proj, g + 1)
                if late(g, 2):
                    act.wait_ge(scored, 2 * g - 2)
                for j in range(2):
                    nc.scalar.mul(qT[:, s % 2, j, :], ps_qk[:, 0:S], c.half[:, j:j + 1])
                nc.scalar.copy(kT[:, s % 2, :], ps_qk[:, S:2 * S]).then_inc(q_ready, 1)

            def exponentials(g, s, j):
                r = 2 * (s % 2) + j
                act.wait_ge(negated, 2 * g + j + 1)
                if late(g, 2):
                    act.wait_ge(turned, 2 * g + j - 3)
                for i in range(ST):
                    n = (i + 1) * P
                    last = nc.scalar.activation(pr[:, r, i, 0:n], sm[:, j, i, 0:n], ACT.Exp, bias=nmx[:, j, i:i + 1],
                                                accum_out=sums[:, r, i:i + 1])
                last.then_inc(exped, 1)

            def take_prT(g, s, j):
                r = 2 * (s % 2) + j
                act.wait_ge(turned, 2 * g + j + 1)
                if late(g, 2):
                    act.wait_ge(z_done, g - 1)
                nc.scalar.copy(prT[:, r, 0, :], ps_t[:, 0:S])
                nc.scalar.copy(prT[:, r, 1, P:S], ps_t[:, S + P:2 * S]).then_inc(prT_ready, 1)

            def take_zT(g, s):
                act.wait_ge(z_done, g + 1)
                if late(g, 2):
                    act.wait_ge(backed, g - 1)
                nc.scalar.copy(zT[:, s % 2, :], ps_z[:, 0:S]).then_inc(zT_ready, 1)

            def take_zgT(g, k):
                act.wait_ge(zg_ps, K * g + k + 1)
                if late(g, 1) or k >= 2:
                    act.wait_ge(out_ps, K * g + k - 1)
                nc.scalar.copy(zgT[:, k % 2].rearrange("p e s -> p (e s)"), ps_g[:]).then_inc(zgT_ready, 1)

            def slot(b, s):
                now, one, two, five = (lagged(b, s, d, STEPS) for d in (0, 1, 2, 5))
                if now:
                    if s == 0:
                        take_gates(b)
                    take_qk(now[0], s)
                for k in range(K):
                    if one and k % 2 == 0:
                        exponentials(one[0], one[1], k // 2)
                    if two and k % 2:
                        take_prT(two[0], two[1], k // 2)
                    if five:
                        take_zgT(five[0], k)
                if s == STEPS - 1 and (not isinstance(b, int) or b + 1 < B):
                    take_xT(b + 1)
                if at := lagged(b, s, 3, STEPS):
                    take_zT(at[0], at[1])

            take_xT(0)
            run_steps(act, STEPS, slot, LAST)


def layouts(v):
    import numpy as np

    def pairs_hda(*ws):
        return np.stack([w.reshape(-1, 2, DC, P, 64).transpose(3, 0, 2, 1, 4).reshape(P, -1, DC, P) for w in ws], 2)

    def pairs_ed(*ws):
        return np.stack([w.reshape(-1, P, DC, P).transpose(3, 0, 2, 1) for w in ws], 2)

    def rows(w):
        return w.reshape(-1, P, w.shape[-1]).transpose(1, 0, 2)

    x = v["x"].reshape(TILES, P, D).transpose(1, 0, 2)
    ctx = v["ctx_1024"].reshape(B, S, DC, P).transpose(3, 0, 2, 1)
    mask = v["fside_Bx1xSxS2_0"].reshape(B, ST, P, S).transpose(2, 0, 1, 3)
    out = {
        "x": x, "ctxT": ctx, "mask": mask,
        "a0_w": pairs_hda(v["L0_attn_Wq"], v["L0_attn_Wk"], v["L0_attn_Wv"]),
        "a0_wo": rows(v["L0_attn_Wo"].reshape(-1, D)),
        "a0_bq": v["L0_attn_bq"].reshape(-1, P).T, "a0_bk": v["L0_attn_bk"].reshape(-1, P).T,
        "a0_bv": v["L0_attn_bv"].reshape(-1, P).T, "a0_bo": v["L0_attn_bo"],
        "c0_w": pairs_ed(v["L0_xattn_Wq"], v["L0_xattn_Wk"], v["L0_xattn_Wv"]),
        "c0_wo": rows(v["L0_xattn_Wo"].T),
        "l1_qk": v["L1_attn_w_qkv"][:2 * D].reshape(2, 2, P, DC, P).transpose(4, 1, 0, 3, 2),
        "l1_v": rows(v["L1_attn_w_qkv"][2 * D:].T),
        "l1_out": rows(v["L1_attn_w_out"].T),
        "c1_qk": np.stack([v["L1_xattn_Wq"], v["L1_xattn_Wk"]]).reshape(2, 2, P, DC, P).transpose(4, 1, 0, 3, 2),
        "c1_v": rows(v["L1_xattn_Wv"].T),
        "c1_bq": v["L1_xattn_bq"].reshape(2, P).T, "c1_bk": v["L1_xattn_bk"].reshape(2, P).T,
        "c1_bv": v["L1_xattn_bv"],
        "f1_qk": np.stack([v["L1_ffn_w_q"], v["L1_ffn_w_k"]]).reshape(2, DC, P, 4, P).transpose(2, 3, 0, 1, 4),
        "f1_gate": rows(v["L1_ffn_w_gate"]),
        "f1_val": v["L1_ffn_value_experts"].reshape(8, 8, DC, P, 64).transpose(3, 1, 2, 0, 4).reshape(P, 8, DC, 512),
        "f1_out": v["L1_ffn_output_experts"].reshape(4, 2, 8, 64, D).transpose(1, 3, 2, 0, 4).reshape(P, 8, 4, D),
        "f0_w1": v["L0_ffn_w1"].reshape(8, 4, P, DC, P).transpose(4, 0, 1, 3, 2),
        "f0_w2": v["L0_ffn_w2"].reshape(8, D, 4, P).transpose(3, 0, 2, 1),
        "f0_gate": rows(v["L0_ffn_gate_w"].T),
        "f0_b1": v["L0_ffn_b1"].reshape(-1, P).T,
        "f0_b2": np.pad(v["L0_ffn_b2"], ((0, P - 8), (0, 0))),
        "f0_norm": v["L0_ffn_norm_weight"].reshape(DC, P).T,
    }
    return {k: np.ascontiguousarray(a) for k, a in out.items()}


def program(nc, dram, out, phases=6):
    c = Core()
    c.dram = dram
    c.spent = []
    c.out = out
    with ExitStack() as ctx:
        sb = lambda name, shape: ctx.enter_context(nc.sbuf_tensor(name, shape, F32))
        sem = lambda name: ctx.enter_context(nc.semaphore(name))
        c.x = sb("x_sb", [P, TILES, D])
        c.mv = sb("mean_var", [P, TILES, 2])
        c.bn = sb("bn", [P, ST, 6])
        c.mv2 = sb("mv2", [P, ST, 2])
        c.begun = sem("begun")
        c.waited = sem("waited")
        c.pool_waited = sem("pool_waited")
        c.eps = sb("eps", [P, 1])
        c.ident = sb("ident", [P, P])
        c.causal = sb("causal", [P, 2 * P])
        c.causal_min = sb("causal_min", [P, 2 * P])
        c.keep = sb("keep", [P, 3 * P])
        c.half = sb("half", [P, 2])
        c.half1 = sb("half1", [P, 2])
        c.head16 = sb("head16", [P, 8])
        c.head16k = sb("head16k", [P, 8])
        arena_a = sb("arena_a", [P, 73 * 256])
        arena_b = sb("arena_b", [P, 40 * 256])

        def carve(arena, at, shape):
            n = 1
            for k in shape:
                n *= k
            v = arena[:, at:at + n]
            names = " ".join("abcde"[:len(shape)])
            return v.rearrange(f"p ({names}) -> p {names}", **dict(zip("abcde", shape))), at + n

        c.x_in = [sem(f"x_in{q}") for q in range(4)]
        loads = {}

        def load(eng, tag, dst, src):
            eng.dma_start(dst, src).then_inc(loads[tag][0], 16)
            loads[tag][1] += 16

        for tag in ("a0", "c0", "f0", "l1", "c1", "f1"):
            loads[tag] = [sem(f"w_{tag}"), 0]

        c.wait_weights = lambda eng, tag: eng.wait_ge(loads[tag][0], loads[tag][1])
        c.wait_small = c.wait_weights

        a0_w, o = carve(arena_a, 0, [8, 3, DC, P])
        a0_wo, o = carve(arena_a, o, [8, D])
        c0_w, o = carve(arena_b, 0, [8, 3, DC, P])
        c0_wo, o = carve(arena_b, o, [8, D])
        a0_bq, a0_bk = sb("a0_bq", [P, 8]), sb("a0_bk", [P, 8])
        a0_bv, a0_bo = sb("a0_bv", [P, 8]), sb("a0_bo", [P, D])

        with nc.Block() as block:
            @block.scalar
            def _(act):
                load(act, "a0", a0_w, dram["a0_w"])
                load(act, "a0", a0_wo, dram["a0_wo"])
                load(act, "a0", a0_bq[:], dram["a0_bq"])
                load(act, "a0", a0_bk[:], dram["a0_bk"])
                load(act, "a0", a0_bv[:], dram["a0_bv"])
                load(act, "a0", a0_bo[:], dram["a0_bo"].partition_broadcast(P))
        constants(nc, c)

        def load_c0(sp):
            load(sp, "c0", c0_w, dram["c0_w"])
            load(sp, "c0", c0_wo, dram["c0_wo"])

        f0_w1, o = carve(arena_a, 0, [8, 4, DC, P])
        f0_w2, o = carve(arena_a, o, [8, 4, D])
        f0_gate, o = carve(arena_a, o, [DC, 8])
        f0_b1, o = carve(arena_a, o, [1, 32])
        f0_norm, o = carve(arena_a, o, [1, DC])
        f0_b2, o = carve(arena_a, o, [1, D])

        def load_f0(sp):
            load(sp, "f0", f0_w1, dram["f0_w1"])
            load(sp, "f0", f0_w2, dram["f0_w2"])
            load(sp, "f0", f0_gate, dram["f0_gate"])
            load(sp, "f0", f0_b1[:, 0, :], dram["f0_b1"])
            load(sp, "f0", f0_norm[:, 0, :], dram["f0_norm"])
            load(sp, "f0", f0_b2[:, 0, :], dram["f0_b2"])

        l1_qk, o = carve(arena_b, 32 * 256, [2, 2, DC, P])
        l1_v, o = carve(arena_b, o, [DC, D])
        l1_out, o = carve(arena_b, o, [DC, D])
        c1_qk, o = carve(arena_b, 0, [2, 2, DC, P])
        c1_v, o = carve(arena_b, o, [DC, D])
        c1_bv, o = carve(arena_b, o, [1, D])
        c1_bq, o = carve(arena_b, o, [1, 2])
        c1_bk, o = carve(arena_b, o, [1, 2])

        def load_l1_c1(sp):
            load(sp, "l1", l1_qk, dram["l1_qk"])
            load(sp, "l1", l1_v, dram["l1_v"])
            load(sp, "l1", l1_out, dram["l1_out"])
            load(sp, "c1", c1_qk, dram["c1_qk"])
            load(sp, "c1", c1_v, dram["c1_v"])
            load(sp, "c1", c1_bv[:, 0, :], dram["c1_bv"].partition_broadcast(P))
            load(sp, "c1", c1_bq[:, 0, :], dram["c1_bq"])
            load(sp, "c1", c1_bk[:, 0, :], dram["c1_bk"])

        f1_qk, o = carve(arena_a, 0, [4, 2, DC, P])
        f1_gate, o = carve(arena_a, o, [DC, 64])
        f1_val, o = carve(arena_a, o, [8, DC, 512])
        f1_out, o = carve(arena_a, o, [8, 4, D])

        def load_f1(sp):
            load(sp, "f1", f1_qk, dram["f1_qk"])
            load(sp, "f1", f1_gate, dram["f1_gate"])
            load(sp, "f1", f1_val, dram["f1_val"])
            load(sp, "f1", f1_out, dram["f1_out"])

        def load_none(sp):
            pass

        attention(nc, c, "a0", a0_w, a0_wo, load_c0, causal=True,
                  bias={"q": a0_bq, "k": a0_bk, "v": a0_bv}, bo=a0_bo)
        if phases > 1:
            attention(nc, c, "c0", c0_w, c0_wo, load_f0, cross=True)
        if phases > 2:
            experts(nc, c, "f0", f0_w1, f0_w2, f0_gate, f0_b1[:, 0, :], f0_b2[:, 0, :], f0_norm[:, 0, :], load_l1_c1)
        if phases > 3:
            small_heads(nc, c, "l1", l1_qk, l1_v, load_f1, softmax=False, w_out=l1_out)
        if phases > 4:
            small_heads(nc, c, "c1", c1_qk, c1_v, load_none, softmax=True, bq=c1_bq[:, 0, :], bk=c1_bk[:, 0, :],
                        bv=c1_bv[:, 0, :])

        if phases > 5:
            gated_heads(nc, c, "f1", f1_qk, f1_gate, f1_val, f1_out, load_none)
        else:
            with nc.semaphore("stored") as stored, nc.Block() as block:
                @block.sync
                def _(sp):
                    sp.dma_start(out, c.x[:]).then_inc(stored, 16)
                    sp.wait_ge(stored, 16)


PHASES = 6


def kernel(**inputs):
    import numpy as np
    import concourse.bacc as bacc
    from concourse.bass_utils import run_bass_kernel_spmd

    nc = bacc.Bacc("TRN2", target_bir_lowering=False, num_devices=1)
    arrays, dram = {}, {}
    for name, a in layouts({k: np.asarray(v) for k, v in inputs.items()}).items():
        arrays[f"in_{name}"] = a
        dram[name] = nc.dram_tensor(f"in_{name}", a.shape, mybir.dt.from_np(a.dtype), kind="ExternalInput").ap()
    out = nc.dram_tensor("out_x", (P, TILES, D), F32, kind="ExternalOutput").ap()
    program(nc, dram, out, PHASES)
    r = run_bass_kernel_spmd(nc, [arrays], core_ids=[0])
    return r.results[0]["out_x"].transpose(1, 0, 2).reshape(B, S, D)
```

```python
from contextlib import ExitStack

import concourse.bass as bass
from concourse import mybir

ALU = mybir.AluOpType
ACT = mybir.ActivationFunctionType
F32 = mybir.dt.float32
F32R = mybir.dt.float32r
X = mybir.AxisListType.X

P = 128
D = 256
DC = D // P
S = 256
ST = S // P
B = 16
TILES = B * ST
LN_EPS = 1e-5
NEG_L0 = -100000.0
NEG_MIN = -1.0e30


def late(g, n):
    return not isinstance(g, int) or g >= n


class Core:
    pass


def run_steps(eng, steps, stages, last_lag):
    def batch(b):
        for s in range(steps):
            stages(b, s)
    lead = -(-last_lag // steps)
    for b in range(lead):
        batch(b)
    with eng.Fori(lead, B - 1) as b:
        batch(b)
    batch(B - 1)
    for s in range(last_lag):
        stages(B, s)


def lagged(b, s, d, steps):
    back = s - d
    at = back % steps
    over = (at - back) // steps
    if isinstance(b, int):
        n = b * steps + back
        if n < 0 or n >= B * steps:
            return None
        return n, at, b - over
    return b * steps + back, at, (b - over if over else b)



PIECE = 1024


class Pieces:
    STAGES = 2

    def __init__(self, nc, ctx, tag, stage, list):
        self.stage, self.list = stage, list
        self.moved = [ctx.enter_context(nc.semaphore(f"{tag}_moved{n}")) for n in range(self.STAGES)]
        self.rounded = ctx.enter_context(nc.semaphore(f"{tag}_rounded"))
        self.split = ctx.enter_context(nc.semaphore(f"{tag}_split"))

    def load(self, eng, first, last):
        for n in range(first, min(last, len(self.list))):
            src = self.list[n][2]
            if n >= self.STAGES:
                eng.wait_ge(self.split, n - self.STAGES + 1)
            eng.dma_start(self.stage[:, n % self.STAGES, 0:src.shape[1]], src).then_inc(self.moved[n % self.STAGES], 16)

    def load_rest(self, eng):
        self.load(eng, self.STAGES, len(self.list))
        eng.wait_ge(self.split, len(self.list))

    def round(self, nc, act, first, last):
        for n in range(first, min(last, len(self.list))):
            high, _, src = self.list[n]
            act.wait_ge(self.moved[n % self.STAGES], 16 * (n // self.STAGES + 1))
            nc.scalar.copy(high, self.stage[:, n % self.STAGES, 0:src.shape[1]]).then_inc(self.rounded, 1)

    def rest(self, nc, dve, first, last):
        for n in range(first, min(last, len(self.list))):
            high, low, src = self.list[n]
            dve.wait_ge(self.rounded, n + 1)
            nc.vector.tensor_tensor(low, self.stage[:, n % self.STAGES, 0:src.shape[1]], high.bitcast(F32),
                                    ALU.subtract).then_inc(self.split, 1)


def product3(nc, out, stationary, moving, start, stop, **kw):
    (sh, sl), (mh, ml) = stationary, moving
    nc.tensor.matmul(out, sh, mh, start=start, stop=False, **kw)
    nc.tensor.matmul(out, sh, ml, start=False, stop=False, **kw)
    return nc.tensor.matmul(out, sl, mh, start=False, stop=stop, **kw)


def constants(nc, c):
    with nc.semaphore("s_zero") as filled, nc.semaphore("s_const") as const_ready, \
            nc.semaphore("s_stats") as stats, nc.Block() as block:
        c.spent += [filled, const_ready, stats]

        @block.gpsimd
        def _(pool):
            nc.gpsimd.memset(c.ident[:], 0.0).then_inc(filled, 1)
            nc.gpsimd.memset(c.causal[:], 0.0).then_inc(filled, 1)
            nc.gpsimd.memset(c.causal_min[:], 0.0).then_inc(filled, 1)
            nc.gpsimd.memset(c.keep[:], 1.0).then_inc(filled, 1)
            nc.gpsimd.memset(c.half[:], 64 ** -0.5).then_inc(filled, 1)
            nc.gpsimd.memset(c.half1[:], 1.0).then_inc(filled, 1)
            nc.gpsimd.memset(c.head16[:], 0.25).then_inc(filled, 1)
            nc.gpsimd.memset(c.head16k[:], 1.0).then_inc(filled, 1)
            pool.wait_ge(filled, 8)
            nc.gpsimd.affine_select(out=c.ident[:], in_=c.ident[:], compare_op=ALU.not_equal, fill=1.0,
                                    base=0, pattern=[[-1, P]], channel_multiplier=1).then_inc(const_ready, 1)
            for mask, fill in ((c.causal, NEG_L0), (c.causal_min, NEG_MIN)):
                nc.gpsimd.affine_select(out=mask[:, P:], in_=mask[:, P:], compare_op=ALU.is_ge, fill=fill,
                                        base=0, pattern=[[-1, P]], channel_multiplier=1).then_inc(const_ready, 1)
            for blk in (0, 2):
                nc.gpsimd.affine_select(out=c.keep[:, blk * P:(blk + 1) * P], in_=c.keep[:, blk * P:(blk + 1) * P],
                                        compare_op=ALU.is_ge, fill=0.0, base=0, pattern=[[1, P]],
                                        channel_multiplier=-1).then_inc(const_ready, 1)
            ready = 5
            for mask, width in ((c.half, 64), (c.half1, 64), (c.head16, 16), (c.head16k, 16)):
                n = P // width
                nc.gpsimd.affine_select(out=mask[:], in_=mask[:], compare_op=ALU.is_ge, fill=0.0, base=0,
                                        pattern=[[-width, n]], channel_multiplier=1).then_inc(const_ready, 1)
                ready += 1
                pool.wait_ge(const_ready, ready)
                nc.gpsimd.affine_select(out=mask[:], in_=mask[:], compare_op=ALU.is_ge, fill=0.0, base=width - 1,
                                        pattern=[[width, n]], channel_multiplier=-1).then_inc(const_ready, 1)
                ready += 1

        @block.sync
        def _(sp):
            for q in range(4):
                t = TILES // 4
                sp.dma_start(c.x[:, q * t:(q + 1) * t, :], c.dram["x"][:, q * t:(q + 1) * t, :]).then_inc(c.x_in[q], 16)

        @block.vector
        def _(dve):
            nc.vector.memset(c.eps[:], LN_EPS).then_inc(c.begun, 1)
            for b in range(B):
                if b % (B // 4) == 0:
                    dve.wait_ge(c.x_in[b // (B // 4)], 16)
                batch_stats(nc, dve, c, stats, b)


def batch_stats(nc, dve, c, stats, b):
    if late(b, 1):
        dve.wait_ge(stats, 3 * b)
    dve.sem_inc(c.waited, 1)
    for i in range(ST):
        last = nc.vector.bn_stats(c.bn[:, i, :], c.x[:, bass.ds(b * ST + i, 1), :].rearrange("p a d -> p (a d)"))
    last.then_inc(stats, 1)
    dve.wait_ge(stats, 3 * b + 1)
    dve.sem_inc(c.waited, 1)
    for i in range(ST):
        last = nc.vector.bn_aggr(c.mv2[:, i, :], c.bn[:, i, :])
    last.then_inc(stats, 1)
    dve.wait_ge(stats, 3 * b + 2)
    nc.vector.tensor_scalar(c.mv[:, bass.ds(b * ST, ST), :].rearrange("p a d -> p (a d)"),
                            c.mv2[:].rearrange("p a d -> p (a d)"), 1.0, None, ALU.mult).then_inc(stats, 1)


def attention(nc, c, tag, pieces, w, load_next, cross=False, causal=False, bias=None, bo=None):
    PAIRS = 8
    LAST = 5
    AHEAD = 3
    with ExitStack() as ctx:
        sb = lambda name, shape, dt=F32: ctx.enter_context(nc.sbuf_tensor(f"{tag}_{name}", shape, dt))
        ps = lambda name: ctx.enter_context(nc.psum_tensor(f"{tag}_{name}", [P, 512], F32))

        def sem(name):
            c.spent.append(ctx.enter_context(nc.semaphore(f"{tag}_{name}")))
            return c.spent[-1]


        rstd = sb("rstd", [P, TILES])
        xn = sb("xn", [P, ST, D])
        xnT = [sb(f"xnT{n}", [P, DC, S], F32R) for n in range(2)]
        if cross:
            ctx_stage = sb("ctx_stage", [P, DC, S])
            ctxT = [sb(f"ctxT{n}", [P, DC, S], F32R) for n in range(2)]
            mask_stage = sb("mask_stage", [P, ST, S])
            mask = sb("mask", [P, ST, S])
        qT = sb("qT", [P, 2, 2, S])
        kT = sb("kT", [P, 2, S])
        v = sb("v", [P, PAIRS, ST, P])
        sm = sb("sm", [P, 2, ST, S])
        pr = sb("pr", [P, 8, ST, S])
        prT = sb("prT", [P, 4, ST, S])
        zT = [sb(f"zT{n}", [P, 2, S], F32R) for n in range(2)]
        nmx = sb("nmx", [P, 2, ST])
        sums = sb("sums", [P, 8, ST])
        inv = sb("inv", [P, 8, ST])

        ps_q, ps_kv, ps_z, ps_out = ps("ps_q"), ps("ps_kv"), ps("ps_z"), ps("ps_out")
        ps_s = [ps("ps_s0"), ps("ps_s1")]
        ps_t = [ps("ps_t0"), ps("ps_t1")]

        rstd_s = sem("rstd")
        xn_ready = sem("xn_ready")
        xnT_ps = sem("xnT_ps")
        xnT_round = sem("xnT_round")
        xnT_ready = sem("xnT_ready")
        ctx_in = sem("ctx_in")
        ctx_round = sem("ctx_round")
        ctx_ready = sem("ctx_ready")
        mask_in = sem("mask_in")
        mask_ready = sem("mask_ready")
        proj = sem("proj")
        q_ready = sem("q_ready")
        k_ready = sem("k_ready")
        v_ready = sem("v_ready")
        scored = sem("scored")
        maxed = sem("maxed")
        exped = sem("exped")
        inverted = sem("inverted")
        normed = sem("normed")
        turned = sem("turned")
        prT_ready = sem("prT_ready")
        z_done = sem("z_done")
        zT_round = sem("zT_round")
        zT_ready = sem("zT_ready")
        projected = sem("projected")
        out_read = sem("out_read")
        biased = sem("biased")
        stats = sem("stats")

        block = ctx.enter_context(nc.Block())

        def steps(eng, slot):
            run_steps(eng, PAIRS, slot, LAST)

        @block.sync
        def _(sp):
            def context(b):
                if late(b, 1):
                    sp.wait_ge(ctx_ready, b)
                    sp.wait_ge(mask_ready, b)
                sp.dma_start(ctx_stage[:], c.dram["ctxT"][:, bass.ds(b, 1), :, :].rearrange("p a c s -> p (a c) s")).then_inc(ctx_in, 16)
                sp.dma_start(mask_stage[:], c.dram["mask"][:, bass.ds(b, 1), :, :].rearrange("p a c s -> p (a c) s")).then_inc(mask_in, 16)
            if cross:
                context(0)
            pieces.load_rest(sp)
            load_next(sp)
            if cross:
                with sp.Fori(1, B) as b:
                    context(b)

        @block.tensor
        def _(pe):
            part = lambda s, n: [t[:, s, n * D:(n + 1) * D] for t in w]

            def turn_x(b):
                pe.wait_ge(xn_ready, b + 1)
                if late(b, 1):
                    pe.wait_ge(q_ready, PAIRS * b)
                for dc in range(DC):
                    for i in range(ST):
                        last = nc.tensor.transpose(ps_q[:, dc * S + i * P:dc * S + (i + 1) * P],
                                                   xn[:, i, dc * P:(dc + 1) * P], c.ident[:])
                last.then_inc(xnT_ps, 1)

            def project(g, s, b):
                if s == 0:
                    pe.wait_ge(xnT_ready, b + 1)
                if late(g, 1):
                    pe.wait_ge(q_ready, g)
                if not late(b, 1):
                    pe.wait_ge(pieces.split, s + 2 - s % 2)
                cols = lambda n, dc: [t[:, dc * P:(dc + 1) * P] for t in part(s, n)]
                for dc in range(DC):
                    last = product3(nc, ps_q[:, 0:S], cols(0, dc), [t[:, dc, :] for t in xnT], dc == 0, dc == DC - 1)
                last.then_inc(proj, 1)
                if s == 0 and cross:
                    pe.wait_ge(ctx_ready, b + 1)
                src = ctxT if cross else xnT
                if late(g, 1):
                    pe.wait_ge(v_ready, g)
                for dc in range(DC):
                    product3(nc, ps_kv[:, 0:S], cols(1, dc), [t[:, dc, :] for t in src], dc == 0, dc == DC - 1)
                i = s % 2
                for dc in range(DC):
                    last = product3(nc, ps_kv[:, S:2 * S], [t[:, dc, i * P:(i + 1) * P] for t in src],
                                    part(s - i + dc, 2), dc == 0, dc == DC - 1)
                last.then_inc(proj, 1)

            def scores(g, s):
                pe.wait_ge(q_ready, g + 1)
                pe.wait_ge(k_ready, g + 1)
                for j in range(2):
                    if late(g, 1):
                        pe.wait_ge(maxed, 2 * g + j - 1)
                    for i in range(ST):
                        n = (i + 1) * P if causal else S
                        last = nc.tensor.matmul(ps_s[j][:, i * S:i * S + n], qT[:, s % 2, j, i * P:(i + 1) * P],
                                                kT[:, s % 2, 0:n], start=True, stop=True)
                    last.then_inc(scored, 1)

            def turn(g, s):
                for j in range(2):
                    pe.wait_ge(normed, 2 * g + j + 1)
                    if late(g, 1):
                        pe.wait_ge(prT_ready, 2 * g + j - 1)
                    for i in range(ST):
                        for t in range(i + 1 if causal else ST):
                            last = nc.tensor.transpose(ps_t[j][:, t * S + i * P:t * S + (i + 1) * P],
                                                       pr[:, 2 * (s % 4) + j, i, t * P:(t + 1) * P], c.ident[:])
                    last.then_inc(turned, 1)

            def values(g, s):
                pe.wait_ge(v_ready, g + 2 - s % 2)
                pe.wait_ge(prT_ready, 2 * g + 2)
                if late(g, 1):
                    pe.wait_ge(zT_ready, g)
                z0 = (s % 2) * S
                for t in range(ST):
                    q0 = t * P if causal else 0
                    for j in range(2):
                        last = nc.tensor.matmul(ps_z[64 * j:64 * j + 64, z0 + q0:z0 + S],
                                                v[:, s, t, 64 * j:64 * j + 64],
                                                prT[:, 2 * (s % 2) + j, t, q0:S], start=(t == 0), stop=(t == ST - 1))
                last.then_inc(z_done, 1)

            def output(g, s, b):
                pe.wait_ge(zT_ready, g + 1)
                if s == 0 and late(g, PAIRS):
                    pe.wait_ge(out_read, b)
                for i in range(ST):
                    last = product3(nc, ps_out[:, i * D:(i + 1) * D], [t[:, s % 2, i * P:(i + 1) * P] for t in zT],
                                    part(s, 3), s == 0 and i == 0, s == PAIRS - 1, skip_group_check=True)
                last.then_inc(projected, 1)

            def slot(b, s):
                if at := lagged(b, s, 0, PAIRS):
                    project(*at)
                if s == PAIRS - 1 and (not isinstance(b, int) or b + 1 < B):
                    turn_x(b + 1)
                if at := lagged(b, s, 1, PAIRS):
                    scores(at[0], at[1])
                if at := lagged(b, s, 3, PAIRS):
                    turn(at[0], at[1])
                if at := lagged(b, s, 4, PAIRS):
                    values(at[0], at[1])
                if at := lagged(b, s, 5, PAIRS):
                    output(*at)

            turn_x(0)
            steps(pe, slot)

        @block.vector
        def _(dve):
            dve.wait_ge(rstd_s, 1)
            nc.vector.reciprocal(rstd[:], rstd[:]).then_inc(rstd_s, 1)
            dve.wait_ge(rstd_s, 2)

            def normalise(b):
                if late(b, 1):
                    dve.wait_ge(xnT_ps, b)
                for i in range(ST):
                    n = b * ST + i
                    last = nc.vector.tensor_scalar(xn[:, i, :], c.x[:, bass.ds(n, 1), :].rearrange("p a d -> p (a d)"),
                                                   c.mv[:, bass.ds(n, 1), 0:1].rearrange("p a d -> p (a d)"),
                                                   rstd[:, bass.ds(n, 1)], ALU.subtract, ALU.mult)
                last.then_inc(xn_ready, 1)

            def take_mask(b):
                dve.wait_ge(mask_in, 16 * b + 16)
                nc.vector.tensor_copy(mask[:], mask_stage[:]).then_inc(mask_ready, 1)
                dve.wait_ge(mask_ready, b + 1)

            def take_q(g, s):
                dve.wait_ge(proj, 2 * g + 1)
                if late(g, 2):
                    dve.wait_ge(scored, 2 * g - 2)
                for j in range(2):
                    if bias is not None:
                        last = nc.vector.tensor_scalar(qT[:, s % 2, j, :], ps_q[:, 0:S], bias["q"][:, s:s + 1],
                                                       c.half[:, j:j + 1], ALU.add, ALU.mult)
                    else:
                        last = nc.vector.tensor_scalar(qT[:, s % 2, j, :], ps_q[:, 0:S], c.half1[:, j:j + 1],
                                                       None, ALU.mult)
                last.then_inc(q_ready, 1)

            def row_max(g, s, j):
                dve.wait_ge(scored, 2 * g + j + 1)
                if late(g, 1):
                    dve.wait_ge(exped, 2 * g + j - 1)
                dve.sem_inc(c.waited, 1)
                for i in range(ST):
                    n = (i + 1) * P if causal else S
                    add = c.causal[:, (ST - 1 - i) * P:(ST - 1 - i) * P + n] if causal else mask[:, i, :]
                    last = nc.vector.tensor_tensor_reduce(sm[:, j, i, 0:n], ps_s[j][:, i * S:i * S + n], add, -1.0,
                                                          3.0e38, ALU.add, ALU.min, nmx[:, j, i:i + 1])
                last.then_inc(maxed, 1)

            def invert(g, s):
                dve.wait_ge(exped, 2 * g + 2)
                r = 2 * (s % 4)
                nc.vector.reciprocal(inv[:, r:r + 2, :], sums[:, r:r + 2, :]).then_inc(inverted, 1)

            def norm(g, s):
                dve.wait_ge(inverted, g + 1)
                for j in range(2):
                    r = 2 * (s % 4) + j
                    for i in range(ST):
                        n = (i + 1) * P if causal else S
                        last = nc.vector.tensor_scalar(pr[:, r, i, 0:n], pr[:, r, i, 0:n], inv[:, r, i:i + 1], None, ALU.mult)
                    last.then_inc(normed, 1)

            def rest_z(g, s):
                dve.wait_ge(zT_round, g + 1)
                z = ps_z[:, (s % 2) * S:(s % 2 + 1) * S]
                high = zT[0][:, s % 2, :].bitcast(F32)
                if bias is not None:
                    nc.vector.scalar_tensor_tensor(zT[1][:, s % 2, :], z, bias["v"][:, s:s + 1], high,
                                                   ALU.add, ALU.subtract).then_inc(zT_ready, 1)
                else:
                    nc.vector.tensor_tensor(zT[1][:, s % 2, :], z, high, ALU.subtract).then_inc(zT_ready, 1)

            def rest_inputs(b):
                flat = lambda t: t[:].rearrange("p c s -> p (c s)")
                dve.wait_ge(xnT_round, b + 1)
                nc.vector.tensor_tensor(flat(xnT[1]), ps_q[:], flat(xnT[0]).bitcast(F32), ALU.subtract).then_inc(xnT_ready, 1)
                if cross:
                    dve.wait_ge(ctx_round, b + 1)
                    nc.vector.tensor_tensor(flat(ctxT[1]), flat(ctx_stage), flat(ctxT[0]).bitcast(F32),
                                            ALU.subtract).then_inc(ctx_ready, 1)

            def add_to_x(b):
                dve.wait_ge(projected, PAIRS * b + PAIRS)
                xb = c.x[:, bass.ds(b * ST, ST), :].rearrange("p a d -> p (a d)")
                nc.vector.tensor_tensor(xb, xb, ps_out[:], ALU.add).then_inc(out_read, 1)

            def add_bias(b):
                dve.wait_ge(out_read, b + 1)
                for i in range(ST):
                    xt = c.x[:, bass.ds(b * ST + i, 1), :].rearrange("p a d -> p (a d)")
                    last = nc.vector.tensor_tensor(xt, xt, bo[:], ALU.add)
                last.then_inc(biased, 1)

            def new_stats(b):
                if bo is not None:
                    dve.wait_ge(biased, b + 1)
                else:
                    dve.wait_ge(out_read, b + 1)
                batch_stats(nc, dve, c, stats, b)

            def slot(b, s):
                if at := lagged(b, s, 5, PAIRS):
                    rest_z(at[0], at[1])
                if at := lagged(b, s, 0, PAIRS):
                    if not late(b, 1):
                        pieces.rest(nc, dve, s + AHEAD, s + AHEAD + 1)
                    take_q(at[0], at[1])
                if s == PAIRS - 1 and (not isinstance(b, int) or b + 1 < B):
                    rest_inputs(b + 1)
                if at := lagged(b, s, 1, PAIRS):
                    if at[1] == 0 and cross:
                        take_mask(at[2])
                    row_max(at[0], at[1], 0)
                    row_max(at[0], at[1], 1)
                if at := lagged(b, s, 2, PAIRS):
                    invert(at[0], at[1])
                    norm(at[0], at[1])
                if s == 2 and (not isinstance(b, int) or b + 1 < B):
                    normalise(b + 1)
                after = b - 1
                if late(b, 1) and s == 4:
                    add_to_x(after)
                if late(b, 1) and s == 5 and bo is not None:
                    add_bias(after)
                if late(b, 1) and s == 6:
                    new_stats(after)

            normalise(0)
            rest_inputs(0)
            pieces.rest(nc, dve, 0, AHEAD)
            steps(dve, slot)
            if bo is not None:
                add_bias(B - 1)
            new_stats(B - 1)

        @block.scalar
        def _(act):
            nc.scalar.activation(rstd[:], c.mv[:, :, 1:2].rearrange("p a d -> p (a d)"), ACT.Sqrt,
                                 bias=c.eps[:]).then_inc(rstd_s, 1)
            if bias is not None:
                c.wait_weights(act, tag)

            def take_xT(b):
                act.wait_ge(xnT_ps, b + 1)
                nc.scalar.copy(xnT[0][:].rearrange("p c s -> p (c s)"), ps_q[:]).then_inc(xnT_round, 1)
                if cross:
                    act.wait_ge(ctx_in, 16 * b + 16)
                    if late(b, 1):
                        act.wait_ge(proj, 2 * PAIRS * b)
                    nc.scalar.copy(ctxT[0][:], ctx_stage[:]).then_inc(ctx_round, 1)

            def take_kv(g, s):
                act.wait_ge(proj, 2 * g + 2)
                if late(g, 2):
                    act.wait_ge(scored, 2 * g - 2)
                if bias is not None:
                    nc.scalar.activation(kT[:, s % 2, :], ps_kv[:, 0:S], ACT.Identity,
                                         bias=bias["k"][:, s:s + 1]).then_inc(k_ready, 1)
                else:
                    nc.scalar.copy(kT[:, s % 2, :], ps_kv[:, 0:S]).then_inc(k_ready, 1)
                if late(g, PAIRS):
                    act.wait_ge(z_done, g + 2 - s % 2 - PAIRS)
                nc.scalar.copy(v[:, s - s % 2:s - s % 2 + 2, s % 2, :],
                               ps_kv[:, S:2 * S].rearrange("p (n m) -> p n m", n=2)).then_inc(v_ready, 1)

            def take_z(g, s):
                act.wait_ge(z_done, g + 1)
                if late(g, 2):
                    act.wait_ge(projected, g - 1)
                z = ps_z[:, (s % 2) * S:(s % 2 + 1) * S]
                if bias is not None:
                    nc.scalar.activation(zT[0][:, s % 2, :], z, ACT.Identity, bias=bias["v"][:, s:s + 1]).then_inc(zT_round, 1)
                else:
                    nc.scalar.copy(zT[0][:, s % 2, :], z).then_inc(zT_round, 1)

            def exponentials(g, s, j):
                r = 2 * (s % 4) + j
                act.wait_ge(maxed, 2 * g + j + 1)
                if late(g, 4):
                    act.wait_ge(turned, 2 * g + j - 7)
                for i in range(ST):
                    n = (i + 1) * P if causal else S
                    last = nc.scalar.activation(pr[:, r, i, 0:n], sm[:, j, i, 0:n], ACT.Exp, bias=nmx[:, j, i:i + 1], scale=-1.0,
                                                accum_out=sums[:, r, i:i + 1])
                last.then_inc(exped, 1)

            def take_prT(g, s, j):
                r = 2 * (s % 2) + j
                act.wait_ge(turned, 2 * g + j + 1)
                if late(g, 2):
                    act.wait_ge(z_done, g - 1)
                if causal:
                    nc.scalar.copy(prT[:, r, 0, :], ps_t[j][:, 0:S])
                    nc.scalar.copy(prT[:, r, 1, P:S], ps_t[j][:, S + P:2 * S]).then_inc(prT_ready, 1)
                else:
                    nc.scalar.copy(prT[:, r, :, :].rearrange("p t s -> p (t s)"), ps_t[j][:]).then_inc(prT_ready, 1)

            def slot(b, s):
                if at := lagged(b, s, 5, PAIRS):
                    take_z(at[0], at[1])
                if at := lagged(b, s, 0, PAIRS):
                    if not late(b, 1):
                        pieces.round(nc, act, s + AHEAD, s + AHEAD + 1)
                    take_kv(at[0], at[1])
                if s == PAIRS - 1 and (not isinstance(b, int) or b + 1 < B):
                    take_xT(b + 1)
                if at := lagged(b, s, 3, PAIRS):
                    take_prT(at[0], at[1], 0)
                    take_prT(at[0], at[1], 1)
                if at := lagged(b, s, 1, PAIRS):
                    exponentials(at[0], at[1], 0)
                    exponentials(at[0], at[1], 1)

            take_xT(0)
            pieces.round(nc, act, 0, AHEAD)
            steps(act, slot)


def experts(nc, c, tag, pieces, w1, w2, gate_w, load_next):
    E, FC, LAST = 8, 4, 1
    with ExitStack() as ctx:
        sb = lambda name, shape, dt=F32: ctx.enter_context(nc.sbuf_tensor(f"{tag}_{name}", shape, dt))
        ps = lambda name: ctx.enter_context(nc.psum_tensor(f"{tag}_{name}", [P, 512], F32))
        sem = lambda name: ctx.enter_context(nc.semaphore(f"{tag}_{name}"))
        rstd = sb("rstd", [P, TILES])
        ms = sb("ms", [P, TILES])
        rms_eps = sb("rms_eps", [P, 1])
        t = sb("t", [P, ST, D])
        tT = [sb(f"tT{n}", [P, DC, S], F32R) for n in range(2)]
        h = sb("h", [P, FC, S])
        hT = [sb(f"hT{n}", [P, 2, FC, S], F32R) for n in range(2)]
        b1 = sb("b1", [P, E * FC])
        b2 = sb("b2", [P, D])
        norm_w = sb("norm_w", [P, DC])
        rev = sb("rev", [P, ST, E])
        logits = sb("logits", [P, ST, E])
        eq = sb("eq", [P, ST, E])
        one = sb("one", [P, 2, ST, E])
        top = sb("top", [P, 2, ST])
        pick = sb("pick", [P, ST])
        diff = sb("diff", [P, ST])
        ex = sb("ex", [P, ST])
        wt = sb("wt", [P, 2, ST])
        part = sb("part", [P, 2, ST, E])
        mix = sb("mix", [P, ST, P])
        mixT = sb("mixT", [P, ST, P])
        ps_h = [ps(f"ps_h{n}") for n in range(FC)]
        ps_o = [ps("ps_o0"), ps("ps_o1")]
        ps_m, ps_c = ps("ps_m"), ps("ps_c")

        small_in = sem("small_in")
        root = sem("root")
        t_ready = sem("t_ready")
        tT_ps = sem("tT_ps")
        tT_round = sem("tT_round")
        tT_ready = sem("tT_ready")
        gated = sem("gated")
        pick_s = sem("pick_s")
        ex_ready = sem("ex_ready")
        mixT_ps = sem("mixT_ps")
        mixT_ready = sem("mixT_ready")
        b2_ps = sem("b2_ps")
        h_ps = sem("h_ps")
        h_act = sem("h_act")
        h_round = sem("h_round")
        h_ready = sem("h_ready")
        o_ps = sem("o_ps")
        y_s = sem("y_s")
        summed = sem("summed")
        stats = sem("stats")
        weighed = sem("weighed")
        SUMS = 2 + 2 * E
        PICKS = 14

        def late_batch(b):
            return not isinstance(b, int) or b < B

        def place(e):
            return 2 + 2 * e + (1 if e >= 3 else 0)

        block = ctx.enter_context(nc.Block())

        @block.sync
        def _(sp):
            sp.dma_start(norm_w[:], c.dram["f0_norm"]).then_inc(small_in, 16)
            sp.dma_start(b1[:], c.dram["f0_b1"]).then_inc(small_in, 16)
            sp.dma_start(b2[:], c.dram["f0_b2"]).then_inc(small_in, 16)
            pieces.load_rest(sp)
            load_next(sp)

        @block.gpsimd
        def _(pool):
            for spent in c.spent:
                pool.sem_clear(spent)
            nc.gpsimd.iota(rev[:], pattern=[[0, ST], [-1, E]], base=E, channel_multiplier=0,
                           allow_small_or_imprecise_dtypes=True).then_inc(root, 1)
            nc.gpsimd.memset(mix[:], 0.0).then_inc(root, 1)
            nc.gpsimd.memset(rms_eps[:], 1e-6).then_inc(root, 1)

        @block.tensor
        def _(pe):
            pe.wait_ge(small_in, 48)

            def turn_t(b):
                pe.wait_ge(t_ready, b + 1)
                if late(b, 1):
                    pe.wait_ge(summed, SUMS * (b - 1) + 8)
                for dc in range(DC):
                    for i in range(ST):
                        last = nc.tensor.transpose(ps_m[:, dc * S + i * P:dc * S + (i + 1) * P],
                                                   t[:, i, dc * P:(dc + 1) * P], c.ident[:])
                last.then_inc(tT_ps, 1)

            def gates(b):
                pe.wait_ge(tT_ready, b + 1)
                if not late(b, 1):
                    pe.wait_ge(pieces.split, 1)
                for i in range(ST):
                    for dc in range(DC):
                        last = product3(nc, ps_m[:, i * E:(i + 1) * E], [a[:, dc, i * P:(i + 1) * P] for a in tT],
                                        [a[:, dc, :] for a in gate_w], dc == 0, dc == DC - 1)
                last.then_inc(gated, 1)

            def turn_mix(b):
                pe.wait_ge(pick_s, PICKS * b + PICKS)
                if late(b, 1):
                    pe.wait_ge(mixT_ready, b)
                for i in range(ST):
                    last = nc.tensor.transpose(ps_c[:, i * P:(i + 1) * P], mix[:, i, :], c.ident[:])
                last.then_inc(mixT_ps, 1)

            def weighted_b2(b):
                pe.wait_ge(mixT_ready, b + 1)
                for i in range(ST):
                    last = nc.tensor.matmul(ps_m[:, i * D:(i + 1) * D], mixT[:, i, :], b2[:], start=True, stop=True)
                last.then_inc(b2_ps, 1)

            def first(g, s, b):
                if s == 0:
                    pe.wait_ge(tT_ready, b + 1)
                if not late(b, 1):
                    pe.wait_ge(pieces.split, 2 * s + 2)
                for f in range(FC):
                    if late(g, 1):
                        pe.wait_ge(h_act, FC * g + f - FC + 1)
                    for dc in range(DC):
                        last = product3(nc, ps_h[f][:, 0:S], [a[:, s, f, dc, :] for a in w1],
                                        [a[:, dc, :] for a in tT], dc == 0, dc == DC - 1)
                    last.then_inc(h_ps, 1)

            def second(g, s, b):
                pe.wait_ge(h_ready, FC * g + FC)
                if not late(b, 1):
                    pe.wait_ge(pieces.split, 2 * s + 3)
                for i in range(ST):
                    if late(g, 1):
                        pe.wait_ge(summed, SUMS * b + place(s - 1) + i if s else SUMS * (b - 1) + place(E - 1) + i)
                    for f in range(FC):
                        last = product3(nc, ps_o[i][:, 0:D], [a[:, s % 2, f, i * P:(i + 1) * P] for a in hT],
                                        [a[:, s, f, :] for a in w2], f == 0, f == FC - 1)
                    last.then_inc(o_ps, 1)

            def slot(b, s):
                if s == 0 and late_batch(b):
                    gates(b)
                if at := lagged(b, s, 0, E):
                    first(*at)
                if s == E - 1 and (not isinstance(b, int) or b + 1 < B):
                    turn_t(b + 1)
                if at := lagged(b, s, 1, E):
                    second(*at)
                if s == 2:
                    turn_mix(b)
                if s == 3:
                    weighted_b2(b)

            turn_t(0)
            run_steps(pe, E, slot, LAST)

        @block.vector
        def _(dve):
            dve.wait_ge(root, 4)
            nc.vector.reciprocal(rstd[:], rstd[:]).then_inc(root, 1)
            dve.wait_ge(root, 5)
            nc.vector.tensor_tensor(ms[:], rstd[:], rstd[:], ALU.mult).then_inc(root, 1)
            dve.wait_ge(root, 6)
            nc.vector.tensor_tensor(ms[:], ms[:], c.mv[:, :, 1:2].rearrange("p a d -> p (a d)"), ALU.mult).then_inc(root, 1)
            dve.wait_ge(root, 8)
            nc.vector.reciprocal(ms[:], ms[:]).then_inc(root, 1)
            dve.wait_ge(root, 9)
            nc.vector.tensor_tensor(ms[:], ms[:], rstd[:], ALU.mult).then_inc(root, 1)
            dve.wait_ge(root, 10)

            def normalise(b):
                if late(b, 1):
                        dve.wait_ge(summed, SUMS * (b - 1) + 1)
                for i in range(ST):
                    n = b * ST + i
                    last = nc.vector.tensor_scalar(t[:, i, :], c.x[:, bass.ds(n, 1), :].rearrange("p a d -> p (a d)"),
                                                   c.mv[:, bass.ds(n, 1), 0:1].rearrange("p a d -> p (a d)"),
                                                   ms[:, bass.ds(n, 1)], ALU.subtract, ALU.mult)
                last.then_inc(t_ready, 1)

            def add_y(b):
                dve.wait_ge(tT_ps, b + 1)
                for i in range(ST):
                    n = b * ST + i
                    last = nc.vector.tensor_scalar(t[:, i, :], c.x[:, bass.ds(n, 1), :].rearrange("p a d -> p (a d)"),
                                                   c.mv[:, bass.ds(n, 1), 0:1].rearrange("p a d -> p (a d)"),
                                                   rstd[:, bass.ds(n, 1)], ALU.subtract, ALU.mult)
                last.then_inc(y_s, 1)
                dve.wait_ge(y_s, b + 1)
                xb = c.x[:, bass.ds(b * ST, ST), :].rearrange("p a d -> p (a d)")
                nc.vector.tensor_tensor(xb, xb, t[:].rearrange("p a d -> p (a d)"), ALU.add).then_inc(summed, 1)

            def chosen(ins, b, k):
                ins.then_inc(pick_s, 1)
                dve.wait_ge(pick_s, PICKS * b + k + 1)

            def take_logits(b):
                dve.wait_ge(gated, b + 1)
                chosen(nc.vector.tensor_copy(logits[:].rearrange("p i e -> p (i e)"), ps_m[:, 0:ST * E]), b, 0)

            def best(b, r):
                k = 1 + 6 * r
                chosen(nc.vector.tensor_reduce(top[:, r, :], logits[:], X, ALU.max), b, k)
                chosen(nc.vector.tensor_tensor(eq[:], logits[:], top[:, r, :].unsqueeze(2).broadcast_to([P, ST, E]),
                                               ALU.is_equal), b, k + 1)
                chosen(nc.vector.tensor_tensor(eq[:], eq[:], rev[:], ALU.mult), b, k + 2)
                chosen(nc.vector.tensor_reduce(pick[:], eq[:], X, ALU.max), b, k + 3)
                chosen(nc.vector.tensor_tensor(one[:, r], eq[:], pick[:].unsqueeze(2).broadcast_to([P, ST, E]),
                                               ALU.is_equal), b, k + 4)

            def strike_best(b):
                chosen(nc.vector.scalar_tensor_tensor(logits[:], one[:, 0], NEG_MIN, logits[:], ALU.mult, ALU.add), b, 6)

            def take_diff(b):
                chosen(nc.vector.tensor_tensor(diff[:], top[:, 1, :], top[:, 0, :], ALU.subtract), b, 12)

            def weigh(b):
                dve.wait_ge(ex_ready, b + 1)
                if late(b, 1):
                    dve.wait_ge(mixT_ps, b)
                nc.vector.tensor_scalar(wt[:, 0, :], ex[:], 1.0, None, ALU.add).then_inc(weighed, 1)
                dve.wait_ge(weighed, 5 * b + 1)
                nc.vector.reciprocal(wt[:, 0, :], wt[:, 0, :]).then_inc(weighed, 1)
                dve.wait_ge(weighed, 5 * b + 2)
                nc.vector.tensor_tensor(wt[:, 1, :], wt[:, 0, :], ex[:], ALU.mult).then_inc(weighed, 1)
                dve.wait_ge(weighed, 5 * b + 3)
                for r in range(2):
                    nc.vector.tensor_tensor(part[:, r], one[:, r], wt[:, r, :].unsqueeze(2).broadcast_to([P, ST, E]),
                                            ALU.mult).then_inc(weighed, 1)
                dve.wait_ge(weighed, 5 * b + 5)
                chosen(nc.vector.tensor_tensor(mix[:, :, 0:E], part[:, 0], part[:, 1], ALU.add), b, PICKS - 1)

            def take_mixT(b):
                dve.wait_ge(mixT_ps, b + 1)
                if late(b, 1):
                    dve.wait_ge(b2_ps, b)
                nc.vector.tensor_copy(mixT[:].rearrange("p i e -> p (i e)"), ps_c[:, 0:ST * P]).then_inc(mixT_ready, 1)

            def add_b2(b):
                dve.wait_ge(b2_ps, b + 1)
                dve.wait_ge(summed, SUMS * b + 7)
                xb = c.x[:, bass.ds(b * ST, ST), :].rearrange("p a d -> p (a d)")
                nc.vector.tensor_tensor(xb, xb, ps_m[:], ALU.add).then_inc(summed, 1)

            def rest_tT(b):
                dve.wait_ge(tT_round, b + 1)
                for dc in range(DC):
                    last = nc.vector.scalar_tensor_tensor(tT[1][:, dc, :], ps_m[:, dc * S:(dc + 1) * S], norm_w[:, dc:dc + 1],
                                                          tT[0][:, dc, :].bitcast(F32), ALU.mult, ALU.subtract)
                last.then_inc(tT_ready, 1)

            def new_stats(b):
                dve.wait_ge(summed, SUMS * b + SUMS)
                batch_stats(nc, dve, c, stats, b)

            def split_h(g, s, chunks):
                for f in chunks:
                    dve.wait_ge(h_act, FC * g + f + 1)
                    if late(g, 2) and f == 0:
                        dve.wait_ge(o_ps, 2 * g - 2)
                    nc.vector.tensor_copy(hT[0][:, s % 2, f, :], h[:, f, :]).then_inc(h_round, 1)
                    dve.wait_ge(h_round, FC * g + f + 1)
                    nc.vector.tensor_tensor(hT[1][:, s % 2, f, :], h[:, f, :], hT[0][:, s % 2, f, :].bitcast(F32),
                                            ALU.subtract).then_inc(h_ready, 1)

            def add_expert(g, s, b):
                for i in range(ST):
                    dve.wait_ge(o_ps, 2 * g + i + 1)
                    dve.wait_ge(summed, SUMS * b + (1, 2 + i, 4 + i, 8)[s] if s < 4 else SUMS * b + place(s - 1) + i)
                    xt = c.x[:, bass.ds(b * ST + i, 1), :].rearrange("p a d -> p (a d)")
                    nc.vector.scalar_tensor_tensor(xt, ps_o[i][:, 0:D], mix[:, i, s:s + 1], xt, ALU.mult, ALU.add).then_inc(summed, 1)

            def slot(b, s):
                now = lagged(b, s, 0, E)
                if s == 0 and late_batch(b):
                    take_logits(b)
                    best(b, 0)
                    strike_best(b)
                if now:
                    split_h(now[0], s, (0, 1))
                if s == 0 and late_batch(b):
                    best(b, 1)
                    take_diff(b)
                if s == 1:
                    weigh(b)
                if now:
                    split_h(now[0], s, (2, 3))
                    if not late(b, 1):
                        pieces.rest(nc, dve, 2 * s + 5, 2 * s + 7)
                if s == E - 1 and (not isinstance(b, int) or b + 1 < B):
                    rest_tT(b + 1)
                if at := lagged(b, s, 1, E):
                    if at[1] == 0:
                        add_y(at[2])
                    add_expert(*at)
                if s == 2:
                    take_mixT(b)
                if s == 3:
                    add_b2(b)
                if s == 4 and (not isinstance(b, int) or b + 1 < B):
                    normalise(b + 1)
                if late(b, 1) and s == 5:
                    new_stats(b - 1)

            normalise(0)
            dve.wait_ge(small_in, 48)
            rest_tT(0)
            pieces.rest(nc, dve, 0, 5)
            run_steps(dve, E, slot, LAST)
            new_stats(B - 1)

        @block.scalar
        def _(act):
            act.wait_ge(root, 3)
            nc.scalar.activation(rstd[:], c.mv[:, :, 1:2].rearrange("p a d -> p (a d)"), ACT.Sqrt, bias=c.eps[:]).then_inc(root, 1)
            act.wait_ge(root, 7)
            nc.scalar.activation(ms[:], ms[:], ACT.Sqrt, bias=rms_eps[:]).then_inc(root, 1)
            act.wait_ge(small_in, 48)

            def take_tT(b):
                act.wait_ge(tT_ps, b + 1)
                for dc in range(DC):
                    last = nc.scalar.mul(tT[0][:, dc, :], ps_m[:, dc * S:(dc + 1) * S], norm_w[:, dc:dc + 1])
                last.then_inc(tT_round, 1)

            def gelu(g, s):
                for f in range(FC):
                    act.wait_ge(h_ps, FC * g + f + 1)
                    if late(g, 1):
                        act.wait_ge(h_ready, FC * g + f - FC + 1)
                    nc.scalar.activation(h[:, f, :], ps_h[f][:, 0:S], ACT.Gelu,
                                         bias=b1[:, FC * s + f:FC * s + f + 1]).then_inc(h_act, 1)

            def slot(b, s):
                if at := lagged(b, s, 0, E):
                    gelu(at[0], at[1])
                    if not late(b, 1):
                        pieces.round(nc, act, 2 * s + 5, 2 * s + 7)
                if s == 0 and late_batch(b):
                    act.wait_ge(pick_s, PICKS * b + PICKS - 1)
                    if late(b, 1):
                        act.wait_ge(weighed, 5 * b)
                    nc.scalar.activation(ex[:], diff[:], ACT.Exp).then_inc(ex_ready, 1)
                if s == E - 1 and (not isinstance(b, int) or b + 1 < B):
                    take_tT(b + 1)

            take_tT(0)
            pieces.round(nc, act, 0, 5)
            run_steps(act, E, slot, LAST)


def small_heads(nc, c, tag, w_qk, w_v, load_next, softmax, bq=None, bk=None, bv=None, w_out=None):
    STEPS, J, HD, W = 4, 4, 16, 32
    V_LAG = 3 if softmax else 2
    B_LAG = V_LAG + 1
    LAST = B_LAG if softmax else B_LAG + 2
    SW = ST * S if softmax else 3 * P
    with ExitStack() as ctx:
        sb = lambda name, shape: ctx.enter_context(nc.sbuf_tensor(f"{tag}_{name}", shape, F32))
        ps = lambda name: ctx.enter_context(nc.psum_tensor(f"{tag}_{name}", [P, 512], F32))
        sem = lambda name: ctx.enter_context(nc.semaphore(f"{tag}_{name}"))
        rstd = sb("rstd", [P, TILES])
        xn = sb("xn", [P, ST, D])
        xnT = sb("xnT", [P, DC, S])
        v_all = sb("v_all", [P, ST, D])
        qk = sb("qk", [P, 2, 2, S])
        split = sb("split", [P, 2, J, S])
        vp = sb("vp", [P, STEPS, ST, J, W])
        wT = sb("wT", [P, 2, J, SW])
        zT = sb("zT", [P, 2, S])
        den = sb("den", [P, ST, J])
        inv = sb("inv", [P, ST, J])
        if softmax:
            ctx_stage = sb("ctx_stage", [P, DC, S])
            ctxT = sb("ctxT", [P, DC, S])
            nmx = sb("nmx", [P, J, ST])
            pr = sb("pr", [P, J, ST, S])
            o = sb("o", [P, ST, J, HD])
        else:
            low = sb("low", [P, 2 * S])
            o_all = sb("o_all", [P, ST, D])
            oT = sb("oT", [P, DC, S])
        ps_p = ps("ps_p")
        ps_s = [ps(f"ps_s{j}") for j in range(J)]
        ps_z = ps("ps_z")
        ps_t = [ps("ps_t0"), ps("ps_t1")]

        root = sem("root")
        xn_ready = sem("xn_ready")
        xnT_ps = sem("xnT_ps")
        xnT_ready = sem("xnT_ready")
        ctx_in = sem("ctx_in")
        ctx_ready = sem("ctx_ready")
        proj = sem("proj")
        v_ps = sem("v_ps")
        v_taken = sem("v_taken")
        qk_ready = sem("qk_ready")
        phi_s = sem("phi_s")
        filled = sem("filled")
        v_ready = sem("v_ready")
        split_ready = sem("split_ready")
        scored = sem("scored")
        maxed = sem("maxed")
        exped = sem("exped")
        turned = sem("turned")
        w_even = sem("w_even")
        w_odd = sem("w_odd")
        z_done = sem("z_done")
        zT_ready = sem("zT_ready")
        backed = sem("backed")
        den_s = sem("den_s")
        o_ready = sem("o_ready")
        oT_ps = sem("oT_ps")
        oT_ready = sem("oT_ready")
        out_ps = sem("out_ps")
        added = sem("added")
        stats = sem("stats")

        block = ctx.enter_context(nc.Block())

        @block.sync
        def _(sp):
            if not softmax:
                load_next(sp)
            else:
                def batch(b):
                    if late(b, 1):
                        sp.wait_ge(ctx_ready, b)
                    sp.dma_start(ctx_stage[:], c.dram["ctxT"][:, bass.ds(b, 1), :, :].rearrange("p a c s -> p (a c) s")).then_inc(ctx_in, 16)
                batch(0)
                load_next(sp)
                with sp.Fori(1, B) as b:
                    batch(b)

        if softmax:
            @block.gpsimd
            def _(pool):
                def batch(b):
                    pool.wait_ge(ctx_in, 16 * b + 16)
                    if late(b, 1):
                        pool.wait_ge(proj, 2 * b)
                    pool.sem_inc(c.pool_waited, 1)
                    nc.gpsimd.tensor_copy(ctxT[:], ctx_stage[:]).then_inc(ctx_ready, 1)
                batch(0)
                with pool.Fori(1, B) as b:
                    batch(b)

        @block.tensor
        def _(pe):
            c.wait_weights(pe, tag)
            src = ctxT if softmax else xnT

            def turn_x(b):
                pe.wait_ge(xn_ready, b + 1)
                if late(b, 1):
                    pe.wait_ge(qk_ready, 2 * b)
                for dc in range(DC):
                    for i in range(ST):
                        last = nc.tensor.transpose(ps_p[:, dc * S + i * P:dc * S + (i + 1) * P],
                                                   xn[:, i, dc * P:(dc + 1) * P], c.ident[:])
                last.then_inc(xnT_ps, 1)

            def project(g, s, b):
                if s == 0:
                    pe.wait_ge(xnT_ready, b + 1)
                    if softmax:
                        pe.wait_ge(ctx_ready, b + 1)
                if s == 1:
                    pe.wait_ge(qk_ready, 2 * b + 1)
                    for i in range(ST):
                        for dc in range(DC):
                            last = nc.tensor.matmul(ps_p[:, i * D:(i + 1) * D], src[:, dc, i * P:(i + 1) * P],
                                                    w_v[:, dc, :], start=(dc == 0), stop=(dc == DC - 1))
                    last.then_inc(v_ps, 1)
                if s == 2:
                    pe.wait_ge(v_taken, b + 1)
                if s % 2 == 0:
                    for w in range(2):
                        for dc in range(DC):
                            last = nc.tensor.matmul(ps_p[:, w * S:(w + 1) * S], w_qk[:, s // 2, w, dc, :],
                                                    (xnT if w == 0 else src)[:, dc, :], start=(dc == 0), stop=(dc == DC - 1))
                    last.then_inc(proj, 1)

            def scores(g, s, j):
                if j == 0:
                    pe.wait_ge(split_ready, g + 1)
                if late(g, 1):
                    if softmax:
                        pe.wait_ge(exped, J * g + j - J + 1)
                    else:
                        pe.wait_ge((w_even, w_odd)[j % 2], 2 * g - 1 + j // 2)
                for i in range(ST):
                    if softmax:
                        last = nc.tensor.matmul(ps_s[j][:, i * S:(i + 1) * S], split[:, s % 2, j, i * P:(i + 1) * P],
                                                qk[:, s // 2, 1, :], start=True, stop=True)
                    else:
                        last = nc.tensor.matmul(ps_s[j][:, i * S:(i + 1) * S - i * P], split[:, s % 2, j, i * P:(i + 1) * P],
                                                qk[:, s // 2, 0, i * P:S], start=True, stop=True)
                last.then_inc(scored, 1)

            def turn(g, s, j):
                pe.wait_ge(exped, J * g + j + 1)
                if late(g, 1) or j >= 2:
                    pe.wait_ge((w_even, w_odd)[j % 2], 2 * g + j // 2)
                for i in range(ST):
                    for t in range(ST):
                        last = nc.tensor.transpose(ps_t[j % 2][:, t * S + i * P:t * S + (i + 1) * P],
                                                   pr[:, j, i, t * P:(t + 1) * P], c.ident[:])
                last.then_inc(turned, 1)

            def values(g, s):
                pe.wait_ge(v_ready, g + 1)
                pe.wait_ge(w_even, 2 * g + 2)
                pe.wait_ge(w_odd, 2 * g + 2)
                if late(g, 1):
                    pe.wait_ge(zT_ready, g)
                    pe.wait_ge(o_ready, g)
                for t in range(ST):
                    q0 = 0 if softmax else t * P
                    for j in range(J):
                        last = nc.tensor.matmul(ps_z[W * j:W * (j + 1), q0:S], vp[:, s, t, j, :],
                                                wT[:, s % 2, j, t * S:t * S + S - q0], start=(t == 0), stop=(t == ST - 1),
                                                tile_position=(0, W * j))
                last.then_inc(z_done, 1)

            def back(g, s):
                pe.wait_ge(zT_ready, g + 1)
                for i in range(ST):
                    last = nc.tensor.transpose(ps_z[:, S + i * P:S + (i + 1) * P], zT[:, s % 2, i * P:(i + 1) * P], c.ident[:])
                last.then_inc(backed, 1)

            def turn_o(b):
                pe.wait_ge(o_ready, STEPS * b + STEPS)
                if late(b, 1):
                    pe.wait_ge(added, b)
                for dc in range(DC):
                    for i in range(ST):
                        last = nc.tensor.transpose(ps_t[0][:, dc * S + i * P:dc * S + (i + 1) * P],
                                                   o_all[:, i, dc * P:(dc + 1) * P], c.ident[:])
                last.then_inc(oT_ps, 1)

            def output(b):
                pe.wait_ge(oT_ready, b + 1)
                for i in range(ST):
                    for dc in range(DC):
                        last = nc.tensor.matmul(ps_t[0][:, i * D:(i + 1) * D], oT[:, dc, i * P:(i + 1) * P],
                                                w_out[:, dc, :], start=(dc == 0), stop=(dc == DC - 1))
                last.then_inc(out_ps, 1)

            def slot(b, s):
                if at := lagged(b, s, 0, STEPS):
                    project(*at)
                if at := lagged(b, s, B_LAG, STEPS):
                    back(at[0], at[1])
                if w_out is not None and (at := lagged(b, s, B_LAG + 1, STEPS)) and at[1] == STEPS - 1:
                    turn_o(at[2])
                for j in range(J):
                    if at := lagged(b, s, 1, STEPS):
                        scores(at[0], at[1], j)
                    if softmax and (at := lagged(b, s, 2, STEPS)):
                        turn(at[0], at[1], j)
                if s == STEPS - 1 and (not isinstance(b, int) or b + 1 < B):
                    turn_x(b + 1)
                if at := lagged(b, s, V_LAG, STEPS):
                    values(at[0], at[1])
                if w_out is not None:
                    if (at := lagged(b, s, B_LAG + 2, STEPS)) and at[1] == STEPS - 1:
                        output(at[2])

            turn_x(0)
            run_steps(pe, STEPS, slot, LAST)

        @block.vector
        def _(dve):
            nc.vector.memset(vp[:], 0.0).then_inc(filled, 1)
            dve.wait_ge(filled, 1)
            nc.vector.memset(vp[:, :, :, :, HD:HD + 1], 1.0).then_inc(filled, 1)
            dve.wait_ge(root, 1)
            nc.vector.reciprocal(rstd[:], rstd[:]).then_inc(root, 1)
            dve.wait_ge(root, 2)
            dve.wait_ge(filled, 2)
            c.wait_weights(dve, tag)

            def normalise(b):
                if late(b, 1):
                    dve.wait_ge(xnT_ps, b)
                for i in range(ST):
                    n = b * ST + i
                    last = nc.vector.tensor_scalar(xn[:, i, :], c.x[:, bass.ds(n, 1), :].rearrange("p a d -> p (a d)"),
                                                   c.mv[:, bass.ds(n, 1), 0:1].rearrange("p a d -> p (a d)"),
                                                   rstd[:, bass.ds(n, 1)], ALU.subtract, ALU.mult)
                last.then_inc(xn_ready, 1)

            def features(g, s, b):
                n = 2 * b + s // 2
                dve.wait_ge(proj, n + 1)
                if late(g, 1):
                    dve.wait_ge(qk_ready, n)
                nc.vector.tensor_scalar(low[:], ps_p[:], 0.0, None, ALU.min).then_inc(phi_s, 1)
                dve.wait_ge(phi_s, 2 * n + 2)
                if late(g, STEPS):
                    dve.wait_ge(scored, J * g - 2 * J)
                nc.vector.scalar_tensor_tensor(qk[:, s // 2].rearrange("p w s -> p (w s)"), ps_p[:], 0.0, low[:],
                                               ALU.max, ALU.add).then_inc(qk_ready, 1)

            def fill_v(g, s, b):
                dve.wait_ge(v_taken, b + 1)
                if late(g, STEPS):
                    dve.wait_ge(z_done, g - STEPS + 1)
                for i in range(ST):
                    got = v_all[:, i, s * J * HD:(s + 1) * J * HD].rearrange("p (j e) -> p j e", j=J)
                    if bv is not None:
                        last = nc.vector.tensor_tensor(vp[:, s, i, :, 0:HD], got,
                                                       bv[:, s * J * HD:(s + 1) * J * HD].rearrange("p (j e) -> p j e", j=J), ALU.add)
                    else:
                        last = nc.vector.tensor_copy(vp[:, s, i, :, 0:HD], got)
                last.then_inc(v_ready, 1)

            def apart(g, s, b):
                dve.wait_ge(qk_ready, 2 * b + s // 2 + 1)
                if late(g, 2):
                    dve.wait_ge(scored, J * g - J)
                which, mask = (0, c.head16) if softmax else (1, c.head16k)
                for j in range(J):
                    m = J * (s % 2) + j
                    last = nc.vector.tensor_scalar(split[:, s % 2, j, :], qk[:, s // 2, which, :], mask[:, m:m + 1], None, ALU.mult)
                last.then_inc(split_ready, 1)

            def row_max(g, s, j):
                dve.wait_ge(scored, J * g + j + 1)
                if late(g, 1):
                    dve.wait_ge(exped, J * g + j - J + 1)
                nc.vector.tensor_reduce(nmx[:, j, :], ps_s[j][:].rearrange("p (i s) -> p i s", i=ST), X, ALU.max,
                                        negate=True).then_inc(maxed, 1)

            def take_odd(g, s, j):
                dve.wait_ge(turned, J * g + j + 1)
                if late(g, 2):
                    dve.wait_ge(z_done, g - 1)
                nc.vector.tensor_copy(wT[:, s % 2, j, :], ps_t[1][:]).then_inc(w_odd, 1)

            def keep_past(g, s, j):
                dve.wait_ge(scored, J * g + j + 1)
                if late(g, 2):
                    dve.wait_ge(z_done, g - 1)
                nc.vector.tensor_tensor(wT[:, s % 2, j, :], ps_s[j][:, 0:SW], c.keep[:], ALU.mult).then_inc((w_even, w_odd)[j % 2], 1)

            def finish(g, s, b):
                z = ps_z[:, S:2 * S].rearrange("p (i j w) -> p i j w", i=ST, j=J)
                dve.wait_ge(backed, g + 1)
                nc.vector.tensor_scalar(den[:], z[:, :, :, HD:HD + 1].rearrange("p i j w -> p i (j w)"), 1e-6, None,
                                        ALU.max).then_inc(den_s, 1)
                dve.wait_ge(den_s, 2 * g + 1)
                nc.vector.reciprocal(inv[:], den[:]).then_inc(den_s, 1)
                dve.wait_ge(den_s, 2 * g + 2)
                if softmax:
                    if late(g, 1):
                        dve.wait_ge(added, g)
                    dst = o[:]
                else:
                    if s == 0 and late(g, STEPS):
                        dve.wait_ge(oT_ps, b)
                    dst = o_all[:, :, s * J * HD:(s + 1) * J * HD].rearrange("p i (j e) -> p i j e", j=J)
                for i in range(ST):
                    last = nc.vector.tensor_tensor(dst[:, i], z[:, i, :, 0:HD],
                                                   inv[:, i, :].unsqueeze(2).broadcast_to([P, J, HD]), ALU.mult)
                last.then_inc(o_ready, 1)
                if softmax:
                    dve.wait_ge(o_ready, g + 1)
                    xs = c.x[:, bass.ds(b * ST, ST), s * J * HD:(s + 1) * J * HD]
                    nc.vector.tensor_tensor(xs, xs, o[:].rearrange("p i j e -> p i (j e)"), ALU.add).then_inc(added, 1)
                    if s == STEPS - 1:
                        dve.wait_ge(added, g + 1)
                        batch_stats(nc, dve, c, stats, b)

            def add_output(b):
                dve.wait_ge(out_ps, b + 1)
                xb = c.x[:, bass.ds(b * ST, ST), :].rearrange("p a d -> p (a d)")
                nc.vector.tensor_tensor(xb, xb, ps_t[0][:], ALU.add).then_inc(added, 1)
                dve.wait_ge(added, b + 1)
                batch_stats(nc, dve, c, stats, b)

            def slot(b, s):
                if at := lagged(b, s, 0, STEPS):
                    if not softmax and s % 2 == 0:
                        features(*at)
                    apart(*at)
                if at := lagged(b, s, B_LAG, STEPS):
                    finish(*at)
                if at := lagged(b, s, 1, STEPS):
                    fill_v(*at)
                for j in range(J):
                    if at := lagged(b, s, 1, STEPS):
                        if softmax:
                            row_max(at[0], at[1], j)
                        else:
                            keep_past(at[0], at[1], j)
                    if softmax and j % 2 and (at := lagged(b, s, 2, STEPS)):
                        take_odd(at[0], at[1], j)
                if w_out is not None and (at := lagged(b, s, B_LAG + 2, STEPS)) and at[1] == STEPS - 1:
                    add_output(at[2])
                if s == 1 and (not isinstance(b, int) or b + 1 < B):
                    normalise(b + 1)

            normalise(0)
            run_steps(dve, STEPS, slot, LAST)

        @block.scalar
        def _(act):
            nc.scalar.activation(rstd[:], c.mv[:, :, 1:2].rearrange("p a d -> p (a d)"), ACT.Sqrt,
                                 bias=c.eps[:]).then_inc(root, 1)
            c.wait_weights(act, tag)

            def take_xT(b):
                act.wait_ge(xnT_ps, b + 1)
                nc.scalar.copy(xnT[:].rearrange("p c s -> p (c s)"), ps_p[:]).then_inc(xnT_ready, 1)

            def take_qk(g, s, b):
                if s % 2:
                    return
                n = 2 * b + s // 2
                if softmax:
                    act.wait_ge(proj, n + 1)
                    if late(g, STEPS):
                        act.wait_ge(scored, J * g - 2 * J)
                    for w, bias in enumerate((bq, bk)):
                        last = nc.scalar.activation(qk[:, s // 2, w, :], ps_p[:, w * S:(w + 1) * S], ACT.Identity,
                                                    bias=bias[:, s // 2:s // 2 + 1])
                    last.then_inc(qk_ready, 1)
                else:
                    act.wait_ge(phi_s, 2 * n + 1)
                    nc.scalar.activation(low[:], low[:], ACT.Exp).then_inc(phi_s, 1)

            def take_v(b):
                act.wait_ge(v_ps, b + 1)
                if late(b, 1):
                    act.wait_ge(v_ready, STEPS * b)
                nc.scalar.copy(v_all[:].rearrange("p i d -> p (i d)"), ps_p[:]).then_inc(v_taken, 1)

            def exponentials(g, s, j):
                act.wait_ge(maxed, J * g + j + 1)
                if late(g, 1):
                    act.wait_ge(turned, J * g + j - J + 1)
                for i in range(ST):
                    last = nc.scalar.activation(pr[:, j, i, :], ps_s[j][:, i * S:(i + 1) * S], ACT.Exp, bias=nmx[:, j, i:i + 1])
                last.then_inc(exped, 1)

            def take_even(g, s, j):
                act.wait_ge(turned, J * g + j + 1)
                if late(g, 2):
                    act.wait_ge(z_done, g - 1)
                nc.scalar.copy(wT[:, s % 2, j, :], ps_t[0][:]).then_inc(w_even, 1)

            def take_z(g, s):
                act.wait_ge(z_done, g + 1)
                if late(g, 2):
                    act.wait_ge(backed, g - 1)
                nc.scalar.copy(zT[:, s % 2, :], ps_z[:, 0:S]).then_inc(zT_ready, 1)

            def slot(b, s):
                if at := lagged(b, s, 0, STEPS):
                    take_qk(*at)
                    if s == 1:
                        take_v(b)
                if softmax:
                    for j in range(J):
                        if j % 2 == 0 and (at := lagged(b, s, 2, STEPS)):
                            take_even(at[0], at[1], j)
                        if at := lagged(b, s, 1, STEPS):
                            exponentials(at[0], at[1], j)
                if s == STEPS - 1 and (not isinstance(b, int) or b + 1 < B):
                    take_xT(b + 1)
                if at := lagged(b, s, V_LAG, STEPS):
                    take_z(at[0], at[1])
                if w_out is not None and (at := lagged(b, s, B_LAG + 1, STEPS)) and at[1] == STEPS - 1:
                    act.wait_ge(oT_ps, at[2] + 1)
                    if late(at[2], 1):
                        act.wait_ge(out_ps, at[2])
                    nc.scalar.copy(oT[:].rearrange("p c s -> p (c s)"), ps_t[0][:]).then_inc(oT_ready, 1)

            take_xT(0)
            run_steps(act, STEPS, slot, LAST)


def gated_heads(nc, c, tag, w_qk, w_gate, w_val, w_out, load_next):
    STEPS, E, HEADS, LAST = 4, 8, 8, 5
    K = 4
    with ExitStack() as ctx:
        sb = lambda name, shape: ctx.enter_context(nc.sbuf_tensor(f"{tag}_{name}", shape, F32))
        ps = lambda name: ctx.enter_context(nc.psum_tensor(f"{tag}_{name}", [P, 512], F32))
        sem = lambda name: ctx.enter_context(nc.semaphore(f"{tag}_{name}"))
        rstd = sb("rstd", [P, TILES])
        xn = sb("xn", [P, ST, D])
        xnT = sb("xnT", [P, DC, S])
        rev = sb("rev", [P, ST * HEADS, E])
        gate = sb("gate", [P, ST * HEADS, E])
        eq = sb("eq", [P, ST * HEADS, E])
        best = sb("best", [P, ST * HEADS])
        gm = sb("gm", [P, ST * HEADS, E])
        gm_step = sb("gm_step", [P, STEPS, ST, 2, E])
        gm_late = sb("gm_late", [P, STEPS, ST, 2, E])
        qT = sb("qT", [P, 2, 2, S])
        kT = sb("kT", [P, 2, S])
        gv = sb("gv", [P, 2, E, 64])
        v = sb("v", [P, STEPS, ST, P])
        sm = sb("sm", [P, 2, ST, S])
        mx = sb("mx", [P, 2, ST])
        nmx = sb("nmx", [P, 2, ST])
        pr = sb("pr", [P, 4, ST, S])
        sums = sb("sums", [P, 4, ST])
        inv = sb("inv", [P, 4, ST])
        prT = sb("prT", [P, 4, ST, S])
        zT = sb("zT", [P, 2, S])
        z = sb("z", [P, ST, P])
        zg = sb("zg", [P, 2, E, 64])
        zgT = sb("zgT", [P, 2, 4, P])
        ps_qk, ps_s, ps_t, ps_g, ps_z, ps_out = (ps(n) for n in ("ps_qk", "ps_s", "ps_t", "ps_g", "ps_z", "ps_out"))
        ps_v = [ps("ps_v0"), ps("ps_v1")]

        root = sem("root")
        xn_ready = sem("xn_ready")
        xnT_ps = sem("xnT_ps")
        xnT_ready = sem("xnT_ready")
        gate_ps = sem("gate_ps")
        gate_exp = sem("gate_exp")
        pick_s = sem("pick_s")
        piece = sem("piece")
        kept = sem("kept")
        proj = sem("proj")
        q_ready = sem("q_ready")
        v_ps = sem("v_ps")
        v_gated = sem("v_gated")
        v_ready = sem("v_ready")
        scored = sem("scored")
        maxed = sem("maxed")
        negated = sem("negated")
        exped = sem("exped")
        inverted = sem("inverted")
        normed = sem("normed")
        turned = sem("turned")
        prT_ready = sem("prT_ready")
        z_done = sem("z_done")
        zT_ready = sem("zT_ready")
        backed = sem("backed")
        z_ready = sem("z_ready")
        zg_ready = sem("zg_ready")
        zg_ps = sem("zg_ps")
        zgT_ready = sem("zgT_ready")
        out_ps = sem("out_ps")
        added = sem("added")
        stored = sem("stored")
        PICKS = 8

        block = ctx.enter_context(nc.Block())

        @block.sync
        def _(sp):
            load_next(sp)

            def batch(b):
                sp.wait_ge(added, b + 1)
                sp.dma_start(c.out[:, bass.ds(b * ST, ST), :], c.x[:, bass.ds(b * ST, ST), :]).then_inc(stored, 16)
            batch(0)
            with sp.Fori(1, B) as b:
                batch(b)
            sp.wait_ge(stored, 16 * B)

        @block.gpsimd
        def _(pool):
            nc.gpsimd.iota(rev[:], pattern=[[0, ST * HEADS], [-1, E]], base=E, channel_multiplier=0,
                           allow_small_or_imprecise_dtypes=True).then_inc(root, 1)

        @block.tensor
        def _(pe):
            c.wait_weights(pe, tag)

            def turn_x(b):
                pe.wait_ge(xn_ready, b + 1)
                if late(b, 1):
                    pe.wait_ge(q_ready, STEPS * b)
                for dc in range(DC):
                    for i in range(ST):
                        last = nc.tensor.transpose(ps_qk[:, dc * S + i * P:dc * S + (i + 1) * P],
                                                   xn[:, i, dc * P:(dc + 1) * P], c.ident[:])
                last.then_inc(xnT_ps, 1)

            def gates(b):
                pe.wait_ge(xnT_ready, b + 1)
                if late(b, 2):
                    pe.wait_ge(zgT_ready, K * (STEPS * b - LAST))
                for i in range(ST):
                    for dc in range(DC):
                        last = nc.tensor.matmul(ps_g[:, i * E * HEADS:(i + 1) * E * HEADS], xnT[:, dc, i * P:(i + 1) * P],
                                                w_gate[:, dc, :], start=(dc == 0), stop=(dc == DC - 1))
                last.then_inc(gate_ps, 1)

            def project(g, s):
                if late(g, 1):
                    pe.wait_ge(q_ready, g)
                for w in range(2):
                    for dc in range(DC):
                        last = nc.tensor.matmul(ps_qk[:, w * S:(w + 1) * S], w_qk[:, s, w, dc, :], xnT[:, dc, :],
                                                start=(dc == 0), stop=(dc == DC - 1))
                last.then_inc(proj, 1)

            def project_v(g, s, k):
                j, i = k // 2, k % 2
                if late(g, 1) or k >= 2:
                    pe.wait_ge(v_gated, K * g + k - 1)
                for dc in range(DC):
                    last = nc.tensor.matmul(ps_v[i][:], xnT[:, dc, i * P:(i + 1) * P], w_val[:, 2 * s + j, dc, :],
                                            start=(dc == 0), stop=(dc == DC - 1))
                last.then_inc(v_ps, 1)

            def scores(g, s, j):
                pe.wait_ge(q_ready, g + 1)
                if late(g, 1) or j:
                    pe.wait_ge(maxed, 2 * g + j)
                for i in range(ST):
                    last = nc.tensor.matmul(ps_s[:, i * S:i * S + (i + 1) * P], qT[:, s % 2, j, i * P:(i + 1) * P],
                                            kT[:, s % 2, 0:(i + 1) * P], start=True, stop=True)
                last.then_inc(scored, 1)

            def turn(g, s, j):
                pe.wait_ge(normed, 2 * g + j + 1)
                if late(g, 1) or j:
                    pe.wait_ge(prT_ready, 2 * g + j)
                for i in range(ST):
                    for t in range(i + 1):
                        last = nc.tensor.transpose(ps_t[:, t * S + i * P:t * S + (i + 1) * P],
                                                   pr[:, 2 * (s % 2) + j, i, t * P:(t + 1) * P], c.ident[:])
                last.then_inc(turned, 1)

            def values(g, s):
                pe.wait_ge(v_ready, K * g + K)
                pe.wait_ge(prT_ready, 2 * g + 2)
                if late(g, 1):
                    pe.wait_ge(zT_ready, g)
                    pe.wait_ge(z_ready, g)
                for t in range(ST):
                    for j in range(2):
                        last = nc.tensor.matmul(ps_z[64 * j:64 * j + 64, t * P:S], v[:, s, t, 64 * j:64 * j + 64],
                                                prT[:, 2 * (s % 2) + j, t, t * P:S], start=(t == 0), stop=(t == ST - 1))
                last.then_inc(z_done, 1)

            def back(g, s):
                pe.wait_ge(zT_ready, g + 1)
                for i in range(ST):
                    last = nc.tensor.transpose(ps_z[:, S + i * P:S + (i + 1) * P], zT[:, s % 2, i * P:(i + 1) * P], c.ident[:])
                last.then_inc(backed, 1)

            def turn_zg(g, s, k, b):
                pe.wait_ge(zg_ready, K * g + k + 1)
                if late(g, 1) or k:
                    pe.wait_ge(zgT_ready, K * g + k)
                if s == STEPS - LAST % STEPS and k == 0:
                    pe.wait_ge(gate_exp, b)
                for p in range(E // 2):
                    last = nc.tensor.transpose(ps_g[:, p * P:(p + 1) * P],
                                               zg[:, k % 2, 2 * p:2 * p + 2, :].rearrange("p e k -> p (e k)"), c.ident[:])
                last.then_inc(zg_ps, 1)

            def output(g, s, k, b):
                j, i = k // 2, k % 2
                pe.wait_ge(zgT_ready, K * g + k + 1)
                if s == 0 and k == 0 and late(g, STEPS):
                    pe.wait_ge(added, b)
                for p in range(E // 2):
                    last = nc.tensor.matmul(ps_out[:, i * D:(i + 1) * D], zgT[:, k % 2, p, :], w_out[:, 2 * s + j, p, :],
                                            start=(s == 0 and k == 0 and p == 0), stop=(s == STEPS - 1 and j == 1 and p == E // 2 - 1),
                                            skip_group_check=True)
                last.then_inc(out_ps, 1)

            def slot(b, s):
                now, one, two = (lagged(b, s, d, STEPS) for d in range(3))
                five = lagged(b, s, 5, STEPS)
                if now:
                    if s == 0:
                        gates(b)
                    project(now[0], s)
                if at := lagged(b, s, 4, STEPS):
                    back(at[0], at[1])
                for k in range(K):
                    if now:
                        project_v(now[0], s, k)
                    if k % 2 == 0 and one:
                        scores(one[0], one[1], k // 2)
                    if k % 2 and two:
                        turn(two[0], two[1], k // 2)
                    if five:
                        turn_zg(five[0], five[1], k, b if now else B)
                        if k:
                            output(five[0], five[1], k - 1, five[2])
                if s == STEPS - 1 and (not isinstance(b, int) or b + 1 < B):
                    turn_x(b + 1)
                if at := lagged(b, s, 3, STEPS):
                    values(at[0], at[1])
                if five:
                    output(five[0], five[1], K - 1, five[2])

            turn_x(0)
            run_steps(pe, STEPS, slot, LAST)

        @block.vector
        def _(dve):
            dve.wait_ge(root, 2)
            nc.vector.reciprocal(rstd[:], rstd[:]).then_inc(root, 1)
            dve.wait_ge(root, 3)

            def normalise(b):
                if late(b, 1):
                    dve.wait_ge(xnT_ps, b)
                for i in range(ST):
                    n = b * ST + i
                    last = nc.vector.tensor_scalar(xn[:, i, :], c.x[:, bass.ds(n, 1), :].rearrange("p a d -> p (a d)"),
                                                   c.mv[:, bass.ds(n, 1), 0:1].rearrange("p a d -> p (a d)"),
                                                   rstd[:, bass.ds(n, 1)], ALU.subtract, ALU.mult)
                last.then_inc(xn_ready, 1)

            def choose(b):
                k = 0

                def done(ins):
                    nonlocal k
                    k += 1
                    ins.then_inc(pick_s, 1)
                    dve.wait_ge(pick_s, PICKS * b + k)

                wide = lambda a: a[:].unsqueeze(2).broadcast_to([P, ST * HEADS, E])
                dve.wait_ge(gate_exp, b + 1)
                done(nc.vector.tensor_scalar(gate[:], gate[:], 1.0, None, ALU.add))
                done(nc.vector.reciprocal(gate[:], gate[:]))
                done(nc.vector.tensor_reduce(best[:], gate[:], X, ALU.max))
                done(nc.vector.tensor_tensor(eq[:], gate[:], wide(best), ALU.is_equal))
                done(nc.vector.tensor_tensor(eq[:], eq[:], rev[:], ALU.mult))
                done(nc.vector.tensor_reduce(best[:], eq[:], X, ALU.max))
                done(nc.vector.tensor_tensor(eq[:], eq[:], wide(best), ALU.is_equal))
                if late(b, 1):
                    dve.wait_ge(piece, STEPS * b)
                done(nc.vector.tensor_tensor(gm[:], eq[:], gate[:], ALU.mult))

            def cut_piece(g, s):
                if late(g, STEPS):
                    dve.wait_ge(kept, g - STEPS + 1)
                nc.vector.tensor_scalar(gm_step[:, s], gm[:].rearrange("p (i h) e -> p i h e", i=ST)[:, :, 2 * s:2 * s + 2, :],
                                        1.0, None, ALU.mult).then_inc(piece, 1)
                dve.wait_ge(piece, g + 1)

            def keep_piece(g, s):
                if late(g, STEPS):
                    dve.wait_ge(zg_ready, K * (g - STEPS + 1))
                nc.vector.tensor_copy(gm_late[:, s], gm_step[:, s]).then_inc(kept, 1)

            def gate_v(g, s, k):
                j, i = k // 2, k % 2
                dve.wait_ge(v_ps, K * g + k + 1)
                if late(g, 1) or k >= 2:
                    dve.wait_ge(v_ready, K * g + k - 1)
                nc.vector.tensor_tensor(gv[:, k % 2], ps_v[i][:].rearrange("p (e k) -> p e k", e=E),
                                        gm_step[:, s, i, j, :].unsqueeze(2).broadcast_to([P, E, 64]), ALU.mult).then_inc(v_gated, 1)

            def sum_v(g, s, k):
                j, i = k // 2, k % 2
                dve.wait_ge(v_gated, K * g + k + 1)
                if late(g, STEPS):
                    dve.wait_ge(z_done, g - STEPS + 1)
                nc.vector.tensor_reduce(v[:, s, i, 64 * j:64 * j + 64], gv[:, k % 2].rearrange("p e k -> p k e"), X,
                                        ALU.add).then_inc(v_ready, 1)

            def row_max(g, s, j):
                dve.wait_ge(scored, 2 * g + j + 1)
                if late(g, 1):
                    dve.wait_ge(exped, 2 * g + j - 1)
                dve.sem_inc(c.waited, 1)
                for i in range(ST):
                    n = (i + 1) * P
                    add = c.causal_min[:, (ST - 1 - i) * P:(ST - 1 - i) * P + n]
                    last = nc.vector.tensor_tensor_reduce(sm[:, j, i, 0:n], ps_s[:, i * S:i * S + n], add, 1.0,
                                                          -3.0e38, ALU.add, ALU.max, mx[:, j, i:i + 1])
                last.then_inc(maxed, 1)
                dve.wait_ge(maxed, 2 * g + j + 1)
                nc.vector.tensor_scalar(nmx[:, j, :], mx[:, j, :], -1.0, None, ALU.mult).then_inc(negated, 1)

            def norm(g, s, j):
                r = 2 * (s % 2) + j
                dve.wait_ge(exped, 2 * g + j + 1)
                nc.vector.reciprocal(inv[:, r, :], sums[:, r, :]).then_inc(inverted, 1)
                dve.wait_ge(inverted, 2 * g + j + 1)
                for i in range(ST):
                    n = (i + 1) * P
                    last = nc.vector.tensor_scalar(pr[:, r, i, 0:n], pr[:, r, i, 0:n], inv[:, r, i:i + 1], None, ALU.mult)
                last.then_inc(normed, 1)

            def take_z(g):
                dve.wait_ge(backed, g + 1)
                if late(g, 1):
                    dve.wait_ge(zg_ready, K * g)
                nc.vector.tensor_copy(z[:].rearrange("p i m -> p (i m)"), ps_z[:, S:2 * S]).then_inc(z_ready, 1)

            def gate_z(g, s, k):
                j, i = k // 2, k % 2
                dve.wait_ge(z_ready, g + 1)
                dve.wait_ge(kept, g + 1)
                if late(g, 1) or k >= 2:
                    dve.wait_ge(zg_ps, K * g + k - 1)
                nc.vector.tensor_tensor(zg[:, k % 2], z[:, i, 64 * j:64 * j + 64].unsqueeze(1).broadcast_to([P, E, 64]),
                                        gm_late[:, s, i, j, :].unsqueeze(2).broadcast_to([P, E, 64]), ALU.mult).then_inc(zg_ready, 1)

            def add_to_x(b):
                dve.wait_ge(out_ps, K * STEPS * (b + 1))
                xb = c.x[:, bass.ds(b * ST, ST), :].rearrange("p a d -> p (a d)")
                nc.vector.tensor_tensor(xb, xb, ps_out[:], ALU.add).then_inc(added, 1)

            def slot(b, s):
                now, one, five = (lagged(b, s, d, STEPS) for d in (0, 1, 5))
                if now and s == 0:
                    choose(b)
                for k in range(K):
                    if five:
                        gate_z(five[0], five[1], k)
                    if now:
                        if k == 0:
                            cut_piece(now[0], s)
                        gate_v(now[0], s, k)
                    if one and k % 2 == 0:
                        row_max(one[0], one[1], k // 2)
                    if now:
                        sum_v(now[0], s, k)
                    if one and k % 2:
                        norm(one[0], one[1], k // 2)
                if at := lagged(b, s, 3, STEPS):
                    keep_piece(at[0], at[1])
                if at := lagged(b, s, 4, STEPS):
                    take_z(at[0])
                if five and five[1] == STEPS - 1:
                    add_to_x(five[2])
                if s == 1 and (not isinstance(b, int) or b + 1 < B):
                    normalise(b + 1)

            normalise(0)
            run_steps(dve, STEPS, slot, LAST)

        @block.scalar
        def _(act):
            act.wait_ge(root, 1)
            nc.scalar.activation(rstd[:], c.mv[:, :, 1:2].rearrange("p a d -> p (a d)"), ACT.Sqrt,
                                 bias=c.eps[:]).then_inc(root, 1)

            def take_xT(b):
                act.wait_ge(xnT_ps, b + 1)
                nc.scalar.copy(xnT[:].rearrange("p c s -> p (c s)"), ps_qk[:]).then_inc(xnT_ready, 1)

            def take_gates(b):
                act.wait_ge(gate_ps, b + 1)
                if late(b, 1):
                    act.wait_ge(pick_s, PICKS * b)
                nc.scalar.activation(gate[:].rearrange("p h e -> p (h e)"), ps_g[:, 0:ST * HEADS * E], ACT.Exp,
                                     scale=-1.0).then_inc(gate_exp, 1)

            def take_qk(g, s):
                act.wait_ge(proj, g + 1)
                if late(g, 2):
                    act.wait_ge(scored, 2 * g - 2)
                for j in range(2):
                    nc.scalar.mul(qT[:, s % 2, j, :], ps_qk[:, 0:S], c.half[:, j:j + 1])
                nc.scalar.copy(kT[:, s % 2, :], ps_qk[:, S:2 * S]).then_inc(q_ready, 1)

            def exponentials(g, s, j):
                r = 2 * (s % 2) + j
                act.wait_ge(negated, 2 * g + j + 1)
                if late(g, 2):
                    act.wait_ge(turned, 2 * g + j - 3)
                for i in range(ST):
                    n = (i + 1) * P
                    last = nc.scalar.activation(pr[:, r, i, 0:n], sm[:, j, i, 0:n], ACT.Exp, bias=nmx[:, j, i:i + 1],
                                                accum_out=sums[:, r, i:i + 1])
                last.then_inc(exped, 1)

            def take_prT(g, s, j):
                r = 2 * (s % 2) + j
                act.wait_ge(turned, 2 * g + j + 1)
                if late(g, 2):
                    act.wait_ge(z_done, g - 1)
                nc.scalar.copy(prT[:, r, 0, :], ps_t[:, 0:S])
                nc.scalar.copy(prT[:, r, 1, P:S], ps_t[:, S + P:2 * S]).then_inc(prT_ready, 1)

            def take_zT(g, s):
                act.wait_ge(z_done, g + 1)
                if late(g, 2):
                    act.wait_ge(backed, g - 1)
                nc.scalar.copy(zT[:, s % 2, :], ps_z[:, 0:S]).then_inc(zT_ready, 1)

            def take_zgT(g, k):
                act.wait_ge(zg_ps, K * g + k + 1)
                if late(g, 1) or k >= 2:
                    act.wait_ge(out_ps, K * g + k - 1)
                nc.scalar.copy(zgT[:, k % 2].rearrange("p e s -> p (e s)"), ps_g[:]).then_inc(zgT_ready, 1)

            def slot(b, s):
                now, one, two, five = (lagged(b, s, d, STEPS) for d in (0, 1, 2, 5))
                if now:
                    if s == 0:
                        take_gates(b)
                    take_qk(now[0], s)
                for k in range(K):
                    if one and k % 2 == 0:
                        exponentials(one[0], one[1], k // 2)
                    if two and k % 2:
                        take_prT(two[0], two[1], k // 2)
                    if five:
                        take_zgT(five[0], k)
                if s == STEPS - 1 and (not isinstance(b, int) or b + 1 < B):
                    take_xT(b + 1)
                if at := lagged(b, s, 3, STEPS):
                    take_zT(at[0], at[1])

            take_xT(0)
            run_steps(act, STEPS, slot, LAST)


def layouts(v):
    import numpy as np

    def pairs_hda(*ws):
        return np.stack([w.reshape(-1, 2, DC, P, 64).transpose(3, 0, 2, 1, 4).reshape(P, -1, DC, P) for w in ws], 2)

    def pairs_ed(*ws):
        return np.stack([w.reshape(-1, P, DC, P).transpose(3, 0, 2, 1) for w in ws], 2)

    def with_out(w, wo):
        v2 = w[:, :, 2].reshape(P, 4, 2, DC, P).transpose(0, 1, 3, 2, 4).reshape(P, 8, D)
        return np.concatenate([w[:, :, 0].reshape(P, 8, D), w[:, :, 1].reshape(P, 8, D), v2, wo], 2)

    def rows(w):
        return w.reshape(-1, P, w.shape[-1]).transpose(1, 0, 2)

    x = v["x"].reshape(TILES, P, D).transpose(1, 0, 2)
    ctx = v["ctx_1024"].reshape(B, S, DC, P).transpose(3, 0, 2, 1)
    mask = v["fside_Bx1xSxS2_0"].reshape(B, ST, P, S).transpose(2, 0, 1, 3)
    out = {
        "x": x, "ctxT": ctx, "mask": mask,
        "a0_w": with_out(pairs_hda(v["L0_attn_Wq"], v["L0_attn_Wk"], v["L0_attn_Wv"]), rows(v["L0_attn_Wo"].reshape(-1, D))),
        "a0_bq": v["L0_attn_bq"].reshape(-1, P).T, "a0_bk": v["L0_attn_bk"].reshape(-1, P).T,
        "a0_bv": v["L0_attn_bv"].reshape(-1, P).T, "a0_bo": v["L0_attn_bo"],
        "c0_w": with_out(pairs_ed(v["L0_xattn_Wq"], v["L0_xattn_Wk"], v["L0_xattn_Wv"]), rows(v["L0_xattn_Wo"].T)),
        "l1_qk": v["L1_attn_w_qkv"][:2 * D].reshape(2, 2, P, DC, P).transpose(4, 1, 0, 3, 2),
        "l1_v": rows(v["L1_attn_w_qkv"][2 * D:].T),
        "l1_out": rows(v["L1_attn_w_out"].T),
        "c1_qk": np.stack([v["L1_xattn_Wq"], v["L1_xattn_Wk"]]).reshape(2, 2, P, DC, P).transpose(4, 1, 0, 3, 2),
        "c1_v": rows(v["L1_xattn_Wv"].T),
        "c1_bq": v["L1_xattn_bq"].reshape(2, P).T, "c1_bk": v["L1_xattn_bk"].reshape(2, P).T,
        "c1_bv": v["L1_xattn_bv"],
        "f1_qk": np.stack([v["L1_ffn_w_q"], v["L1_ffn_w_k"]]).reshape(2, DC, P, 4, P).transpose(2, 3, 0, 1, 4),
        "f1_gate": rows(v["L1_ffn_w_gate"]),
        "f1_val": v["L1_ffn_value_experts"].reshape(8, 8, DC, P, 64).transpose(3, 1, 2, 0, 4).reshape(P, 8, DC, 512),
        "f1_out": v["L1_ffn_output_experts"].reshape(4, 2, 8, 64, D).transpose(1, 3, 2, 0, 4).reshape(P, 8, 4, D),
        "f0_w1": v["L0_ffn_w1"].reshape(8, 4, P, DC, P).transpose(4, 0, 1, 3, 2),
        "f0_w2": v["L0_ffn_w2"].reshape(8, D, 4, P).transpose(3, 0, 2, 1),
        "f0_gate": rows(v["L0_ffn_gate_w"].T),
        "f0_b1": v["L0_ffn_b1"].reshape(-1, P).T,
        "f0_b2": np.pad(v["L0_ffn_b2"], ((0, P - 8), (0, 0))),
        "f0_norm": v["L0_ffn_norm_weight"].reshape(DC, P).T,
    }
    return {k: np.ascontiguousarray(a) for k, a in out.items()}


def program(nc, dram, out, phases=6):
    c = Core()
    c.dram = dram
    c.spent = []
    c.out = out
    with ExitStack() as ctx:
        sb = lambda name, shape: ctx.enter_context(nc.sbuf_tensor(name, shape, F32))
        sem = lambda name: ctx.enter_context(nc.semaphore(name))
        c.x = sb("x_sb", [P, TILES, D])
        c.mv = sb("mean_var", [P, TILES, 2])
        c.bn = sb("bn", [P, ST, 6])
        c.mv2 = sb("mv2", [P, ST, 2])
        c.begun = sem("begun")
        c.waited = sem("waited")
        c.pool_waited = sem("pool_waited")
        c.eps = sb("eps", [P, 1])
        c.ident = sb("ident", [P, P])
        c.causal_min = sb("causal_min", [P, 2 * P])
        c.keep = sb("keep", [P, 3 * P])
        c.half = sb("half", [P, 2])
        c.half1 = sb("half1", [P, 2])
        c.head16 = sb("head16", [P, 8])
        c.head16k = sb("head16k", [P, 8])
        c.x_in = [sem(f"x_in{q}") for q in range(4)]
        loads = {}

        def load(eng, tag, dst, src):
            eng.dma_start(dst, src).then_inc(loads[tag][0], 16)
            loads[tag][1] += 16

        for tag in ("a0", "c0", "f0", "l1", "c1", "f1"):
            loads[tag] = [sem(f"w_{tag}"), 0]

        c.wait_weights = lambda eng, tag: eng.wait_ge(loads[tag][0], loads[tag][1])
        c.wait_small = c.wait_weights

        def weights(ctx, tag, **shapes):
            w = {k: ctx.enter_context(nc.sbuf_tensor(f"{tag}_weights_{k}", [P, *shape], F32)) for k, shape in shapes.items()}

            def fetch(eng):
                for k in w:
                    src = dram[f"{tag}_{k}"]
                    if len(src.shape) == 1:
                        src = src.partition_broadcast(P)
                    load(eng, tag, w[k][:], src)
            return w, fetch

        def load_none(sp):
            pass

        def halves(ctx, name, shape):
            return [ctx.enter_context(nc.sbuf_tensor(f"{name}_{n}", [P, *shape], F32R)) for n in ("rounded", "rest")]

        small = sb("small", [P, Pieces.STAGES * PIECE])
        stage = small[:].rearrange("p (n m) -> p n m", n=Pieces.STAGES)
        pieces = {tag: Pieces(nc, ctx, tag, stage, []) for tag in ("a0", "c0", "f0")}

        def attention_pieces(tag, w):
            src = dram[f"{tag}_w"]
            pieces[tag].list += [(w[0][:, n], w[1][:, n], src[:, n]) for n in range(8)]

        pieces["c0"].list += [(None, None, dram["c0_w"][:, n]) for n in range(Pieces.STAGES)]

        def load_c0(sp):
            pieces["c0"].load(sp, 0, Pieces.STAGES)

        with ExitStack() as room:
            c.causal = room.enter_context(nc.sbuf_tensor("causal", [P, 2 * P], F32))
            w = halves(room, "a0_w", [8, 4 * D])
            attention_pieces("a0", w)
            a0, load_a0 = weights(room, "a0", bq=[8], bk=[8], bv=[8], bo=[D])
            with nc.Block() as block:
                @block.scalar
                def _(act):
                    pieces["a0"].load(act, 0, Pieces.STAGES)
                    load_a0(act)
            constants(nc, c)
            attention(nc, c, "a0", pieces["a0"], w, load_c0, causal=True,
                      bias={"q": a0["bq"], "k": a0["bk"], "v": a0["bv"]}, bo=a0["bo"])
        pieces["c0"].list.clear()
        f0_flat = lambda ap: ap.rearrange("p a b m -> p (a b m)") if len(ap.shape) == 4 else ap.rearrange("p a m -> p (a m)")
        f0_src = [f0_flat(dram["f0_gate"])]
        for e in range(8):
            f0_src += [f0_flat(dram["f0_w1"][:, e]), f0_flat(dram["f0_w2"][:, e])]
        pieces["f0"].list += [(None, None, src) for src in f0_src]

        def load_f0(sp):
            pieces["f0"].load(sp, 0, Pieces.STAGES)

        if phases > 1:
            with ExitStack() as room:
                w = halves(room, "c0_w", [8, 4 * D])
                attention_pieces("c0", w)
                attention(nc, c, "c0", pieces["c0"], w, load_f0, cross=True)
        if phases > 2:
            l1_qk = small[:, 0:1024].rearrange("p (t h c m) -> p t h c m", t=2, h=2, c=DC)
            l1_v = small[:, 1024:1536].rearrange("p (c d) -> p c d", c=DC)
            l1_out = small[:, 1536:2048].rearrange("p (c d) -> p c d", c=DC)

            def load_l1(sp):
                load(sp, "l1", l1_qk, dram["l1_qk"])
                load(sp, "l1", l1_v, dram["l1_v"])
                load(sp, "l1", l1_out, dram["l1_out"])

            with ExitStack() as room:
                gate = halves(room, "f0_gate", [DC, 8])
                w1 = halves(room, "f0_w1", [8, 4, DC, P])
                w2 = halves(room, "f0_w2", [8, 4, D])
                places = [tuple(f0_flat(t[:]) for t in gate)]
                for e in range(8):
                    places += [tuple(f0_flat(t[:, e]) for t in w1), tuple(f0_flat(t[:, e]) for t in w2)]
                pieces["f0"].list[:] = [(*place, src) for place, src in zip(places, f0_src)]
                experts(nc, c, "f0", pieces["f0"], w1, w2, gate, load_l1)
        c1, load_c1 = weights(ctx, "c1", qk=[2, 2, DC, P], v=[DC, D], bv=[D], bq=[2], bk=[2])
        f1, load_f1 = weights(ctx, "f1", qk=[4, 2, DC, P], gate=[DC, 64], val=[8, DC, 512], out=[8, 4, D])

        def load_c1_f1(sp):
            load_c1(sp)
            load_f1(sp)

        if phases > 3:
            small_heads(nc, c, "l1", l1_qk, l1_v, load_c1_f1, softmax=False, w_out=l1_out)
        if phases > 4:
            small_heads(nc, c, "c1", c1["qk"], c1["v"], load_none, softmax=True, bq=c1["bq"], bk=c1["bk"], bv=c1["bv"])
        if phases > 5:
            gated_heads(nc, c, "f1", f1["qk"], f1["gate"], f1["val"], f1["out"], load_none)
        else:
            with nc.semaphore("stored") as stored, nc.Block() as block:
                @block.sync
                def _(sp):
                    sp.dma_start(out, c.x[:]).then_inc(stored, 16)
                    sp.wait_ge(stored, 16)


PHASES = 6


def kernel(**inputs):
    import numpy as np
    import concourse.bacc as bacc
    from concourse.bass_utils import run_bass_kernel_spmd

    nc = bacc.Bacc("TRN2", target_bir_lowering=False, num_devices=1)
    arrays, dram = {}, {}
    for name, a in layouts({k: np.asarray(v) for k, v in inputs.items()}).items():
        arrays[f"in_{name}"] = a
        dram[name] = nc.dram_tensor(f"in_{name}", a.shape, mybir.dt.from_np(a.dtype), kind="ExternalInput").ap()
    out = nc.dram_tensor("out_x", (P, TILES, D), F32, kind="ExternalOutput").ap()
    program(nc, dram, out, PHASES)
    r = run_bass_kernel_spmd(nc, [arrays], core_ids=[0])
    return r.results[0]["out_x"].transpose(1, 0, 2).reshape(B, S, D)
```

```python
from contextlib import ExitStack

import concourse.bass as bass
from concourse import mybir

ALU = mybir.AluOpType
ACT = mybir.ActivationFunctionType
F32 = mybir.dt.float32
F32R = mybir.dt.float32r
X = mybir.AxisListType.X

P = 128
D = 256
DC = D // P
S = 256
ST = S // P
B = 16
TILES = B * ST
X_PARTS = 8
LN_EPS = 1e-5
NEG_L0 = -100000.0
NEG_MIN = -1.0e30


def late(g, n):
    return not isinstance(g, int) or g >= n


class Core:
    pass


def run_steps(eng, steps, stages, last_lag):
    def batch(b):
        for s in range(steps):
            stages(b, s)
    lead = -(-last_lag // steps)
    for b in range(lead):
        batch(b)
    with eng.Fori(lead, B - 1) as b:
        batch(b)
    batch(B - 1)
    for s in range(last_lag):
        stages(B, s)


def lagged(b, s, d, steps):
    back = s - d
    at = back % steps
    over = (at - back) // steps
    if isinstance(b, int):
        n = b * steps + back
        if n < 0 or n >= B * steps:
            return None
        return n, at, b - over
    return b * steps + back, at, (b - over if over else b)



PIECE = 1024


class Pieces:
    STAGES = 2

    def __init__(self, nc, ctx, tag, stage, list):
        self.stage, self.list = stage, list
        self.moved = [ctx.enter_context(nc.semaphore(f"{tag}_moved{n}")) for n in range(self.STAGES)]
        self.rounded = ctx.enter_context(nc.semaphore(f"{tag}_rounded"))
        self.split = ctx.enter_context(nc.semaphore(f"{tag}_split"))

    def load(self, eng, first, last):
        for n in range(first, min(last, len(self.list))):
            src = self.list[n][2]
            if n >= self.STAGES:
                eng.wait_ge(self.split, n - self.STAGES + 1)
            eng.dma_start(self.stage[:, n % self.STAGES, 0:src.shape[1]], src).then_inc(self.moved[n % self.STAGES], 16)

    def load_rest(self, eng):
        self.load(eng, self.STAGES, len(self.list))
        eng.wait_ge(self.split, len(self.list))

    def round(self, nc, act, first, last):
        for n in range(first, min(last, len(self.list))):
            high, _, src = self.list[n]
            act.wait_ge(self.moved[n % self.STAGES], 16 * (n // self.STAGES + 1))
            nc.scalar.copy(high, self.stage[:, n % self.STAGES, 0:src.shape[1]]).then_inc(self.rounded, 1)

    def rest(self, nc, dve, first, last):
        for n in range(first, min(last, len(self.list))):
            high, low, src = self.list[n]
            dve.wait_ge(self.rounded, n + 1)
            nc.vector.tensor_tensor(low, self.stage[:, n % self.STAGES, 0:src.shape[1]], high.bitcast(F32),
                                    ALU.subtract).then_inc(self.split, 1)


def product3(nc, out, stationary, moving, start, stop, **kw):
    (sh, sl), (mh, ml) = stationary, moving
    nc.tensor.matmul(out, sh, mh, start=start, stop=False, **kw)
    nc.tensor.matmul(out, sh, ml, start=False, stop=False, **kw)
    return nc.tensor.matmul(out, sl, mh, start=False, stop=stop, **kw)


def constants(nc, c):
    with nc.semaphore("s_zero") as filled, nc.semaphore("s_const") as const_ready, \
            nc.semaphore("s_stats") as stats, nc.sbuf_tensor("bn_all", [P, TILES, 6], F32) as bn_all, \
            nc.Block() as block:
        c.spent += [filled, const_ready, stats]

        @block.gpsimd
        def _(pool):
            nc.gpsimd.memset(c.ident[:], 0.0).then_inc(filled, 1)
            nc.gpsimd.memset(c.causal[:], 0.0).then_inc(filled, 1)
            nc.gpsimd.memset(c.causal_min[:], 0.0).then_inc(filled, 1)
            nc.gpsimd.memset(c.half[:], 64 ** -0.5).then_inc(filled, 1)
            nc.gpsimd.memset(c.half1[:], 1.0).then_inc(filled, 1)
            nc.gpsimd.memset(c.head16[:], 0.25).then_inc(filled, 1)
            nc.gpsimd.memset(c.head16k[:], 1.0).then_inc(filled, 1)
            pool.wait_ge(filled, 7)
            nc.gpsimd.affine_select(out=c.ident[:], in_=c.ident[:], compare_op=ALU.not_equal, fill=1.0,
                                    base=0, pattern=[[-1, P]], channel_multiplier=1).then_inc(const_ready, 1)
            for mask, fill in ((c.causal, NEG_L0), (c.causal_min, NEG_MIN)):
                nc.gpsimd.affine_select(out=mask[:, P:], in_=mask[:, P:], compare_op=ALU.is_ge, fill=fill,
                                        base=0, pattern=[[-1, P]], channel_multiplier=1).then_inc(const_ready, 1)
            ready = 3
            for mask, width in ((c.half, 64), (c.half1, 64), (c.head16, 16), (c.head16k, 16)):
                n = P // width
                nc.gpsimd.affine_select(out=mask[:], in_=mask[:], compare_op=ALU.is_ge, fill=0.0, base=0,
                                        pattern=[[-width, n]], channel_multiplier=1).then_inc(const_ready, 1)
                ready += 1
                pool.wait_ge(const_ready, ready)
                nc.gpsimd.affine_select(out=mask[:], in_=mask[:], compare_op=ALU.is_ge, fill=0.0, base=width - 1,
                                        pattern=[[width, n]], channel_multiplier=-1).then_inc(const_ready, 1)
                ready += 1

        @block.sync
        def _(sp):
            for q in range(X_PARTS):
                t = TILES // X_PARTS
                sp.dma_start(c.x[:, q * t:(q + 1) * t, :], c.dram["x"][:, q * t:(q + 1) * t, :]).then_inc(c.x_in[q], 16)

        @block.vector
        def _(dve):
            nc.vector.memset(c.eps[:], LN_EPS).then_inc(c.begun, 1)
            for n in range(TILES):
                if n % (TILES // X_PARTS) == 0:
                    dve.wait_ge(c.x_in[n // (TILES // X_PARTS)], 16)
                nc.vector.bn_stats(bn_all[:, n, :], c.x[:, n, :]).then_inc(stats, 1)
            dve.wait_ge(stats, TILES)
            for n in range(TILES):
                nc.vector.bn_aggr(c.mv[:, n, :], bn_all[:, n, :])


def batch_stats(nc, dve, c, stats, b):
    if late(b, 1):
        dve.wait_ge(stats, 3 * b)
    dve.sem_inc(c.waited, 1)
    for i in range(ST):
        last = nc.vector.bn_stats(c.bn[:, i, :], c.x[:, bass.ds(b * ST + i, 1), :].rearrange("p a d -> p (a d)"))
    last.then_inc(stats, 1)
    dve.wait_ge(stats, 3 * b + 1)
    dve.sem_inc(c.waited, 1)
    for i in range(ST):
        last = nc.vector.bn_aggr(c.mv2[:, i, :], c.bn[:, i, :])
    last.then_inc(stats, 1)
    dve.wait_ge(stats, 3 * b + 2)
    nc.vector.tensor_scalar(c.mv[:, bass.ds(b * ST, ST), :].rearrange("p a d -> p (a d)"),
                            c.mv2[:].rearrange("p a d -> p (a d)"), 1.0, None, ALU.mult).then_inc(stats, 1)


def attention(nc, c, tag, pieces, w, load_next, cross=False, causal=False, bias=None, bo=None):
    PAIRS = 8
    LAST = 5
    AHEAD = 3
    with ExitStack() as ctx:
        sb = lambda name, shape, dt=F32: ctx.enter_context(nc.sbuf_tensor(f"{tag}_{name}", shape, dt))
        ps = lambda name: ctx.enter_context(nc.psum_tensor(f"{tag}_{name}", [P, 512], F32))

        def sem(name):
            c.spent.append(ctx.enter_context(nc.semaphore(f"{tag}_{name}")))
            return c.spent[-1]


        rstd = sb("rstd", [P, TILES])
        xn = sb("xn", [P, ST, D])
        xnT = [sb(f"xnT{n}", [P, DC, S], F32R) for n in range(2)]
        if cross:
            ctx_stage = sb("ctx_stage", [P, DC, S])
            ctxT = [sb(f"ctxT{n}", [P, DC, S], F32R) for n in range(2)]
            mask_stage = sb("mask_stage", [P, ST, S])
            mask = sb("mask", [P, ST, S])
        if cross:
            qT = [sb(f"qT{n}", [P, 2, 2, S], F32R) for n in range(2)]
            kT = [sb(f"kT{n}", [P, 2, S], F32R) for n in range(2)]
        else:
            qT = sb("qT", [P, 2, 2, S])
            kT = sb("kT", [P, 2, S])
        v = sb("v", [P, PAIRS, ST, P])
        sm = sb("sm", [P, 2, ST, S])
        pr = sb("pr", [P, 8, ST, S])
        prT = sb("prT", [P, 4, ST, S])
        zT = [sb(f"zT{n}", [P, 2, S], F32R) for n in range(2)]
        nmx = sb("nmx", [P, 2, ST])
        sums = sb("sums", [P, 8, ST])
        inv = sb("inv", [P, 8, ST])

        ps_q, ps_kv, ps_z, ps_out = ps("ps_q"), ps("ps_kv"), ps("ps_z"), ps("ps_out")
        ps_s = [ps("ps_s0"), ps("ps_s1")]
        ps_t = [ps("ps_t0"), ps("ps_t1")]

        rstd_s = sem("rstd")
        xn_ready = sem("xn_ready")
        xnT_ps = sem("xnT_ps")
        xnT_round = sem("xnT_round")
        xnT_ready = sem("xnT_ready")
        ctx_in = sem("ctx_in")
        ctx_round = sem("ctx_round")
        ctx_ready = sem("ctx_ready")
        mask_in = sem("mask_in")
        mask_ready = sem("mask_ready")
        proj = sem("proj")
        q_round = sem("q_round")
        q_ready = sem("q_ready")
        k_ready = sem("k_ready")
        v_ready = sem("v_ready")
        scored = sem("scored")
        maxed = sem("maxed")
        exped = sem("exped")
        inverted = sem("inverted")
        normed = sem("normed")
        turned = sem("turned")
        prT_ready = sem("prT_ready")
        z_done = sem("z_done")
        zT_round = sem("zT_round")
        zT_ready = sem("zT_ready")
        projected = sem("projected")
        out_read = sem("out_read")
        biased = sem("biased")
        stats = sem("stats")

        block = ctx.enter_context(nc.Block())

        def steps(eng, slot):
            run_steps(eng, PAIRS, slot, LAST)

        @block.sync
        def _(sp):
            def context(b):
                if late(b, 1):
                    sp.wait_ge(ctx_ready, b)
                    sp.wait_ge(mask_ready, b)
                sp.dma_start(ctx_stage[:], c.dram["ctxT"][:, bass.ds(b, 1), :, :].rearrange("p a c s -> p (a c) s")).then_inc(ctx_in, 16)
                sp.dma_start(mask_stage[:], c.dram["mask"][:, bass.ds(b, 1), :, :].rearrange("p a c s -> p (a c) s")).then_inc(mask_in, 16)
            if cross:
                context(0)
            pieces.load_rest(sp)
            load_next(sp)
            if cross:
                with sp.Fori(1, B) as b:
                    context(b)

        @block.tensor
        def _(pe):
            part = lambda s, n: [t[:, s, n * D:(n + 1) * D] for t in w]

            def turn_x(b):
                pe.wait_ge(xn_ready, b + 1)
                if late(b, 1):
                    pe.wait_ge(q_ready, PAIRS * b)
                for dc in range(DC):
                    for i in range(ST):
                        last = nc.tensor.transpose(ps_q[:, dc * S + i * P:dc * S + (i + 1) * P],
                                                   xn[:, i, dc * P:(dc + 1) * P], c.ident[:])
                last.then_inc(xnT_ps, 1)

            def project(g, s, b):
                if s == 0:
                    pe.wait_ge(xnT_ready, b + 1)
                if late(g, 1):
                    pe.wait_ge(q_ready, g)
                if not late(b, 1):
                    pe.wait_ge(pieces.split, s + 2 - s % 2)
                cols = lambda n, dc: [t[:, dc * P:(dc + 1) * P] for t in part(s, n)]
                for dc in range(DC):
                    last = product3(nc, ps_q[:, 0:S], cols(0, dc), [t[:, dc, :] for t in xnT], dc == 0, dc == DC - 1)
                last.then_inc(proj, 1)
                if s == 0 and cross:
                    pe.wait_ge(ctx_ready, b + 1)
                src = ctxT if cross else xnT
                if late(g, 1):
                    pe.wait_ge(v_ready, g)
                    if cross:
                        pe.wait_ge(k_ready, g)
                for dc in range(DC):
                    product3(nc, ps_kv[:, 0:S], cols(1, dc), [t[:, dc, :] for t in src], dc == 0, dc == DC - 1)
                i = s % 2
                for dc in range(DC):
                    last = product3(nc, ps_kv[:, S:2 * S], [t[:, dc, i * P:(i + 1) * P] for t in src],
                                    part(s - i + dc, 2), dc == 0, dc == DC - 1)
                last.then_inc(proj, 1)

            def scores(g, s, heads):
                pe.wait_ge(q_ready, g + 1)
                pe.wait_ge(k_ready, g + 1)
                for j in heads:
                    if late(g, 1):
                        pe.wait_ge(maxed, 2 * g + j - 1)
                    for i in range(ST):
                        if cross:
                            last = product3(nc, ps_s[j][:, i * S:(i + 1) * S], [t[:, s % 2, j, i * P:(i + 1) * P] for t in qT],
                                            [t[:, s % 2, :] for t in kT], True, True)
                        else:
                            n = (i + 1) * P
                            last = nc.tensor.matmul(ps_s[j][:, i * S:i * S + n], qT[:, s % 2, j, i * P:(i + 1) * P],
                                                    kT[:, s % 2, 0:n], start=True, stop=True)
                    last.then_inc(scored, 1)

            def turn(g, s):
                for j in range(2):
                    pe.wait_ge(normed, 2 * g + j + 1)
                    if late(g, 1):
                        pe.wait_ge(prT_ready, 2 * g + j - 1)
                    for i in range(ST):
                        for t in range(i + 1 if causal else ST):
                            last = nc.tensor.transpose(ps_t[j][:, t * S + i * P:t * S + (i + 1) * P],
                                                       pr[:, 2 * (s % 4) + j, i, t * P:(t + 1) * P], c.ident[:])
                    last.then_inc(turned, 1)

            def values(g, s):
                pe.wait_ge(v_ready, g + 2 - s % 2)
                pe.wait_ge(prT_ready, 2 * g + 2)
                if late(g, 1):
                    pe.wait_ge(zT_ready, g)
                z0 = (s % 2) * S
                for t in range(ST):
                    q0 = t * P if causal else 0
                    for j in range(2):
                        last = nc.tensor.matmul(ps_z[64 * j:64 * j + 64, z0 + q0:z0 + S],
                                                v[:, s, t, 64 * j:64 * j + 64],
                                                prT[:, 2 * (s % 2) + j, t, q0:S], start=(t == 0), stop=(t == ST - 1))
                last.then_inc(z_done, 1)

            def output(g, s, b):
                pe.wait_ge(zT_ready, g + 1)
                if s == 0 and late(g, PAIRS):
                    pe.wait_ge(out_read, b)
                for i in range(ST):
                    last = product3(nc, ps_out[:, i * D:(i + 1) * D], [t[:, s % 2, i * P:(i + 1) * P] for t in zT],
                                    part(s, 3), s == 0 and i == 0, s == PAIRS - 1, skip_group_check=True)
                last.then_inc(projected, 1)

            def slot(b, s):
                if at := lagged(b, s, 0, PAIRS):
                    project(*at)
                if at := lagged(b, s, 1, PAIRS):
                    scores(at[0], at[1], (0,))
                if s == PAIRS - 1 and (not isinstance(b, int) or b + 1 < B):
                    turn_x(b + 1)
                if at := lagged(b, s, 1, PAIRS):
                    scores(at[0], at[1], (1,))
                if at := lagged(b, s, 3, PAIRS):
                    turn(at[0], at[1])
                if at := lagged(b, s, 4, PAIRS):
                    values(at[0], at[1])
                if at := lagged(b, s, 5, PAIRS):
                    output(*at)

            turn_x(0)
            steps(pe, slot)

        @block.vector
        def _(dve):
            dve.wait_ge(rstd_s, 1)
            nc.vector.reciprocal(rstd[:], rstd[:]).then_inc(rstd_s, 1)
            dve.wait_ge(rstd_s, 2)

            def normalise(b):
                if late(b, 1):
                    dve.wait_ge(xnT_ps, b)
                for i in range(ST):
                    n = b * ST + i
                    last = nc.vector.tensor_scalar(xn[:, i, :], c.x[:, bass.ds(n, 1), :].rearrange("p a d -> p (a d)"),
                                                   c.mv[:, bass.ds(n, 1), 0:1].rearrange("p a d -> p (a d)"),
                                                   rstd[:, bass.ds(n, 1)], ALU.subtract, ALU.mult)
                last.then_inc(xn_ready, 1)

            def take_mask(b):
                dve.wait_ge(mask_in, 16 * b + 16)
                nc.vector.tensor_copy(mask[:], mask_stage[:]).then_inc(mask_ready, 1)
                dve.wait_ge(mask_ready, b + 1)

            def take_q(g, s):
                if cross:
                    dve.wait_ge(q_round, g + 1)
                else:
                    dve.wait_ge(proj, 2 * g + 1)
                if late(g, 2):
                    dve.wait_ge(scored, 2 * g - 2)
                for j in range(2):
                    if cross:
                        last = nc.vector.scalar_tensor_tensor(qT[1][:, s % 2, j, :], ps_q[:, 0:S], c.half1[:, j:j + 1],
                                                              qT[0][:, s % 2, j, :].bitcast(F32), ALU.mult, ALU.subtract)
                    else:
                        last = nc.vector.tensor_scalar(qT[:, s % 2, j, :], ps_q[:, 0:S], bias["q"][:, s:s + 1],
                                                       c.half[:, j:j + 1], ALU.add, ALU.mult)
                last.then_inc(q_ready, 1)

            def rest_k(g, s):
                dve.wait_ge(v_ready, g + 1)
                nc.vector.tensor_tensor(kT[1][:, s % 2, :], ps_kv[:, 0:S], kT[0][:, s % 2, :].bitcast(F32),
                                        ALU.subtract).then_inc(k_ready, 1)

            def row_max(g, s, j):
                dve.wait_ge(scored, 2 * g + j + 1)
                if late(g, 1):
                    dve.wait_ge(exped, 2 * g + j - 1)
                dve.sem_inc(c.waited, 1)
                for i in range(ST):
                    n = (i + 1) * P if causal else S
                    add = c.causal[:, (ST - 1 - i) * P:(ST - 1 - i) * P + n] if causal else mask[:, i, :]
                    last = nc.vector.tensor_tensor_reduce(sm[:, j, i, 0:n], ps_s[j][:, i * S:i * S + n], add, -1.0,
                                                          3.0e38, ALU.add, ALU.min, nmx[:, j, i:i + 1])
                last.then_inc(maxed, 1)

            def invert(g, s):
                dve.wait_ge(exped, 2 * g + 2)
                r = 2 * (s % 4)
                nc.vector.reciprocal(inv[:, r:r + 2, :], sums[:, r:r + 2, :]).then_inc(inverted, 1)

            def norm(g, s):
                dve.wait_ge(inverted, g + 1)
                for j in range(2):
                    r = 2 * (s % 4) + j
                    for i in range(ST):
                        n = (i + 1) * P if causal else S
                        last = nc.vector.tensor_scalar(pr[:, r, i, 0:n], pr[:, r, i, 0:n], inv[:, r, i:i + 1], None, ALU.mult)
                    last.then_inc(normed, 1)

            def rest_z(g, s):
                dve.wait_ge(zT_round, g + 1)
                z = ps_z[:, (s % 2) * S:(s % 2 + 1) * S]
                high = zT[0][:, s % 2, :].bitcast(F32)
                if bias is not None:
                    nc.vector.scalar_tensor_tensor(zT[1][:, s % 2, :], z, bias["v"][:, s:s + 1], high,
                                                   ALU.add, ALU.subtract).then_inc(zT_ready, 1)
                else:
                    nc.vector.tensor_tensor(zT[1][:, s % 2, :], z, high, ALU.subtract).then_inc(zT_ready, 1)

            def rest_inputs(b):
                flat = lambda t: t[:].rearrange("p c s -> p (c s)")
                dve.wait_ge(xnT_round, b + 1)
                nc.vector.tensor_tensor(flat(xnT[1]), ps_q[:], flat(xnT[0]).bitcast(F32), ALU.subtract).then_inc(xnT_ready, 1)
                if cross:
                    dve.wait_ge(ctx_round, b + 1)
                    nc.vector.tensor_tensor(flat(ctxT[1]), flat(ctx_stage), flat(ctxT[0]).bitcast(F32),
                                            ALU.subtract).then_inc(ctx_ready, 1)

            def add_to_x(b):
                dve.wait_ge(projected, PAIRS * b + PAIRS)
                xb = c.x[:, bass.ds(b * ST, ST), :].rearrange("p a d -> p (a d)")
                nc.vector.tensor_tensor(xb, xb, ps_out[:], ALU.add).then_inc(out_read, 1)

            def add_bias(b):
                dve.wait_ge(out_read, b + 1)
                for i in range(ST):
                    xt = c.x[:, bass.ds(b * ST + i, 1), :].rearrange("p a d -> p (a d)")
                    last = nc.vector.tensor_tensor(xt, xt, bo[:], ALU.add)
                last.then_inc(biased, 1)

            def new_stats(b):
                if bo is not None:
                    dve.wait_ge(biased, b + 1)
                else:
                    dve.wait_ge(out_read, b + 1)
                batch_stats(nc, dve, c, stats, b)

            def slot(b, s):
                if at := lagged(b, s, 5, PAIRS):
                    rest_z(at[0], at[1])
                if at := lagged(b, s, 0, PAIRS):
                    if not late(b, 1):
                        pieces.rest(nc, dve, s + AHEAD, s + AHEAD + 1)
                    take_q(at[0], at[1])
                    if cross:
                        rest_k(at[0], at[1])
                if s == PAIRS - 1 and (not isinstance(b, int) or b + 1 < B):
                    rest_inputs(b + 1)
                if at := lagged(b, s, 1, PAIRS):
                    if at[1] == 0 and cross:
                        take_mask(at[2])
                    row_max(at[0], at[1], 0)
                    row_max(at[0], at[1], 1)
                if at := lagged(b, s, 2, PAIRS):
                    invert(at[0], at[1])
                    norm(at[0], at[1])
                if s == 2 and (not isinstance(b, int) or b + 1 < B):
                    normalise(b + 1)
                after = b - 1
                if late(b, 1) and s == 4:
                    add_to_x(after)
                if late(b, 1) and s == 5 and bo is not None:
                    add_bias(after)
                if late(b, 1) and s == (5 if bo is None else 6):
                    new_stats(after)

            normalise(0)
            rest_inputs(0)
            pieces.rest(nc, dve, 0, AHEAD)
            steps(dve, slot)
            if bo is not None:
                add_bias(B - 1)
            new_stats(B - 1)

        @block.scalar
        def _(act):
            nc.scalar.activation(rstd[:], c.mv[:, :, 1:2].rearrange("p a d -> p (a d)"), ACT.Sqrt,
                                 bias=c.eps[:]).then_inc(rstd_s, 1)
            if bias is not None:
                c.wait_weights(act, tag)

            def take_xT(b):
                act.wait_ge(xnT_ps, b + 1)
                nc.scalar.copy(xnT[0][:].rearrange("p c s -> p (c s)"), ps_q[:]).then_inc(xnT_round, 1)
                if cross:
                    act.wait_ge(ctx_in, 16 * b + 16)
                    if late(b, 1):
                        act.wait_ge(proj, 2 * PAIRS * b)
                    nc.scalar.copy(ctxT[0][:], ctx_stage[:]).then_inc(ctx_round, 1)

            def round_q(g, s):
                act.wait_ge(proj, 2 * g + 1)
                if late(g, 2):
                    act.wait_ge(scored, 2 * g - 2)
                for j in range(2):
                    last = nc.scalar.mul(qT[0][:, s % 2, j, :], ps_q[:, 0:S], c.half1[:, j:j + 1])
                last.then_inc(q_round, 1)

            def take_kv(g, s):
                act.wait_ge(proj, 2 * g + 2)
                if late(g, 2):
                    act.wait_ge(scored, 2 * g - 2)
                if cross:
                    nc.scalar.copy(kT[0][:, s % 2, :], ps_kv[:, 0:S])
                else:
                    nc.scalar.activation(kT[:, s % 2, :], ps_kv[:, 0:S], ACT.Identity,
                                         bias=bias["k"][:, s:s + 1]).then_inc(k_ready, 1)
                if late(g, PAIRS):
                    act.wait_ge(z_done, g + 2 - s % 2 - PAIRS)
                nc.scalar.copy(v[:, s - s % 2:s - s % 2 + 2, s % 2, :],
                               ps_kv[:, S:2 * S].rearrange("p (n m) -> p n m", n=2)).then_inc(v_ready, 1)

            def take_z(g, s):
                act.wait_ge(z_done, g + 1)
                if late(g, 2):
                    act.wait_ge(projected, g - 1)
                z = ps_z[:, (s % 2) * S:(s % 2 + 1) * S]
                if bias is not None:
                    nc.scalar.activation(zT[0][:, s % 2, :], z, ACT.Identity, bias=bias["v"][:, s:s + 1]).then_inc(zT_round, 1)
                else:
                    nc.scalar.copy(zT[0][:, s % 2, :], z).then_inc(zT_round, 1)

            def exponentials(g, s, j):
                r = 2 * (s % 4) + j
                act.wait_ge(maxed, 2 * g + j + 1)
                if late(g, 4):
                    act.wait_ge(turned, 2 * g + j - 7)
                for i in range(ST):
                    n = (i + 1) * P if causal else S
                    last = nc.scalar.activation(pr[:, r, i, 0:n], sm[:, j, i, 0:n], ACT.Exp, bias=nmx[:, j, i:i + 1], scale=-1.0,
                                                accum_out=sums[:, r, i:i + 1])
                last.then_inc(exped, 1)

            def take_prT(g, s, j):
                r = 2 * (s % 2) + j
                act.wait_ge(turned, 2 * g + j + 1)
                if late(g, 2):
                    act.wait_ge(z_done, g - 1)
                if causal:
                    nc.scalar.copy(prT[:, r, 0, :], ps_t[j][:, 0:S])
                    nc.scalar.copy(prT[:, r, 1, P:S], ps_t[j][:, S + P:2 * S]).then_inc(prT_ready, 1)
                else:
                    nc.scalar.copy(prT[:, r, :, :].rearrange("p t s -> p (t s)"), ps_t[j][:]).then_inc(prT_ready, 1)

            def slot(b, s):
                if at := lagged(b, s, 5, PAIRS):
                    take_z(at[0], at[1])
                if at := lagged(b, s, 0, PAIRS):
                    if not late(b, 1):
                        pieces.round(nc, act, s + AHEAD, s + AHEAD + 1)
                    if cross:
                        round_q(at[0], at[1])
                    take_kv(at[0], at[1])
                if s == PAIRS - 1 and (not isinstance(b, int) or b + 1 < B):
                    take_xT(b + 1)
                if at := lagged(b, s, 3, PAIRS):
                    take_prT(at[0], at[1], 0)
                    take_prT(at[0], at[1], 1)
                if at := lagged(b, s, 1, PAIRS):
                    exponentials(at[0], at[1], 0)
                    exponentials(at[0], at[1], 1)

            take_xT(0)
            pieces.round(nc, act, 0, AHEAD)
            steps(act, slot)


def experts(nc, c, tag, pieces, w1, w2, gate_w, b1, b2, norm_w, load_next):
    E, FC, LAST = 8, 4, 1
    with ExitStack() as ctx:
        sb = lambda name, shape, dt=F32: ctx.enter_context(nc.sbuf_tensor(f"{tag}_{name}", shape, dt))
        ps = lambda name: ctx.enter_context(nc.psum_tensor(f"{tag}_{name}", [P, 512], F32))
        sem = lambda name: ctx.enter_context(nc.semaphore(f"{tag}_{name}"))
        rstd = sb("rstd", [P, TILES])
        ms = sb("ms", [P, TILES])
        rms_eps = sb("rms_eps", [P, 1])
        t = sb("t", [P, ST, D])
        tT = [sb(f"tT{n}", [P, DC, S], F32R) for n in range(2)]
        h = sb("h", [P, FC, S])
        hT = [sb(f"hT{n}", [P, 2, FC, S], F32R) for n in range(2)]
        rev = sb("rev", [P, ST, E])
        logits = sb("logits", [P, ST, E])
        eq = sb("eq", [P, ST, E])
        one = sb("one", [P, 2, ST, E])
        top = sb("top", [P, 2, ST])
        pick = sb("pick", [P, ST])
        diff = sb("diff", [P, ST])
        ex = sb("ex", [P, ST])
        wt = sb("wt", [P, 2, ST])
        part = sb("part", [P, 2, ST, E])
        mix = sb("mix", [P, ST, P])
        mixT = sb("mixT", [P, ST, P])
        ps_h = [ps(f"ps_h{n}") for n in range(FC)]
        ps_o = [ps("ps_o0"), ps("ps_o1")]
        ps_m, ps_c = ps("ps_m"), ps("ps_c")

        root = sem("root")
        t_ready = sem("t_ready")
        tT_ps = sem("tT_ps")
        tT_round = sem("tT_round")
        tT_ready = sem("tT_ready")
        gated = sem("gated")
        pick_s = sem("pick_s")
        ex_ready = sem("ex_ready")
        mixT_ps = sem("mixT_ps")
        mixT_ready = sem("mixT_ready")
        b2_ps = sem("b2_ps")
        h_ps = sem("h_ps")
        h_act = sem("h_act")
        h_round = sem("h_round")
        h_ready = sem("h_ready")
        o_ps = sem("o_ps")
        y_s = sem("y_s")
        summed = sem("summed")
        stats = sem("stats")
        weighed = sem("weighed")
        SUMS = 2 + 2 * E
        PICKS = 14

        def late_batch(b):
            return not isinstance(b, int) or b < B

        def place(e):
            return 2 + 2 * e + (1 if e >= 3 else 0)

        block = ctx.enter_context(nc.Block())

        @block.sync
        def _(sp):
            pieces.load_rest(sp)
            load_next(sp)

        @block.gpsimd
        def _(pool):
            nc.gpsimd.iota(rev[:], pattern=[[0, ST], [-1, E]], base=E, channel_multiplier=0,
                           allow_small_or_imprecise_dtypes=True).then_inc(root, 1)
            nc.gpsimd.memset(mix[:], 0.0).then_inc(root, 1)
            nc.gpsimd.memset(rms_eps[:], 1e-6).then_inc(root, 1)
            for spent in c.spent:
                pool.sem_clear(spent)

        @block.tensor
        def _(pe):
            c.wait_weights(pe, tag)

            def turn_t(b):
                pe.wait_ge(t_ready, b + 1)
                if late(b, 1):
                    pe.wait_ge(summed, SUMS * (b - 1) + 8)
                for dc in range(DC):
                    for i in range(ST):
                        last = nc.tensor.transpose(ps_m[:, dc * S + i * P:dc * S + (i + 1) * P],
                                                   t[:, i, dc * P:(dc + 1) * P], c.ident[:])
                last.then_inc(tT_ps, 1)

            def gates(b):
                pe.wait_ge(tT_ready, b + 1)
                if not late(b, 1):
                    pe.wait_ge(pieces.split, 1)
                for i in range(ST):
                    for dc in range(DC):
                        last = product3(nc, ps_m[:, i * E:(i + 1) * E], [a[:, dc, i * P:(i + 1) * P] for a in tT],
                                        [a[:, dc, :] for a in gate_w], dc == 0, dc == DC - 1)
                last.then_inc(gated, 1)

            def turn_mix(b):
                pe.wait_ge(pick_s, PICKS * b + PICKS)
                if late(b, 1):
                    pe.wait_ge(mixT_ready, b)
                for i in range(ST):
                    last = nc.tensor.transpose(ps_c[:, i * P:(i + 1) * P], mix[:, i, :], c.ident[:])
                last.then_inc(mixT_ps, 1)

            def weighted_b2(b):
                pe.wait_ge(mixT_ready, b + 1)
                for i in range(ST):
                    last = nc.tensor.matmul(ps_m[:, i * D:(i + 1) * D], mixT[:, i, :], b2[:], start=True, stop=True)
                last.then_inc(b2_ps, 1)

            def first(g, s, b):
                if s == 0:
                    pe.wait_ge(tT_ready, b + 1)
                if not late(b, 1):
                    pe.wait_ge(pieces.split, 2 * s + 2)
                for f in range(FC):
                    if late(g, 1):
                        pe.wait_ge(h_act, FC * g + f - FC + 1)
                    for dc in range(DC):
                        last = product3(nc, ps_h[f][:, 0:S], [a[:, s, f, dc, :] for a in w1],
                                        [a[:, dc, :] for a in tT], dc == 0, dc == DC - 1)
                    last.then_inc(h_ps, 1)

            def second(g, s, b):
                pe.wait_ge(h_ready, FC * g + FC)
                if not late(b, 1):
                    pe.wait_ge(pieces.split, 2 * s + 3)
                for i in range(ST):
                    if late(g, 1):
                        pe.wait_ge(summed, SUMS * b + place(s - 1) + i if s else SUMS * (b - 1) + place(E - 1) + i)
                    for f in range(FC):
                        last = product3(nc, ps_o[i][:, 0:D], [a[:, s % 2, f, i * P:(i + 1) * P] for a in hT],
                                        [a[:, s, f, :] for a in w2], f == 0, f == FC - 1)
                    last.then_inc(o_ps, 1)

            def slot(b, s):
                if s == 0 and late_batch(b):
                    gates(b)
                if at := lagged(b, s, 0, E):
                    first(*at)
                if s == E - 1 and (not isinstance(b, int) or b + 1 < B):
                    turn_t(b + 1)
                if at := lagged(b, s, 1, E):
                    second(*at)
                if s == 2:
                    turn_mix(b)
                if s == 3:
                    weighted_b2(b)

            turn_t(0)
            run_steps(pe, E, slot, LAST)

        @block.vector
        def _(dve):
            dve.wait_ge(root, 4)
            nc.vector.reciprocal(rstd[:], rstd[:]).then_inc(root, 1)
            dve.wait_ge(root, 5)
            nc.vector.tensor_tensor(ms[:], rstd[:], rstd[:], ALU.mult).then_inc(root, 1)
            dve.wait_ge(root, 6)
            nc.vector.tensor_tensor(ms[:], ms[:], c.mv[:, :, 1:2].rearrange("p a d -> p (a d)"), ALU.mult).then_inc(root, 1)
            dve.wait_ge(root, 8)
            nc.vector.reciprocal(ms[:], ms[:]).then_inc(root, 1)
            dve.wait_ge(root, 9)
            nc.vector.tensor_tensor(ms[:], ms[:], rstd[:], ALU.mult).then_inc(root, 1)
            dve.wait_ge(root, 10)

            def normalise(b):
                if late(b, 1):
                        dve.wait_ge(summed, SUMS * (b - 1) + 1)
                for i in range(ST):
                    n = b * ST + i
                    last = nc.vector.tensor_scalar(t[:, i, :], c.x[:, bass.ds(n, 1), :].rearrange("p a d -> p (a d)"),
                                                   c.mv[:, bass.ds(n, 1), 0:1].rearrange("p a d -> p (a d)"),
                                                   ms[:, bass.ds(n, 1)], ALU.subtract, ALU.mult)
                last.then_inc(t_ready, 1)

            def add_y(b):
                dve.wait_ge(tT_ps, b + 1)
                for i in range(ST):
                    n = b * ST + i
                    last = nc.vector.tensor_scalar(t[:, i, :], c.x[:, bass.ds(n, 1), :].rearrange("p a d -> p (a d)"),
                                                   c.mv[:, bass.ds(n, 1), 0:1].rearrange("p a d -> p (a d)"),
                                                   rstd[:, bass.ds(n, 1)], ALU.subtract, ALU.mult)
                last.then_inc(y_s, 1)
                dve.wait_ge(y_s, b + 1)
                xb = c.x[:, bass.ds(b * ST, ST), :].rearrange("p a d -> p (a d)")
                nc.vector.tensor_tensor(xb, xb, t[:].rearrange("p a d -> p (a d)"), ALU.add).then_inc(summed, 1)

            def chosen(ins, b, k):
                ins.then_inc(pick_s, 1)
                dve.wait_ge(pick_s, PICKS * b + k + 1)

            def take_logits(b):
                dve.wait_ge(gated, b + 1)
                chosen(nc.vector.tensor_copy(logits[:].rearrange("p i e -> p (i e)"), ps_m[:, 0:ST * E]), b, 0)

            def best(b, r):
                k = 1 + 6 * r
                chosen(nc.vector.tensor_reduce(top[:, r, :], logits[:], X, ALU.max), b, k)
                chosen(nc.vector.tensor_tensor(eq[:], logits[:], top[:, r, :].unsqueeze(2).broadcast_to([P, ST, E]),
                                               ALU.is_equal), b, k + 1)
                chosen(nc.vector.tensor_tensor(eq[:], eq[:], rev[:], ALU.mult), b, k + 2)
                chosen(nc.vector.tensor_reduce(pick[:], eq[:], X, ALU.max), b, k + 3)
                chosen(nc.vector.tensor_tensor(one[:, r], eq[:], pick[:].unsqueeze(2).broadcast_to([P, ST, E]),
                                               ALU.is_equal), b, k + 4)

            def strike_best(b):
                chosen(nc.vector.scalar_tensor_tensor(logits[:], one[:, 0], NEG_MIN, logits[:], ALU.mult, ALU.add), b, 6)

            def take_diff(b):
                chosen(nc.vector.tensor_tensor(diff[:], top[:, 1, :], top[:, 0, :], ALU.subtract), b, 12)

            def weigh(b):
                dve.wait_ge(ex_ready, b + 1)
                if late(b, 1):
                    dve.wait_ge(mixT_ps, b)
                nc.vector.tensor_scalar(wt[:, 0, :], ex[:], 1.0, None, ALU.add).then_inc(weighed, 1)
                dve.wait_ge(weighed, 5 * b + 1)
                nc.vector.reciprocal(wt[:, 0, :], wt[:, 0, :]).then_inc(weighed, 1)
                dve.wait_ge(weighed, 5 * b + 2)
                nc.vector.tensor_tensor(wt[:, 1, :], wt[:, 0, :], ex[:], ALU.mult).then_inc(weighed, 1)
                dve.wait_ge(weighed, 5 * b + 3)
                for r in range(2):
                    nc.vector.tensor_tensor(part[:, r], one[:, r], wt[:, r, :].unsqueeze(2).broadcast_to([P, ST, E]),
                                            ALU.mult).then_inc(weighed, 1)
                dve.wait_ge(weighed, 5 * b + 5)
                chosen(nc.vector.tensor_tensor(mix[:, :, 0:E], part[:, 0], part[:, 1], ALU.add), b, PICKS - 1)

            def take_mixT(b):
                dve.wait_ge(mixT_ps, b + 1)
                if late(b, 1):
                    dve.wait_ge(b2_ps, b)
                nc.vector.tensor_copy(mixT[:].rearrange("p i e -> p (i e)"), ps_c[:, 0:ST * P]).then_inc(mixT_ready, 1)

            def add_b2(b):
                dve.wait_ge(b2_ps, b + 1)
                dve.wait_ge(summed, SUMS * b + 7)
                xb = c.x[:, bass.ds(b * ST, ST), :].rearrange("p a d -> p (a d)")
                nc.vector.tensor_tensor(xb, xb, ps_m[:], ALU.add).then_inc(summed, 1)

            def rest_tT(b):
                dve.wait_ge(tT_round, b + 1)
                for dc in range(DC):
                    last = nc.vector.scalar_tensor_tensor(tT[1][:, dc, :], ps_m[:, dc * S:(dc + 1) * S], norm_w[:, dc:dc + 1],
                                                          tT[0][:, dc, :].bitcast(F32), ALU.mult, ALU.subtract)
                last.then_inc(tT_ready, 1)

            def new_stats(b):
                dve.wait_ge(summed, SUMS * b + SUMS)
                batch_stats(nc, dve, c, stats, b)

            def split_h(g, s, chunks):
                for f in chunks:
                    dve.wait_ge(h_act, FC * g + f + 1)
                    if late(g, 2) and f == 0:
                        dve.wait_ge(o_ps, 2 * g - 2)
                    nc.vector.tensor_copy(hT[0][:, s % 2, f, :], h[:, f, :]).then_inc(h_round, 1)
                    dve.wait_ge(h_round, FC * g + f + 1)
                    nc.vector.tensor_tensor(hT[1][:, s % 2, f, :], h[:, f, :], hT[0][:, s % 2, f, :].bitcast(F32),
                                            ALU.subtract).then_inc(h_ready, 1)

            def add_expert(g, s, b):
                for i in range(ST):
                    dve.wait_ge(o_ps, 2 * g + i + 1)
                    dve.wait_ge(summed, SUMS * b + (1, 2 + i, 4 + i, 8)[s] if s < 4 else SUMS * b + place(s - 1) + i)
                    xt = c.x[:, bass.ds(b * ST + i, 1), :].rearrange("p a d -> p (a d)")
                    nc.vector.scalar_tensor_tensor(xt, ps_o[i][:, 0:D], mix[:, i, s:s + 1], xt, ALU.mult, ALU.add).then_inc(summed, 1)

            def slot(b, s):
                now = lagged(b, s, 0, E)
                if s == 0 and late_batch(b):
                    take_logits(b)
                    best(b, 0)
                    strike_best(b)
                if now:
                    split_h(now[0], s, (0, 1))
                if s == 0 and late_batch(b):
                    best(b, 1)
                    take_diff(b)
                if s == 1:
                    weigh(b)
                if now:
                    split_h(now[0], s, (2, 3))
                    if not late(b, 1):
                        pieces.rest(nc, dve, 2 * s + 5, 2 * s + 7)
                if s == E - 1 and (not isinstance(b, int) or b + 1 < B):
                    rest_tT(b + 1)
                if at := lagged(b, s, 1, E):
                    if at[1] == 0:
                        add_y(at[2])
                    add_expert(*at)
                if s == 2:
                    take_mixT(b)
                if s == 3:
                    add_b2(b)
                if s == 4 and (not isinstance(b, int) or b + 1 < B):
                    normalise(b + 1)
                if late(b, 1) and s == 5:
                    new_stats(b - 1)

            normalise(0)
            c.wait_weights(dve, tag)
            rest_tT(0)
            pieces.rest(nc, dve, 0, 5)
            run_steps(dve, E, slot, LAST)
            new_stats(B - 1)

        @block.scalar
        def _(act):
            act.wait_ge(root, 3)
            nc.scalar.activation(rstd[:], c.mv[:, :, 1:2].rearrange("p a d -> p (a d)"), ACT.Sqrt, bias=c.eps[:]).then_inc(root, 1)
            act.wait_ge(root, 7)
            nc.scalar.activation(ms[:], ms[:], ACT.Sqrt, bias=rms_eps[:]).then_inc(root, 1)
            c.wait_weights(act, tag)

            def take_tT(b):
                act.wait_ge(tT_ps, b + 1)
                for dc in range(DC):
                    last = nc.scalar.mul(tT[0][:, dc, :], ps_m[:, dc * S:(dc + 1) * S], norm_w[:, dc:dc + 1])
                last.then_inc(tT_round, 1)

            def gelu(g, s):
                for f in range(FC):
                    act.wait_ge(h_ps, FC * g + f + 1)
                    if late(g, 1):
                        act.wait_ge(h_ready, FC * g + f - FC + 1)
                    nc.scalar.activation(h[:, f, :], ps_h[f][:, 0:S], ACT.Gelu,
                                         bias=b1[:, FC * s + f:FC * s + f + 1]).then_inc(h_act, 1)

            def slot(b, s):
                if at := lagged(b, s, 0, E):
                    gelu(at[0], at[1])
                    if not late(b, 1):
                        pieces.round(nc, act, 2 * s + 5, 2 * s + 7)
                if s == 0 and late_batch(b):
                    act.wait_ge(pick_s, PICKS * b + PICKS - 1)
                    if late(b, 1):
                        act.wait_ge(weighed, 5 * b)
                    nc.scalar.activation(ex[:], diff[:], ACT.Exp).then_inc(ex_ready, 1)
                if s == E - 1 and (not isinstance(b, int) or b + 1 < B):
                    take_tT(b + 1)

            take_tT(0)
            pieces.round(nc, act, 0, 5)
            run_steps(act, E, slot, LAST)


def small_heads(nc, c, tag, w_qk, w_v, load_next, softmax, bq=None, bk=None, bv=None, w_out=None):
    STEPS, J, HD, W = 4, 4, 16, 32
    V_LAG = 3 if softmax else 2
    B_LAG = V_LAG + 1
    LAST = B_LAG if softmax else B_LAG + 2
    SW = ST * S if softmax else 3 * P
    with ExitStack() as ctx:
        sb = lambda name, shape: ctx.enter_context(nc.sbuf_tensor(f"{tag}_{name}", shape, F32))
        ps = lambda name: ctx.enter_context(nc.psum_tensor(f"{tag}_{name}", [P, 512], F32))
        sem = lambda name: ctx.enter_context(nc.semaphore(f"{tag}_{name}"))
        rstd = sb("rstd", [P, TILES])
        xn = sb("xn", [P, ST, D])
        xnT = sb("xnT", [P, DC, S])
        v_all = sb("v_all", [P, ST, D])
        qk = sb("qk", [P, 2, 2, S])
        split = sb("split", [P, 2, J, S])
        vp = sb("vp", [P, STEPS, ST, J, W])
        wT = sb("wT", [P, 2, J, SW])
        zT = sb("zT", [P, 2, S])
        den = sb("den", [P, ST, J])
        inv = sb("inv", [P, ST, J])
        if softmax:
            ctx_stage = sb("ctx_stage", [P, DC, S])
            ctxT = sb("ctxT", [P, DC, S])
            nmx = sb("nmx", [P, J, ST])
            pr = sb("pr", [P, J, ST, S])
            o = sb("o", [P, ST, J, HD])
        else:
            low = sb("low", [P, 2 * S])
            keep = sb("keep", [P, 3 * P])
            o_all = sb("o_all", [P, ST, D])
            oT = sb("oT", [P, DC, S])
        ps_p = ps("ps_p")
        ps_s = [ps(f"ps_s{j}") for j in range(J)]
        ps_z = ps("ps_z")
        ps_t = [ps("ps_t0"), ps("ps_t1")]

        root = sem("root")
        xn_ready = sem("xn_ready")
        xnT_ps = sem("xnT_ps")
        xnT_ready = sem("xnT_ready")
        ctx_in = sem("ctx_in")
        ctx_ready = sem("ctx_ready")
        proj = sem("proj")
        v_ps = sem("v_ps")
        v_taken = sem("v_taken")
        qk_ready = sem("qk_ready")
        phi_s = sem("phi_s")
        filled = sem("filled")
        v_ready = sem("v_ready")
        keep_made = sem("keep_made")
        split_ready = sem("split_ready")
        scored = sem("scored")
        maxed = sem("maxed")
        exped = sem("exped")
        turned = sem("turned")
        w_even = sem("w_even")
        w_odd = sem("w_odd")
        z_done = sem("z_done")
        zT_ready = sem("zT_ready")
        backed = sem("backed")
        den_s = sem("den_s")
        o_ready = sem("o_ready")
        oT_ps = sem("oT_ps")
        oT_ready = sem("oT_ready")
        out_ps = sem("out_ps")
        added = sem("added")
        stats = sem("stats")

        block = ctx.enter_context(nc.Block())

        @block.sync
        def _(sp):
            if not softmax:
                load_next(sp)
            else:
                def batch(b):
                    if late(b, 1):
                        sp.wait_ge(ctx_ready, b)
                    sp.dma_start(ctx_stage[:], c.dram["ctxT"][:, bass.ds(b, 1), :, :].rearrange("p a c s -> p (a c) s")).then_inc(ctx_in, 16)
                def store_x(b):
                    sp.wait_ge(added, STEPS * b + STEPS)
                    sp.dma_start(c.mid[bass.ds(b, 1)].rearrange("b p i d -> p (b i) d"),
                                 c.x[:, bass.ds(b * ST, ST), :]).then_inc(c.mid_out, 16)
                batch(0)
                load_next(sp)
                batch(1)
                with sp.Fori(2, B) as b:
                    batch(b)
                    store_x(b - 2)
                store_x(B - 2)
                store_x(B - 1)
                sp.wait_ge(c.mid_out, 16 * B)

        if not softmax:
            @block.gpsimd
            def _(pool):
                nc.gpsimd.memset(keep[:], 1.0).then_inc(keep_made, 1)
                pool.wait_ge(keep_made, 1)
                for blk in (0, 2):
                    nc.gpsimd.affine_select(out=keep[:, blk * P:(blk + 1) * P], in_=keep[:, blk * P:(blk + 1) * P],
                                            compare_op=ALU.is_ge, fill=0.0, base=0, pattern=[[1, P]],
                                            channel_multiplier=-1).then_inc(keep_made, 1)
        else:
            @block.gpsimd
            def _(pool):
                def batch(b):
                    pool.wait_ge(ctx_in, 16 * b + 16)
                    if late(b, 1):
                        pool.wait_ge(proj, 2 * b)
                    pool.sem_inc(c.pool_waited, 1)
                    nc.gpsimd.tensor_copy(ctxT[:], ctx_stage[:]).then_inc(ctx_ready, 1)
                batch(0)
                with pool.Fori(1, B) as b:
                    batch(b)

        @block.tensor
        def _(pe):
            c.wait_weights(pe, tag)
            src = ctxT if softmax else xnT

            def turn_x(b):
                pe.wait_ge(xn_ready, b + 1)
                if late(b, 1):
                    pe.wait_ge(qk_ready, 2 * b)
                for dc in range(DC):
                    for i in range(ST):
                        last = nc.tensor.transpose(ps_p[:, dc * S + i * P:dc * S + (i + 1) * P],
                                                   xn[:, i, dc * P:(dc + 1) * P], c.ident[:])
                last.then_inc(xnT_ps, 1)

            def project(g, s, b):
                if s == 0:
                    pe.wait_ge(xnT_ready, b + 1)
                    if softmax:
                        pe.wait_ge(ctx_ready, b + 1)
                if s == 1:
                    pe.wait_ge(qk_ready, 2 * b + 1)
                    for i in range(ST):
                        for dc in range(DC):
                            last = nc.tensor.matmul(ps_p[:, i * D:(i + 1) * D], src[:, dc, i * P:(i + 1) * P],
                                                    w_v[:, dc, :], start=(dc == 0), stop=(dc == DC - 1))
                    last.then_inc(v_ps, 1)
                if s == 2:
                    pe.wait_ge(v_taken, b + 1)
                if s % 2 == 0:
                    for w in range(2):
                        for dc in range(DC):
                            last = nc.tensor.matmul(ps_p[:, w * S:(w + 1) * S], w_qk[:, s // 2, w, dc, :],
                                                    (xnT if w == 0 else src)[:, dc, :], start=(dc == 0), stop=(dc == DC - 1))
                    last.then_inc(proj, 1)

            def scores(g, s, j):
                if j == 0:
                    pe.wait_ge(split_ready, g + 1)
                if late(g, 1):
                    if softmax:
                        pe.wait_ge(exped, J * g + j - J + 1)
                    else:
                        pe.wait_ge((w_even, w_odd)[j % 2], 2 * g - 1 + j // 2)
                for i in range(ST):
                    if softmax:
                        last = nc.tensor.matmul(ps_s[j][:, i * S:(i + 1) * S], split[:, s % 2, j, i * P:(i + 1) * P],
                                                qk[:, s // 2, 1, :], start=True, stop=True)
                    else:
                        last = nc.tensor.matmul(ps_s[j][:, i * S:(i + 1) * S - i * P], split[:, s % 2, j, i * P:(i + 1) * P],
                                                qk[:, s // 2, 0, i * P:S], start=True, stop=True)
                last.then_inc(scored, 1)

            def turn(g, s, j):
                pe.wait_ge(exped, J * g + j + 1)
                if late(g, 1) or j >= 2:
                    pe.wait_ge((w_even, w_odd)[j % 2], 2 * g + j // 2)
                for i in range(ST):
                    for t in range(ST):
                        last = nc.tensor.transpose(ps_t[j % 2][:, t * S + i * P:t * S + (i + 1) * P],
                                                   pr[:, j, i, t * P:(t + 1) * P], c.ident[:])
                last.then_inc(turned, 1)

            def values(g, s):
                pe.wait_ge(v_ready, g + 1)
                pe.wait_ge(w_even, 2 * g + 2)
                pe.wait_ge(w_odd, 2 * g + 2)
                if late(g, 1):
                    pe.wait_ge(zT_ready, g)
                    pe.wait_ge(o_ready, g)
                for t in range(ST):
                    q0 = 0 if softmax else t * P
                    for j in range(J):
                        last = nc.tensor.matmul(ps_z[W * j:W * (j + 1), q0:S], vp[:, s, t, j, :],
                                                wT[:, s % 2, j, t * S:t * S + S - q0], start=(t == 0), stop=(t == ST - 1),
                                                tile_position=(0, W * j))
                last.then_inc(z_done, 1)

            def back(g, s):
                pe.wait_ge(zT_ready, g + 1)
                for i in range(ST):
                    last = nc.tensor.transpose(ps_z[:, S + i * P:S + (i + 1) * P], zT[:, s % 2, i * P:(i + 1) * P], c.ident[:])
                last.then_inc(backed, 1)

            def turn_o(b):
                pe.wait_ge(o_ready, STEPS * b + STEPS)
                if late(b, 1):
                    pe.wait_ge(added, b)
                for dc in range(DC):
                    for i in range(ST):
                        last = nc.tensor.transpose(ps_t[0][:, dc * S + i * P:dc * S + (i + 1) * P],
                                                   o_all[:, i, dc * P:(dc + 1) * P], c.ident[:])
                last.then_inc(oT_ps, 1)

            def output(b):
                pe.wait_ge(oT_ready, b + 1)
                for i in range(ST):
                    for dc in range(DC):
                        last = nc.tensor.matmul(ps_t[0][:, i * D:(i + 1) * D], oT[:, dc, i * P:(i + 1) * P],
                                                w_out[:, dc, :], start=(dc == 0), stop=(dc == DC - 1))
                last.then_inc(out_ps, 1)

            def slot(b, s):
                if s == STEPS - 1 and (not isinstance(b, int) or b + 1 < B):
                    turn_x(b + 1)
                if at := lagged(b, s, 0, STEPS):
                    project(*at)
                if at := lagged(b, s, B_LAG, STEPS):
                    back(at[0], at[1])
                if w_out is not None and (at := lagged(b, s, B_LAG + 1, STEPS)) and at[1] == STEPS - 1:
                    turn_o(at[2])
                for j in range(J):
                    if at := lagged(b, s, 1, STEPS):
                        scores(at[0], at[1], j)
                    if softmax and (at := lagged(b, s, 2, STEPS)):
                        turn(at[0], at[1], j)
                if at := lagged(b, s, V_LAG, STEPS):
                    values(at[0], at[1])
                if w_out is not None:
                    if (at := lagged(b, s, B_LAG + 2, STEPS)) and at[1] == STEPS - 1:
                        output(at[2])

            turn_x(0)
            run_steps(pe, STEPS, slot, LAST)

        @block.vector
        def _(dve):
            nc.vector.memset(vp[:], 0.0).then_inc(filled, 1)
            dve.wait_ge(filled, 1)
            nc.vector.memset(vp[:, :, :, :, HD:HD + 1], 1.0).then_inc(filled, 1)
            dve.wait_ge(root, 1)
            nc.vector.reciprocal(rstd[:], rstd[:]).then_inc(root, 1)
            dve.wait_ge(root, 2)
            dve.wait_ge(filled, 2)
            if not softmax:
                dve.wait_ge(keep_made, 3)
            c.wait_weights(dve, tag)

            def normalise(b):
                if late(b, 1):
                    dve.wait_ge(xnT_ps, b)
                for i in range(ST):
                    n = b * ST + i
                    last = nc.vector.tensor_scalar(xn[:, i, :], c.x[:, bass.ds(n, 1), :].rearrange("p a d -> p (a d)"),
                                                   c.mv[:, bass.ds(n, 1), 0:1].rearrange("p a d -> p (a d)"),
                                                   rstd[:, bass.ds(n, 1)], ALU.subtract, ALU.mult)
                last.then_inc(xn_ready, 1)

            def low_part(g, s, b):
                n = 2 * b + s // 2
                dve.wait_ge(proj, n + 1)
                if late(g, 1):
                    dve.wait_ge(qk_ready, n)
                nc.vector.tensor_scalar(low[:], ps_p[:], 0.0, None, ALU.min).then_inc(phi_s, 1)

            def features(g, s, b):
                n = 2 * b + s // 2
                dve.wait_ge(phi_s, 2 * n + 2)
                if late(g, STEPS):
                    dve.wait_ge(scored, J * g - 2 * J)
                nc.vector.scalar_tensor_tensor(qk[:, s // 2].rearrange("p w s -> p (w s)"), ps_p[:], 0.0, low[:],
                                               ALU.max, ALU.add).then_inc(qk_ready, 1)

            def fill_v(g, s, b):
                dve.wait_ge(v_taken, b + 1)
                if late(g, STEPS):
                    dve.wait_ge(z_done, g - STEPS + 1)
                for i in range(ST):
                    got = v_all[:, i, s * J * HD:(s + 1) * J * HD].rearrange("p (j e) -> p j e", j=J)
                    if bv is not None:
                        last = nc.vector.tensor_tensor(vp[:, s, i, :, 0:HD], got,
                                                       bv[:, s * J * HD:(s + 1) * J * HD].rearrange("p (j e) -> p j e", j=J), ALU.add)
                    else:
                        last = nc.vector.tensor_copy(vp[:, s, i, :, 0:HD], got)
                last.then_inc(v_ready, 1)

            def apart(g, s, b):
                dve.wait_ge(qk_ready, 2 * b + s // 2 + 1)
                if late(g, 2):
                    dve.wait_ge(scored, J * g - J)
                for j in range(J):
                    m = J * (s % 2) + j
                    last = nc.vector.tensor_scalar(split[:, s % 2, j, :], qk[:, s // 2, 0, :], c.head16[:, m:m + 1], None, ALU.mult)
                last.then_inc(split_ready, 1)

            def row_max(g, s, j):
                dve.wait_ge(scored, J * g + j + 1)
                if late(g, 1):
                    dve.wait_ge(exped, J * g + j - J + 1)
                nc.vector.tensor_reduce(nmx[:, j, :], ps_s[j][:].rearrange("p (i s) -> p i s", i=ST), X, ALU.max,
                                        negate=True).then_inc(maxed, 1)

            def take_odd(g, s, j):
                dve.wait_ge(turned, J * g + j + 1)
                if late(g, 2):
                    dve.wait_ge(z_done, g - 1)
                nc.vector.tensor_copy(wT[:, s % 2, j, :], ps_t[1][:]).then_inc(w_odd, 1)

            def keep_past(g, s, j):
                dve.wait_ge(scored, J * g + j + 1)
                if late(g, 2):
                    dve.wait_ge(z_done, g - 1)
                nc.vector.tensor_tensor(wT[:, s % 2, j, :], ps_s[j][:, 0:SW], keep[:], ALU.mult).then_inc((w_even, w_odd)[j % 2], 1)

            def finish(g, s, b):
                z = ps_z[:, S:2 * S].rearrange("p (i j w) -> p i j w", i=ST, j=J)
                dve.wait_ge(backed, g + 1)
                nc.vector.tensor_scalar(den[:], z[:, :, :, HD:HD + 1].rearrange("p i j w -> p i (j w)"), 1e-6, None,
                                        ALU.max).then_inc(den_s, 1)
                dve.wait_ge(den_s, 2 * g + 1)
                nc.vector.reciprocal(inv[:], den[:]).then_inc(den_s, 1)
                dve.wait_ge(den_s, 2 * g + 2)
                if softmax:
                    if late(g, 1):
                        dve.wait_ge(added, g)
                    dst = o[:]
                else:
                    if s == 0 and late(g, STEPS):
                        dve.wait_ge(oT_ps, b)
                    dst = o_all[:, :, s * J * HD:(s + 1) * J * HD].rearrange("p i (j e) -> p i j e", j=J)
                for i in range(ST):
                    last = nc.vector.tensor_tensor(dst[:, i], z[:, i, :, 0:HD],
                                                   inv[:, i, :].unsqueeze(2).broadcast_to([P, J, HD]), ALU.mult)
                last.then_inc(o_ready, 1)
                if softmax:
                    dve.wait_ge(o_ready, g + 1)
                    xs = c.x[:, bass.ds(b * ST, ST), s * J * HD:(s + 1) * J * HD]
                    nc.vector.tensor_tensor(xs, xs, o[:].rearrange("p i j e -> p i (j e)"), ALU.add).then_inc(added, 1)

            def add_output(b):
                dve.wait_ge(out_ps, b + 1)
                xb = c.x[:, bass.ds(b * ST, ST), :].rearrange("p a d -> p (a d)")
                nc.vector.tensor_tensor(xb, xb, ps_t[0][:], ALU.add).then_inc(added, 1)

            def new_stats(b):
                dve.wait_ge(added, STEPS * b + STEPS if softmax else b + 1)
                batch_stats(nc, dve, c, stats, b)

            def slot(b, s):
                now, one = lagged(b, s, 0, STEPS), lagged(b, s, 1, STEPS)
                if one:
                    fill_v(*one)
                if not softmax and now and s % 2 == 0:
                    low_part(*now)
                ended = lagged(b, s, B_LAG, STEPS)
                if ended and not softmax:
                    finish(*ended)
                for j in range(J):
                    if one:
                        if softmax:
                            row_max(one[0], one[1], j)
                        else:
                            keep_past(one[0], one[1], j)
                    if ended and softmax and j == 0:
                        finish(*ended)
                    if not softmax and now and s % 2 == 0 and j == 0:
                        features(*now)
                    if softmax and j % 2 and (at := lagged(b, s, 2, STEPS)):
                        take_odd(at[0], at[1], j)
                if softmax and now:
                    apart(*now)
                if ended and softmax and ended[1] == STEPS - 1:
                    new_stats(ended[2])
                if w_out is not None and late(b, 2):
                    if s == 1:
                        add_output(b - 2)
                    if s == 3:
                        new_stats(b - 2)
                if s == 1 and (not isinstance(b, int) or b + 1 < B):
                    normalise(b + 1)

            normalise(0)
            run_steps(dve, STEPS, slot, LAST)
            if w_out is not None:
                add_output(B - 1)
                new_stats(B - 1)

        @block.scalar
        def _(act):
            nc.scalar.activation(rstd[:], c.mv[:, :, 1:2].rearrange("p a d -> p (a d)"), ACT.Sqrt,
                                 bias=c.eps[:]).then_inc(root, 1)
            c.wait_weights(act, tag)

            def take_xT(b):
                act.wait_ge(xnT_ps, b + 1)
                nc.scalar.copy(xnT[:].rearrange("p c s -> p (c s)"), ps_p[:]).then_inc(xnT_ready, 1)

            def take_qk(g, s, b):
                if s % 2:
                    return
                n = 2 * b + s // 2
                if softmax:
                    act.wait_ge(proj, n + 1)
                    if late(g, STEPS):
                        act.wait_ge(scored, J * g - 2 * J)
                    for w, bias in enumerate((bq, bk)):
                        last = nc.scalar.activation(qk[:, s // 2, w, :], ps_p[:, w * S:(w + 1) * S], ACT.Identity,
                                                    bias=bias[:, s // 2:s // 2 + 1])
                    last.then_inc(qk_ready, 1)
                else:
                    act.wait_ge(phi_s, 2 * n + 1)
                    nc.scalar.activation(low[:], low[:], ACT.Exp).then_inc(phi_s, 1)

            def apart(g, s, b):
                act.wait_ge(qk_ready, 2 * b + s // 2 + 1)
                if late(g, 2):
                    act.wait_ge(scored, J * g - J)
                for j in range(J):
                    m = J * (s % 2) + j
                    last = nc.scalar.mul(split[:, s % 2, j, :], qk[:, s // 2, 1, :], c.head16k[:, m:m + 1])
                last.then_inc(split_ready, 1)

            def take_v(b):
                act.wait_ge(v_ps, b + 1)
                if late(b, 1):
                    act.wait_ge(v_ready, STEPS * b)
                nc.scalar.copy(v_all[:].rearrange("p i d -> p (i d)"), ps_p[:]).then_inc(v_taken, 1)

            def exponentials(g, s, j):
                act.wait_ge(maxed, J * g + j + 1)
                if late(g, 1):
                    act.wait_ge(turned, J * g + j - J + 1)
                for i in range(ST):
                    last = nc.scalar.activation(pr[:, j, i, :], ps_s[j][:, i * S:(i + 1) * S], ACT.Exp, bias=nmx[:, j, i:i + 1])
                last.then_inc(exped, 1)

            def take_even(g, s, j):
                act.wait_ge(turned, J * g + j + 1)
                if late(g, 2):
                    act.wait_ge(z_done, g - 1)
                nc.scalar.copy(wT[:, s % 2, j, :], ps_t[0][:]).then_inc(w_even, 1)

            def take_z(g, s):
                act.wait_ge(z_done, g + 1)
                if late(g, 2):
                    act.wait_ge(backed, g - 1)
                nc.scalar.copy(zT[:, s % 2, :], ps_z[:, 0:S]).then_inc(zT_ready, 1)

            def slot(b, s):
                now, one, two = (lagged(b, s, d, STEPS) for d in range(3))
                if s == STEPS - 1 and (not isinstance(b, int) or b + 1 < B):
                    take_xT(b + 1)
                if now:
                    take_qk(*now)
                    if s == 1:
                        take_v(b)
                if softmax:
                    for j in range(J):
                        if j % 2 == 0 and two:
                            take_even(two[0], two[1], j)
                        if one:
                            exponentials(one[0], one[1], j)
                if at := lagged(b, s, V_LAG, STEPS):
                    take_z(at[0], at[1])
                if not softmax and now:
                    apart(*now)
                if w_out is not None and (at := lagged(b, s, B_LAG + 1, STEPS)) and at[1] == STEPS - 1:
                    act.wait_ge(oT_ps, at[2] + 1)
                    if late(at[2], 1):
                        act.wait_ge(out_ps, at[2])
                    nc.scalar.copy(oT[:].rearrange("p c s -> p (c s)"), ps_t[0][:]).then_inc(oT_ready, 1)

            take_xT(0)
            run_steps(act, STEPS, slot, LAST)


def gated_heads(nc, c, tag, pieces, w_qk, w_gate, w_val, w_out, load_own):
    STEPS, E, HEADS, LAST = 4, 8, 8, 5
    K = 4
    AHEAD = 3
    with ExitStack() as ctx:
        sb = lambda name, shape, dt=F32: ctx.enter_context(nc.sbuf_tensor(f"{tag}_{name}", shape, dt))
        ps = lambda name: ctx.enter_context(nc.psum_tensor(f"{tag}_{name}", [P, 512], F32))
        sem = lambda name: ctx.enter_context(nc.semaphore(f"{tag}_{name}"))
        rstd = sb("rstd", [P, TILES])
        xn = sb("xn", [P, ST, D])
        xnT = sb("xnT", [P, DC, S])
        xs = [sb(f"xs{n}", [P, DC, S], F32R) for n in range(2)]
        rev = sb("rev", [P, ST * HEADS, E])
        gate = sb("gate", [P, ST * HEADS, E])
        eq = sb("eq", [P, ST * HEADS, E])
        best = sb("best", [P, ST * HEADS])
        gm = sb("gm", [P, ST * HEADS, E])
        gm_step = sb("gm_step", [P, STEPS, ST, 2, E])
        gm_late = sb("gm_late", [P, STEPS, ST, 2, E])
        qT = sb("qT", [P, 2, 2, S])
        kT = sb("kT", [P, 2, S])
        gv = sb("gv", [P, 2, E, 64])
        v = sb("v", [P, STEPS, ST, P])
        keys = lambda i: slice(i * P, i * P + (i + 1) * P)
        sm = sb("sm", [P, 2, 3 * P])
        nmx = sb("nmx", [P, 2, ST])
        pr = sb("pr", [P, 4, 3 * P])
        sums = sb("sums", [P, 4, ST])
        inv = sb("inv", [P, 4, ST])
        prT = sb("prT", [P, 4, 3 * P])
        zT = sb("zT", [P, 2, S])
        z = sb("z", [P, ST, P])
        zg = sb("zg", [P, 2, E, 64])
        zgT = [sb(f"zgT{n}", [P, 2, 4, P], F32R) for n in range(2)]
        x_sum = sb("x_sum", [P, ST, D])
        ps_qk, ps_s, ps_t, ps_g, ps_z, ps_out = (ps(n) for n in ("ps_qk", "ps_s", "ps_t", "ps_g", "ps_z", "ps_out"))
        ps_v = [ps("ps_v0"), ps("ps_v1")]

        root = sem("root")
        xn_ready = sem("xn_ready")
        xnT_ps = sem("xnT_ps")
        xnT_ready = sem("xnT_ready")
        xs_round = sem("xs_round")
        xs_ready = sem("xs_ready")
        gate_ps = sem("gate_ps")
        gate_exp = sem("gate_exp")
        pick_s = sem("pick_s")
        piece = sem("piece")
        kept = sem("kept")
        proj = sem("proj")
        q_ready = sem("q_ready")
        v_ps = sem("v_ps")
        v_gated = sem("v_gated")
        v_ready = sem("v_ready")
        scored = sem("scored")
        maxed = sem("maxed")
        exped = sem("exped")
        inverted = sem("inverted")
        normed = sem("normed")
        turned = sem("turned")
        prT_ready = sem("prT_ready")
        z_done = sem("z_done")
        zT_ready = sem("zT_ready")
        backed = sem("backed")
        z_ready = sem("z_ready")
        zg_ready = sem("zg_ready")
        zg_ps = sem("zg_ps")
        zgT_round = sem("zgT_round")
        zgT_ready = sem("zgT_ready")
        out_ps = sem("out_ps")
        x_in = sem("x_in")
        sum_in = sem("sum_in")
        added = sem("added")
        stored = sem("stored")
        PICKS = 8

        block = ctx.enter_context(nc.Block())

        @block.sync
        def _(sp):
            mid = lambda b: c.mid[bass.ds(b, 1)].rearrange("b p i d -> p (b i) d")

            def load_xn(b):
                if late(b, 1):
                    sp.wait_ge(xnT_ps, b)
                sp.dma_start(xn[:], mid(b)).then_inc(x_in, 16)

            def load_sum(b):
                if late(b, 1):
                    sp.wait_ge(stored, 16 * b)
                sp.dma_start(x_sum[:], mid(b)).then_inc(sum_in, 16)

            def store(b):
                sp.wait_ge(added, b + 1)
                sp.dma_start(c.out[:, bass.ds(b * ST, ST), :], x_sum[:]).then_inc(stored, 16)

            load_xn(0)
            load_own(sp)
            load_sum(0)
            pieces.load(sp, Pieces.STAGES, 7)
            load_xn(1)
            pieces.load(sp, 7, 12)
            load_xn(2)
            pieces.load(sp, 12, len(pieces.list))
            with sp.Fori(2, B - 1) as b:
                load_xn(b + 1)
                store(b - 2)
                load_sum(b - 1)
            for b in range(B - 3, B - 1):
                store(b)
                load_sum(b + 1)
            store(B - 1)
            sp.wait_ge(stored, 16 * B)

        @block.gpsimd
        def _(pool):
            nc.gpsimd.iota(rev[:], pattern=[[0, ST * HEADS], [-1, E]], base=E, channel_multiplier=0,
                           allow_small_or_imprecise_dtypes=True).then_inc(root, 1)

        @block.tensor
        def _(pe):
            c.wait_weights(pe, tag)

            def turn_x(b):
                pe.wait_ge(xn_ready, b + 1)
                if late(b, 1):
                    pe.wait_ge(q_ready, STEPS * b)
                for dc in range(DC):
                    for i in range(ST):
                        last = nc.tensor.transpose(ps_qk[:, dc * S + i * P:dc * S + (i + 1) * P],
                                                   xn[:, i, dc * P:(dc + 1) * P], c.ident[:])
                last.then_inc(xnT_ps, 1)

            def gates(b):
                pe.wait_ge(xnT_ready, b + 1)
                if late(b, 2):
                    pe.wait_ge(zgT_ready, K * (STEPS * b - LAST))
                for i in range(ST):
                    for dc in range(DC):
                        last = nc.tensor.matmul(ps_g[:, i * E * HEADS:(i + 1) * E * HEADS], xnT[:, dc, i * P:(i + 1) * P],
                                                w_gate[:, dc, :], start=(dc == 0), stop=(dc == DC - 1))
                last.then_inc(gate_ps, 1)

            def project(g, s):
                if late(g, 1):
                    pe.wait_ge(q_ready, g)
                for w in range(2):
                    for dc in range(DC):
                        last = nc.tensor.matmul(ps_qk[:, w * S:(w + 1) * S], w_qk[:, s, w, dc, :], xnT[:, dc, :],
                                                start=(dc == 0), stop=(dc == DC - 1))
                last.then_inc(proj, 1)

            def project_v(g, s, k, b):
                j, i = k // 2, k % 2
                if s == 0 and k == 0:
                    pe.wait_ge(xs_ready, b + 1)
                if late(g, 1) or k >= 2:
                    pe.wait_ge(v_gated, K * g + k - 1)
                if not late(b, 1) and i == 0:
                    pe.wait_ge(pieces.split, 2 * s + j + 1)
                for dc in range(DC):
                    last = product3(nc, ps_v[i][:], [t[:, dc, i * P:(i + 1) * P] for t in xs],
                                    [t[:, 2 * s + j, dc, :] for t in w_val], dc == 0, dc == DC - 1)
                last.then_inc(v_ps, 1)

            def scores(g, s, j):
                pe.wait_ge(q_ready, g + 1)
                if late(g, 1) or j:
                    pe.wait_ge(maxed, 2 * g + j)
                for i in range(ST):
                    last = nc.tensor.matmul(ps_s[:, i * S:i * S + (i + 1) * P], qT[:, s % 2, j, i * P:(i + 1) * P],
                                            kT[:, s % 2, 0:(i + 1) * P], start=True, stop=True)
                last.then_inc(scored, 1)

            def turn(g, s, j):
                pe.wait_ge(normed, 2 * g + j + 1)
                if late(g, 1) or j:
                    pe.wait_ge(prT_ready, 2 * g + j)
                for i in range(ST):
                    for t in range(i + 1):
                        last = nc.tensor.transpose(ps_t[:, t * S + i * P:t * S + (i + 1) * P],
                                                   pr[:, 2 * (s % 2) + j, (i + t) * P:(i + t + 1) * P], c.ident[:])
                last.then_inc(turned, 1)

            def values(g, s):
                pe.wait_ge(v_ready, K * g + K)
                pe.wait_ge(prT_ready, 2 * g + 2)
                if late(g, 1):
                    pe.wait_ge(zT_ready, g)
                    pe.wait_ge(z_ready, g)
                for t in range(ST):
                    for j in range(2):
                        last = nc.tensor.matmul(ps_z[64 * j:64 * j + 64, t * P:S], v[:, s, t, 64 * j:64 * j + 64],
                                                prT[:, 2 * (s % 2) + j, t * S:t * S + S - t * P], start=(t == 0), stop=(t == ST - 1))
                last.then_inc(z_done, 1)

            def back(g, s):
                pe.wait_ge(zT_ready, g + 1)
                for i in range(ST):
                    last = nc.tensor.transpose(ps_z[:, S + i * P:S + (i + 1) * P], zT[:, s % 2, i * P:(i + 1) * P], c.ident[:])
                last.then_inc(backed, 1)

            def turn_zg(g, s, k, batches):
                pe.wait_ge(zg_ready, K * g + k + 1)
                if late(g, 1) or k:
                    pe.wait_ge(zgT_ready, K * g + k)
                if s == STEPS - LAST % STEPS and k == 0:
                    pe.wait_ge(gate_exp, batches)
                for p in range(E // 2):
                    last = nc.tensor.transpose(ps_g[:, p * P:(p + 1) * P],
                                               zg[:, k % 2, 2 * p:2 * p + 2, :].rearrange("p e k -> p (e k)"), c.ident[:])
                last.then_inc(zg_ps, 1)

            def output(g, s, k, b):
                j, i = k // 2, k % 2
                pe.wait_ge(zgT_ready, K * g + k + 1)
                if s == 0 and k == 0 and late(g, STEPS):
                    pe.wait_ge(added, b)
                if not late(b, 1) and i == 0:
                    pe.wait_ge(pieces.split, HEADS + 2 * s + j + 1)
                for p in range(E // 2):
                    last = product3(nc, ps_out[:, i * D:(i + 1) * D], [t[:, k % 2, p, :] for t in zgT],
                                    [t[:, 2 * s + j, p, :] for t in w_out], s == 0 and k == 0 and p == 0,
                                    s == STEPS - 1 and j == 1 and p == E // 2 - 1, skip_group_check=True)
                last.then_inc(out_ps, 1)

            def slot(b, s):
                now, one, two = (lagged(b, s, d, STEPS) for d in range(3))
                five = lagged(b, s, 5, STEPS)
                if now:
                    if s == 0:
                        gates(b)
                    project(now[0], s)
                if at := lagged(b, s, 4, STEPS):
                    back(at[0], at[1])
                for k in range(K):
                    if now:
                        project_v(now[0], s, k, b)
                    if k % 2 == 0 and one:
                        scores(one[0], one[1], k // 2)
                    if k % 2 and two:
                        turn(two[0], two[1], k // 2)
                    if five:
                        turn_zg(five[0], five[1], k, b + 1 if now else B)
                        if k:
                            output(five[0], five[1], k - 1, five[2])
                if s == STEPS - 1 and (not isinstance(b, int) or b + 1 < B):
                    turn_x(b + 1)
                if at := lagged(b, s, 3, STEPS):
                    values(at[0], at[1])
                if five:
                    output(five[0], five[1], K - 1, five[2])

            turn_x(0)
            run_steps(pe, STEPS, slot, LAST)

        @block.vector
        def _(dve):
            dve.wait_ge(root, 2)
            nc.vector.reciprocal(rstd[:], rstd[:]).then_inc(root, 1)
            dve.wait_ge(root, 3)

            def normalise(b):
                dve.wait_ge(x_in, 16 * b + 16)
                for i in range(ST):
                    n = b * ST + i
                    last = nc.vector.tensor_scalar(xn[:, i, :], xn[:, i, :],
                                                   c.mv[:, bass.ds(n, 1), 0:1].rearrange("p a d -> p (a d)"),
                                                   rstd[:, bass.ds(n, 1)], ALU.subtract, ALU.mult)
                last.then_inc(xn_ready, 1)

            def rest_x(b):
                dve.wait_ge(xs_round, b + 1)
                nc.vector.tensor_tensor(xs[1][:], xnT[:], xs[0][:].bitcast(F32), ALU.subtract).then_inc(xs_ready, 1)

            def choose(b):
                k = 0

                def done(ins):
                    nonlocal k
                    k += 1
                    ins.then_inc(pick_s, 1)
                    dve.wait_ge(pick_s, PICKS * b + k)

                wide = lambda a: a[:].unsqueeze(2).broadcast_to([P, ST * HEADS, E])
                dve.wait_ge(gate_exp, b + 1)
                done(nc.vector.tensor_scalar(gate[:], gate[:], 1.0, None, ALU.add))
                done(nc.vector.reciprocal(gate[:], gate[:]))
                done(nc.vector.tensor_reduce(best[:], gate[:], X, ALU.max))
                done(nc.vector.tensor_tensor(eq[:], gate[:], wide(best), ALU.is_equal))
                done(nc.vector.tensor_tensor(eq[:], eq[:], rev[:], ALU.mult))
                done(nc.vector.tensor_reduce(best[:], eq[:], X, ALU.max))
                done(nc.vector.tensor_tensor(eq[:], eq[:], wide(best), ALU.is_equal))
                if late(b, 1):
                    dve.wait_ge(piece, STEPS * b)
                done(nc.vector.tensor_tensor(gm[:], eq[:], gate[:], ALU.mult))

            def cut_piece(g, s):
                if late(g, STEPS):
                    dve.wait_ge(kept, g - STEPS + 1)
                nc.vector.tensor_scalar(gm_step[:, s], gm[:].rearrange("p (i h) e -> p i h e", i=ST)[:, :, 2 * s:2 * s + 2, :],
                                        1.0, None, ALU.mult).then_inc(piece, 1)
                dve.wait_ge(piece, g + 1)

            def keep_piece(g, s):
                if late(g, STEPS):
                    dve.wait_ge(zg_ready, K * (g - STEPS + 1))
                nc.vector.tensor_copy(gm_late[:, s], gm_step[:, s]).then_inc(kept, 1)

            def gate_v(g, s, k):
                j, i = k // 2, k % 2
                dve.wait_ge(v_ps, K * g + k + 1)
                if late(g, 1) or k >= 2:
                    dve.wait_ge(v_ready, K * g + k - 1)
                nc.vector.tensor_tensor(gv[:, k % 2], ps_v[i][:].rearrange("p (e k) -> p e k", e=E),
                                        gm_step[:, s, i, j, :].unsqueeze(2).broadcast_to([P, E, 64]), ALU.mult).then_inc(v_gated, 1)

            def sum_v(g, s, k):
                j, i = k // 2, k % 2
                dve.wait_ge(v_gated, K * g + k + 1)
                if late(g, STEPS):
                    dve.wait_ge(z_done, g - STEPS + 1)
                nc.vector.tensor_reduce(v[:, s, i, 64 * j:64 * j + 64], gv[:, k % 2].rearrange("p e k -> p k e"), X,
                                        ALU.add).then_inc(v_ready, 1)

            def row_max(g, s, j):
                dve.wait_ge(scored, 2 * g + j + 1)
                if late(g, 1):
                    dve.wait_ge(exped, 2 * g + j - 1)
                dve.sem_inc(c.waited, 1)
                for i in range(ST):
                    n = (i + 1) * P
                    add = c.causal_min[:, (ST - 1 - i) * P:(ST - 1 - i) * P + n]
                    last = nc.vector.tensor_tensor_reduce(sm[:, j, keys(i)], ps_s[:, i * S:i * S + n], add, -1.0,
                                                          3.0e38, ALU.add, ALU.min, nmx[:, j, i:i + 1])
                last.then_inc(maxed, 1)

            def norm(g, s, j):
                r = 2 * (s % 2) + j
                dve.wait_ge(exped, 2 * g + j + 1)
                nc.vector.reciprocal(inv[:, r, :], sums[:, r, :]).then_inc(inverted, 1)
                dve.wait_ge(inverted, 2 * g + j + 1)
                for i in range(ST):
                    n = (i + 1) * P
                    last = nc.vector.tensor_scalar(pr[:, r, keys(i)], pr[:, r, keys(i)], inv[:, r, i:i + 1], None, ALU.mult)
                last.then_inc(normed, 1)

            def take_z(g):
                dve.wait_ge(backed, g + 1)
                if late(g, 1):
                    dve.wait_ge(zg_ready, K * g)
                nc.vector.tensor_copy(z[:].rearrange("p i m -> p (i m)"), ps_z[:, S:2 * S]).then_inc(z_ready, 1)

            def gate_z(g, s, k):
                j, i = k // 2, k % 2
                dve.wait_ge(z_ready, g + 1)
                dve.wait_ge(kept, g + 1)
                if late(g, 1) or k >= 2:
                    dve.wait_ge(zg_ps, K * g + k - 1)
                nc.vector.tensor_tensor(zg[:, k % 2], z[:, i, 64 * j:64 * j + 64].unsqueeze(1).broadcast_to([P, E, 64]),
                                        gm_late[:, s, i, j, :].unsqueeze(2).broadcast_to([P, E, 64]), ALU.mult).then_inc(zg_ready, 1)

            def add_to_x(b):
                dve.wait_ge(out_ps, K * STEPS * (b + 1))
                dve.wait_ge(sum_in, 16 * b + 16)
                xb = x_sum[:].rearrange("p a d -> p (a d)")
                nc.vector.tensor_tensor(xb, xb, ps_out[:], ALU.add).then_inc(added, 1)

            def rest_zgT(g, k):
                dve.wait_ge(zgT_round, K * g + k + 1)
                flat = lambda t: t[:, k % 2].rearrange("p e s -> p (e s)")
                nc.vector.tensor_tensor(flat(zgT[1]), ps_g[:], flat(zgT[0]).bitcast(F32), ALU.subtract).then_inc(zgT_ready, 1)

            def slot(b, s):
                now, one, five = (lagged(b, s, d, STEPS) for d in (0, 1, 5))
                if five:
                    gate_z(five[0], five[1], 0)
                    gate_z(five[0], five[1], 1)
                if now and s == 0:
                    choose(b)
                for k in range(K):
                    if five and 0 < k < K - 1:
                        gate_z(five[0], five[1], k + 1)
                    if k == K - 1 and (at := lagged(b, s, 4, STEPS)):
                        take_z(at[0])
                    if now:
                        if k == 0:
                            cut_piece(now[0], s)
                        gate_v(now[0], s, k)
                    if one and k % 2 == 0:
                        row_max(one[0], one[1], k // 2)
                    if five:
                        rest_zgT(five[0], k)
                    if now:
                        sum_v(now[0], s, k)
                    if one and k % 2:
                        norm(one[0], one[1], k // 2)
                if at := lagged(b, s, 3, STEPS):
                    keep_piece(at[0], at[1])
                if five and five[1] == STEPS - 1:
                    add_to_x(five[2])
                if s == 1 and (not isinstance(b, int) or b + 1 < B):
                    normalise(b + 1)
                if s == STEPS - 1 and (not isinstance(b, int) or b + 1 < B):
                    rest_x(b + 1)
                if not late(b, 2):
                    n = 2 * (STEPS * b + s) + AHEAD
                    pieces.rest(nc, dve, n, n + 2)

            normalise(0)
            rest_x(0)
            pieces.rest(nc, dve, 0, AHEAD)
            run_steps(dve, STEPS, slot, LAST)

        @block.scalar
        def _(act):
            act.wait_ge(root, 1)
            nc.scalar.activation(rstd[:], c.mv[:, :, 1:2].rearrange("p a d -> p (a d)"), ACT.Sqrt,
                                 bias=c.eps[:]).then_inc(root, 1)

            def take_xT(b):
                act.wait_ge(xnT_ps, b + 1)
                nc.scalar.copy(xnT[:].rearrange("p c s -> p (c s)"), ps_qk[:]).then_inc(xnT_ready, 1)
                act.wait_ge(xnT_ready, b + 1)
                nc.scalar.copy(xs[0][:], xnT[:]).then_inc(xs_round, 1)

            def take_gates(b):
                act.wait_ge(gate_ps, b + 1)
                if late(b, 1):
                    act.wait_ge(pick_s, PICKS * b)
                nc.scalar.activation(gate[:].rearrange("p h e -> p (h e)"), ps_g[:, 0:ST * HEADS * E], ACT.Exp,
                                     scale=-1.0).then_inc(gate_exp, 1)

            def take_qk(g, s):
                act.wait_ge(proj, g + 1)
                if late(g, 2):
                    act.wait_ge(scored, 2 * g - 2)
                for j in range(2):
                    nc.scalar.mul(qT[:, s % 2, j, :], ps_qk[:, 0:S], c.half[:, j:j + 1])
                nc.scalar.copy(kT[:, s % 2, :], ps_qk[:, S:2 * S]).then_inc(q_ready, 1)

            def exponentials(g, s, j):
                r = 2 * (s % 2) + j
                act.wait_ge(maxed, 2 * g + j + 1)
                if late(g, 2):
                    act.wait_ge(turned, 2 * g + j - 3)
                for i in range(ST):
                    n = (i + 1) * P
                    last = nc.scalar.activation(pr[:, r, keys(i)], sm[:, j, keys(i)], ACT.Exp, bias=nmx[:, j, i:i + 1], scale=-1.0,
                                                accum_out=sums[:, r, i:i + 1])
                last.then_inc(exped, 1)

            def take_prT(g, s, j):
                r = 2 * (s % 2) + j
                act.wait_ge(turned, 2 * g + j + 1)
                if late(g, 2):
                    act.wait_ge(z_done, g - 1)
                nc.scalar.copy(prT[:, r, 0:S], ps_t[:, 0:S])
                nc.scalar.copy(prT[:, r, S:S + P], ps_t[:, S + P:2 * S]).then_inc(prT_ready, 1)

            def take_zT(g, s):
                act.wait_ge(z_done, g + 1)
                if late(g, 2):
                    act.wait_ge(backed, g - 1)
                nc.scalar.copy(zT[:, s % 2, :], ps_z[:, 0:S]).then_inc(zT_ready, 1)

            def take_zgT(g, k):
                act.wait_ge(zg_ps, K * g + k + 1)
                if late(g, 1) or k >= 2:
                    act.wait_ge(out_ps, K * g + k - 1)
                nc.scalar.copy(zgT[0][:, k % 2].rearrange("p e s -> p (e s)"), ps_g[:]).then_inc(zgT_round, 1)

            def slot(b, s):
                now, one, two, five = (lagged(b, s, d, STEPS) for d in (0, 1, 2, 5))
                if now:
                    if s == 0:
                        take_gates(b)
                    take_qk(now[0], s)
                for k in range(K):
                    if two and k % 2:
                        take_prT(two[0], two[1], k // 2)
                    if five:
                        take_zgT(five[0], k)
                    if one and k % 2 == 0:
                        exponentials(one[0], one[1], k // 2)
                if s == STEPS - 1 and (not isinstance(b, int) or b + 1 < B):
                    take_xT(b + 1)
                if at := lagged(b, s, 3, STEPS):
                    take_zT(at[0], at[1])
                if not late(b, 2):
                    n = 2 * (STEPS * b + s) + AHEAD
                    pieces.round(nc, act, n, n + 2)

            take_xT(0)
            pieces.round(nc, act, 0, AHEAD)
            run_steps(act, STEPS, slot, LAST)


def layouts(v):
    import numpy as np

    def pairs_hda(*ws):
        return np.stack([w.reshape(-1, 2, DC, P, 64).transpose(3, 0, 2, 1, 4).reshape(P, -1, DC, P) for w in ws], 2)

    def pairs_ed(*ws):
        return np.stack([w.reshape(-1, P, DC, P).transpose(3, 0, 2, 1) for w in ws], 2)

    def with_out(w, wo):
        v2 = w[:, :, 2].reshape(P, 4, 2, DC, P).transpose(0, 1, 3, 2, 4).reshape(P, 8, D)
        return np.concatenate([w[:, :, 0].reshape(P, 8, D), w[:, :, 1].reshape(P, 8, D), v2, wo], 2)

    def rows(w):
        return w.reshape(-1, P, w.shape[-1]).transpose(1, 0, 2)

    x = v["x"].reshape(TILES, P, D).transpose(1, 0, 2)
    ctx = v["ctx_1024"].reshape(B, S, DC, P).transpose(3, 0, 2, 1)
    mask = v["fside_Bx1xSxS2_0"].reshape(B, ST, P, S).transpose(2, 0, 1, 3)
    out = {
        "x": x, "ctxT": ctx, "mask": mask,
        "a0_w": with_out(pairs_hda(v["L0_attn_Wq"], v["L0_attn_Wk"], v["L0_attn_Wv"]), rows(v["L0_attn_Wo"].reshape(-1, D))),
        "a0_bq": v["L0_attn_bq"].reshape(-1, P).T, "a0_bk": v["L0_attn_bk"].reshape(-1, P).T,
        "a0_bv": v["L0_attn_bv"].reshape(-1, P).T, "a0_bo": v["L0_attn_bo"],
        "c0_w": with_out(pairs_ed(v["L0_xattn_Wq"], v["L0_xattn_Wk"], v["L0_xattn_Wv"]), rows(v["L0_xattn_Wo"].T)),
        "l1_qk": v["L1_attn_w_qkv"][:2 * D].reshape(2, 2, P, DC, P).transpose(4, 1, 0, 3, 2),
        "l1_v": rows(v["L1_attn_w_qkv"][2 * D:].T),
        "l1_out": rows(v["L1_attn_w_out"].T),
        "c1_qk": np.stack([v["L1_xattn_Wq"], v["L1_xattn_Wk"]]).reshape(2, 2, P, DC, P).transpose(4, 1, 0, 3, 2),
        "c1_v": rows(v["L1_xattn_Wv"].T),
        "c1_bq": v["L1_xattn_bq"].reshape(2, P).T, "c1_bk": v["L1_xattn_bk"].reshape(2, P).T,
        "c1_bv": v["L1_xattn_bv"],
        "f1_qk": np.stack([v["L1_ffn_w_q"], v["L1_ffn_w_k"]]).reshape(2, DC, P, 4, P).transpose(2, 3, 0, 1, 4),
        "f1_gate": rows(v["L1_ffn_w_gate"]),
        "f1_val": v["L1_ffn_value_experts"].reshape(8, 8, DC, P, 64).transpose(3, 1, 2, 0, 4).reshape(P, 8, DC, 512),
        "f1_out": v["L1_ffn_output_experts"].reshape(4, 2, 8, 64, D).transpose(1, 3, 2, 0, 4).reshape(P, 8, 4, D),
        "f0_w1": v["L0_ffn_w1"].reshape(8, 4, P, DC, P).transpose(4, 0, 1, 3, 2),
        "f0_w2": v["L0_ffn_w2"].reshape(8, D, 4, P).transpose(3, 0, 2, 1),
        "f0_gate": rows(v["L0_ffn_gate_w"].T),
        "f0_b1": v["L0_ffn_b1"].reshape(-1, P).T,
        "f0_b2": np.pad(v["L0_ffn_b2"], ((0, P - 8), (0, 0))),
        "f0_norm": v["L0_ffn_norm_weight"].reshape(DC, P).T,
    }
    return {k: np.ascontiguousarray(a) for k, a in out.items()}


def program(nc, dram, mid, out):
    c = Core()
    c.mid = mid
    c.dram = dram
    c.spent = []
    c.out = out
    with ExitStack() as ctx:
        sb = lambda name, shape: ctx.enter_context(nc.sbuf_tensor(name, shape, F32))
        sem = lambda name: ctx.enter_context(nc.semaphore(name))
        c.mv = sb("mean_var", [P, TILES, 2])
        c.bn = sb("bn", [P, ST, 6])
        c.mv2 = sb("mv2", [P, ST, 2])
        c.begun = sem("begun")
        c.mid_out = sem("mid_out")
        c.waited = sem("waited")
        c.pool_waited = sem("pool_waited")
        c.eps = sb("eps", [P, 1])
        c.ident = sb("ident", [P, P])
        c.causal_min = sb("causal_min", [P, 2 * P])
        c.half = sb("half", [P, 2])
        c.half1 = sb("half1", [P, 2])
        c.head16 = sb("head16", [P, 8])
        c.head16k = sb("head16k", [P, 8])
        c.x_in = [sem(f"x_in{q}") for q in range(X_PARTS)]
        loads = {}

        def load(eng, tag, dst, src):
            eng.dma_start(dst, src).then_inc(loads[tag][0], 16)
            loads[tag][1] += 16

        for tag in ("a0", "c0", "f0", "l1", "c1", "f1"):
            loads[tag] = [sem(f"w_{tag}"), 0]

        c.wait_weights = lambda eng, tag: eng.wait_ge(loads[tag][0], loads[tag][1])

        def weights(ctx, tag, **shapes):
            w = {k: ctx.enter_context(nc.sbuf_tensor(f"{tag}_weights_{k}", [P, *shape], F32)) for k, shape in shapes.items()}

            def fetch(eng):
                for k in w:
                    src = dram[f"{tag}_{k}"]
                    if len(src.shape) == 1:
                        src = src.partition_broadcast(P)
                    load(eng, tag, w[k][:], src)
            return w, fetch

        def load_none(sp):
            pass

        def halves(ctx, name, shape):
            return [ctx.enter_context(nc.sbuf_tensor(f"{name}_{n}", [P, *shape], F32R)) for n in ("rounded", "rest")]

        small = sb("small", [P, Pieces.STAGES * PIECE])
        room_x = ctx.enter_context(ExitStack())
        c.x = room_x.enter_context(nc.sbuf_tensor("x_sb", [P, TILES, D], F32))
        stage = small[:].rearrange("p (n m) -> p n m", n=Pieces.STAGES)
        pieces = {tag: Pieces(nc, ctx, tag, stage, []) for tag in ("a0", "c0", "f0", "f1")}

        def attention_pieces(tag, w):
            src = dram[f"{tag}_w"]
            pieces[tag].list += [(w[0][:, n], w[1][:, n], src[:, n]) for n in range(8)]

        pieces["c0"].list += [(None, None, dram["c0_w"][:, n]) for n in range(Pieces.STAGES)]

        def load_c0(sp):
            pieces["c0"].load(sp, 0, Pieces.STAGES)

        with ExitStack() as room:
            c.causal = room.enter_context(nc.sbuf_tensor("causal", [P, 2 * P], F32))
            w = halves(room, "a0_w", [8, 4 * D])
            attention_pieces("a0", w)
            a0, load_a0 = weights(room, "a0", bq=[8], bk=[8], bv=[8], bo=[D])
            with nc.Block() as block:
                @block.scalar
                def _(act):
                    pieces["a0"].load(act, 0, Pieces.STAGES)
                    load_a0(act)
            constants(nc, c)
            attention(nc, c, "a0", pieces["a0"], w, load_c0, causal=True,
                      bias={"q": a0["bq"], "k": a0["bk"], "v": a0["bv"]}, bo=a0["bo"])
        pieces["c0"].list.clear()
        flat = lambda ap: ap.rearrange("p a b m -> p (a b m)") if len(ap.shape) == 4 else ap.rearrange("p a m -> p (a m)")
        f0_src = [flat(dram["f0_gate"])]
        for e in range(8):
            f0_src += [flat(dram["f0_w1"][:, e]), flat(dram["f0_w2"][:, e])]
        pieces["f0"].list += [(None, None, src) for src in f0_src]

        room_f0 = ctx.enter_context(ExitStack())
        f0, load_f0_small = weights(room_f0, "f0", norm=[DC], b1=[32], b2=[D])

        def load_f0(sp):
            load_f0_small(sp)
            pieces["f0"].load(sp, 0, Pieces.STAGES)

        with ExitStack() as room:
            w = halves(room, "c0_w", [8, 4 * D])
            attention_pieces("c0", w)
            attention(nc, c, "c0", pieces["c0"], w, load_f0, cross=True)
        l1_qk = small[:, 0:1024].rearrange("p (t h c m) -> p t h c m", t=2, h=2, c=DC)
        l1_v = small[:, 1024:1536].rearrange("p (c d) -> p c d", c=DC)
        l1_out = small[:, 1536:2048].rearrange("p (c d) -> p c d", c=DC)

        def load_l1(sp):
            load(sp, "l1", l1_qk, dram["l1_qk"])
            load(sp, "l1", l1_v, dram["l1_v"])
            load(sp, "l1", l1_out, dram["l1_out"])

        with ExitStack() as room:
            gate = halves(room, "f0_gate", [DC, 8])
            w1 = halves(room, "f0_w1", [8, 4, DC, P])
            w2 = halves(room, "f0_w2", [8, 4, D])
            places = [tuple(flat(t[:]) for t in gate)]
            for e in range(8):
                places += [tuple(flat(t[:, e]) for t in w1), tuple(flat(t[:, e]) for t in w2)]
            pieces["f0"].list[:] = [(*place, src) for place, src in zip(places, f0_src)]
            experts(nc, c, "f0", pieces["f0"], w1, w2, gate, f0["b1"], f0["b2"], f0["norm"], load_l1)
        room_f0.close()
        f1_src = [flat(dram[name][:, n]) for name in ("f1_val", "f1_out") for n in range(8)]
        pieces["f1"].list += [(None, None, src) for src in f1_src]
        with ExitStack() as room:
            c1, load_c1 = weights(room, "c1", qk=[2, 2, DC, P], v=[DC, D], bv=[D], bq=[2], bk=[2])

            def load_val(sp):
                pieces["f1"].load(sp, 0, Pieces.STAGES)

            small_heads(nc, c, "l1", l1_qk, l1_v, load_c1, softmax=False, w_out=l1_out)
            small_heads(nc, c, "c1", c1["qk"], c1["v"], load_val, softmax=True, bq=c1["bq"], bk=c1["bk"], bv=c1["bv"])
        room_x.close()
        f1, load_f1 = weights(ctx, "f1", qk=[4, 2, DC, P], gate=[DC, 64])
        w_out = halves(ctx, "f1_out", [8, 4, D])
        w_val = halves(ctx, "f1_val", [8, DC, 512])
        pieces["f1"].list[:] = [(flat(w[0][:, n % 8]), flat(w[1][:, n % 8]), src)
                                for w, n, src in zip([w_val] * 8 + [w_out] * 8, range(16), f1_src)]
        gated_heads(nc, c, "f1", pieces["f1"], f1["qk"], f1["gate"], w_val, w_out, load_f1)


def kernel(**inputs):
    import numpy as np
    import concourse.bacc as bacc
    from concourse.bass_utils import run_bass_kernel_spmd

    nc = bacc.Bacc("TRN2", target_bir_lowering=False, num_devices=1)
    arrays, dram = {}, {}
    for name, a in layouts({k: np.asarray(v) for k, v in inputs.items()}).items():
        arrays[f"in_{name}"] = a
        dram[name] = nc.dram_tensor(f"in_{name}", a.shape, mybir.dt.from_np(a.dtype), kind="ExternalInput").ap()
    out = nc.dram_tensor("out_x", (P, TILES, D), F32, kind="ExternalOutput").ap()
    mid = nc.dram_tensor("x_mid", (B, P, ST, D), F32, kind="Internal").ap()
    program(nc, dram, mid, out)
    r = run_bass_kernel_spmd(nc, [arrays], core_ids=[0])
    return r.results[0]["out_x"].transpose(1, 0, 2).reshape(B, S, D)
```
